# Optimizing a Trainium2 kernel written in Bass

```python
import numpy as np
import jax
import jax.numpy as jnp

def _softmax(x, axis=-1):
    return jax.nn.softmax(x, axis=axis)

def _gelu(x):
    return jax.nn.gelu(x, approximate=True)

def _silu(x):
    return jax.nn.silu(x)

def _sigmoid(x):
    return jax.nn.sigmoid(x)

def _layernorm(x, axis=-1, eps=1e-05):
    m = jnp.mean(x, axis=axis, keepdims=True)
    v = jnp.var(x, axis=axis, keepdims=True)
    return (x - m) / jnp.sqrt(v + eps)

def _scatter_add(tgt, idx, src, axis=0):
    return tgt.at[idx].add(src)

def _segment_sum(src, seg, n):
    return jax.ops.segment_sum(src, seg, n)
kernel_name = 'mk_prb_d2_jaxref_r8_3b51f5'

def setup_inputs(seed: int=0):
    np.random.seed(seed)
    _w = jnp.asarray

    def _L0_attn_setup():
        import math
        import jax, jax.numpy as jnp
        import numpy as np
        HEADS = 16
        DIM_HEAD = 64
        NUM_NULL_KV = 2
        ATTN_SCALE = 8.0
        LN_EPS = 1e-05

        def _alibi_slopes(heads):
            start = 2.0 ** (-2.0 ** (-(math.log2(heads) - 3.0)))
            return np.array([start * start ** i for i in range(heads)], dtype=np.float32)

        def _l2norm(t):
            return t / jnp.maximum(jnp.linalg.norm(t, axis=-1, keepdims=True), 1e-12)
        key = jax.random.key(seed)
        ks = jax.random.split(key, 5)
        b, n, dim = (4, 256, 128)
        return {'x': jax.random.normal(ks[0], (b, n, dim), dtype=jnp.float32), 'gamma': jnp.ones((dim,), dtype=jnp.float32), 'w_q': jax.random.normal(ks[1], (dim, HEADS * DIM_HEAD), dtype=jnp.float32) * 0.02, 'w_kv': jax.random.normal(ks[2], (dim, 2 * HEADS * DIM_HEAD), dtype=jnp.float32) * 0.02, 'null_kv': jax.random.normal(ks[3], (HEADS, 2 * NUM_NULL_KV, DIM_HEAD), dtype=jnp.float32), 'q_scale': jnp.ones((DIM_HEAD,), dtype=jnp.float32), 'k_scale': jnp.ones((DIM_HEAD,), dtype=jnp.float32), 'w_out': jax.random.normal(ks[4], (HEADS * DIM_HEAD, dim), dtype=jnp.float32) * 0.02}
    _L0_attn_in = _L0_attn_setup()

    def _L0_ffn_setup():
        import jax, jax.numpy as jnp
        import numpy as np
        import math
        D_MODEL = 128
        D_FF = 512
        NUM_EXPERTS = 8
        NUM_SHARED = 1
        E_ROUTED = NUM_EXPERTS - NUM_SHARED
        TOP_K = 2
        CAP_FACTOR = 1.25
        B, S = (4, 256)
        T = B * S
        CAPACITY = math.ceil(CAP_FACTOR * T * TOP_K / E_ROUTED)
        SHARED_SCALE = 1.0

        def _layernorm(x, g, b, eps=1e-05):
            mu = jnp.mean(x, axis=-1, keepdims=True)
            var = jnp.mean((x - mu) ** 2, axis=-1, keepdims=True)
            return (x - mu) * jax.lax.rsqrt(var + eps) * g + b
        key = jax.random.key(seed)
        ks = jax.random.split(key, 10)
        s = 0.02
        return {'x': jax.random.normal(ks[0], (B, S, D_MODEL), dtype=jnp.float32), 'ln_g': jnp.ones((D_MODEL,), jnp.float32), 'ln_b': jnp.zeros((D_MODEL,), jnp.float32), 'Wr': jax.random.normal(ks[1], (D_MODEL, E_ROUTED), jnp.float32) * s, 'W1': jax.random.normal(ks[2], (E_ROUTED, D_MODEL, D_FF), jnp.float32) * s, 'W3': jax.random.normal(ks[3], (E_ROUTED, D_MODEL, D_FF), jnp.float32) * s, 'W2': jax.random.normal(ks[4], (E_ROUTED, D_FF, D_MODEL), jnp.float32) * s, 'W1s': jax.random.normal(ks[5], (D_MODEL, D_FF), jnp.float32) * s, 'W3s': jax.random.normal(ks[6], (D_MODEL, D_FF), jnp.float32) * s, 'W2s': jax.random.normal(ks[7], (D_FF, D_MODEL), jnp.float32) * s}
    _L0_ffn_in = _L0_ffn_setup()

    def _L1_attn_setup():
        import jax, jax.numpy as jnp
        import numpy as np
        B, T, D = (4, 256, 128)
        N_HEADS = 16
        HEAD_DIM = D // N_HEADS

        def rope(x):
            t, dh = (x.shape[-2], x.shape[-1])
            half = dh // 2
            theta = 1.0 / 10000.0 ** (jnp.arange(half, dtype=jnp.float32) / half)
            ang = jnp.arange(t, dtype=jnp.float32)[:, None] * theta[None, :]
            sin, cos = (jnp.sin(ang), jnp.cos(ang))
            x1 = x[..., 0::2]
            x2 = x[..., 1::2]
            return jnp.concatenate([x1 * cos - x2 * sin, x1 * sin + x2 * cos], axis=-1)
        key = jax.random.key(seed)
        ks = jax.random.split(key, 9)
        s = 0.02
        return {'x': jax.random.normal(ks[0], (B, T, D), dtype=jnp.float32), 'W_q': jax.random.normal(ks[1], (D, D), dtype=jnp.float32) * s, 'b_q': jnp.zeros((D,), dtype=jnp.float32), 'W_k': jax.random.normal(ks[2], (D, D), dtype=jnp.float32) * s, 'b_k': jnp.zeros((D,), dtype=jnp.float32), 'W_v': jax.random.normal(ks[3], (D, D), dtype=jnp.float32) * s, 'b_v': jnp.zeros((D,), dtype=jnp.float32), 'W_o': jax.random.normal(ks[4], (D, D), dtype=jnp.float32) * s, 'b_o': jnp.zeros((D,), dtype=jnp.float32)}
    _L1_attn_in = _L1_attn_setup()

    def _L1_ffn_setup():
        import jax, jax.numpy as jnp
        import numpy as np
        B, S, D, F, E, K = (2, 256, 128, 512, 8, 2)
        key = jax.random.key(seed)
        ks = jax.random.split(key, 5)
        x = jax.random.normal(ks[0], (B, S, D), dtype=jnp.float32)
        Wg = jax.random.normal(ks[1], (D, E), dtype=jnp.float32) * 0.02
        W1 = jax.random.normal(ks[2], (E, D, F), dtype=jnp.float32) * 0.02
        b1 = jnp.zeros((E, F), dtype=jnp.float32)
        W2 = jax.random.normal(ks[3], (E, F, D), dtype=jnp.float32) * 0.02
        b2 = jnp.zeros((E, D), dtype=jnp.float32)
        return {'x': x, 'Wg': Wg, 'W1': W1, 'b1': b1, 'W2': W2, 'b2': b2}
    _L1_ffn_in = _L1_ffn_setup()
    _d = {'L0_attn_x': _L0_attn_in['x'], 'L0_attn_gamma': _L0_attn_in['gamma'], 'L0_attn_w_q': _L0_attn_in['w_q'], 'L0_attn_w_kv': _L0_attn_in['w_kv'], 'L0_attn_null_kv': _L0_attn_in['null_kv'], 'L0_attn_q_scale': _L0_attn_in['q_scale'], 'L0_attn_k_scale': _L0_attn_in['k_scale'], 'L0_attn_w_out': _L0_attn_in['w_out'], 'L0_ffn_ln_g': _L0_ffn_in['ln_g'], 'L0_ffn_ln_b': _L0_ffn_in['ln_b'], 'L0_ffn_Wr': _L0_ffn_in['Wr'], 'L0_ffn_W1': _L0_ffn_in['W1'], 'L0_ffn_W3': _L0_ffn_in['W3'], 'L0_ffn_W2': _L0_ffn_in['W2'], 'L0_ffn_W1s': _L0_ffn_in['W1s'], 'L0_ffn_W3s': _L0_ffn_in['W3s'], 'L0_ffn_W2s': _L0_ffn_in['W2s'], 'L1_attn_W_q': _L1_attn_in['W_q'], 'L1_attn_b_q': _L1_attn_in['b_q'], 'L1_attn_W_k': _L1_attn_in['W_k'], 'L1_attn_b_k': _L1_attn_in['b_k'], 'L1_attn_W_v': _L1_attn_in['W_v'], 'L1_attn_b_v': _L1_attn_in['b_v'], 'L1_attn_W_o': _L1_attn_in['W_o'], 'L1_attn_b_o': _L1_attn_in['b_o'], 'L1_ffn_Wg': _L1_ffn_in['Wg'], 'L1_ffn_W1': _L1_ffn_in['W1'], 'L1_ffn_b1': _L1_ffn_in['b1'], 'L1_ffn_W2': _L1_ffn_in['W2'], 'L1_ffn_b2': _L1_ffn_in['b2']}
    _x0 = _d['L0_attn_x']
    _d['L0_attn_x'] = jax.random.normal(jax.random.fold_in(jax.random.key(seed), 1), (1, 2048, 128), dtype=_x0.dtype)
    del _x0
    return _d

def reference(L0_attn_x, L0_attn_gamma, L0_attn_w_q, L0_attn_w_kv, L0_attn_null_kv, L0_attn_q_scale, L0_attn_k_scale, L0_attn_w_out, L0_ffn_ln_g, L0_ffn_ln_b, L0_ffn_Wr, L0_ffn_W1, L0_ffn_W3, L0_ffn_W2, L0_ffn_W1s, L0_ffn_W3s, L0_ffn_W2s, L1_attn_W_q, L1_attn_b_q, L1_attn_W_k, L1_attn_b_k, L1_attn_W_v, L1_attn_b_v, L1_attn_W_o, L1_attn_b_o, L1_ffn_Wg, L1_ffn_W1, L1_ffn_b1, L1_ffn_W2, L1_ffn_b2):

    def _L0_attn_ref(x, gamma, w_q, w_kv, null_kv, q_scale, k_scale, w_out):
        import math
        import jax, jax.numpy as jnp
        import numpy as np
        HEADS = 16
        DIM_HEAD = 64
        NUM_NULL_KV = 2
        ATTN_SCALE = 8.0
        LN_EPS = 1e-05

        def _alibi_slopes(heads):
            start = 2.0 ** (-2.0 ** (-(math.log2(heads) - 3.0)))
            return np.array([start * start ** i for i in range(heads)], dtype=np.float32)

        def _l2norm(t):
            return t / jnp.maximum(jnp.linalg.norm(t, axis=-1, keepdims=True), 1e-12)
        b, n, dim = x.shape
        mu = jnp.mean(x, axis=-1, keepdims=True)
        var = jnp.mean(jnp.square(x - mu), axis=-1, keepdims=True)
        xn = (x - mu) * jax.lax.rsqrt(var + LN_EPS) * gamma
        q = (xn @ w_q).reshape(b, n, HEADS, DIM_HEAD).transpose(0, 2, 1, 3)
        kv = xn @ w_kv
        k, v = jnp.split(kv, 2, axis=-1)
        k = k.reshape(b, n, HEADS, DIM_HEAD).transpose(0, 2, 1, 3)
        v = v.reshape(b, n, HEADS, DIM_HEAD).transpose(0, 2, 1, 3)
        nkv = null_kv.reshape(HEADS, NUM_NULL_KV, 2, DIM_HEAD)
        nk = jnp.broadcast_to(nkv[:, :, 0][None], (b, HEADS, NUM_NULL_KV, DIM_HEAD))
        nv = jnp.broadcast_to(nkv[:, :, 1][None], (b, HEADS, NUM_NULL_KV, DIM_HEAD))
        k = jnp.concatenate([nk, k], axis=2)
        v = jnp.concatenate([nv, v], axis=2)
        q = _l2norm(q) * q_scale
        k = _l2norm(k) * k_scale
        sim = jnp.einsum('bhid,bhjd->bhij', q, k) * ATTN_SCALE
        j = n + NUM_NULL_KV
        rows = jnp.arange(n)
        cols = jnp.arange(j)
        dist = -jnp.abs(cols[None, :] - (rows[:, None] + NUM_NULL_KV)).astype(sim.dtype)
        slopes = jnp.asarray(_alibi_slopes(HEADS))
        sim = sim + dist[None, None] * slopes[None, :, None, None]
        causal_mask = cols[None, :] > rows[:, None] + NUM_NULL_KV
        neg = -jnp.finfo(sim.dtype).max
        sim = jnp.where(causal_mask[None, None], neg, sim)
        attn = jax.nn.softmax(sim, axis=-1)
        out = jnp.einsum('bhij,bhjd->bhid', attn, v)
        out = out.transpose(0, 2, 1, 3).reshape(b, n, HEADS * DIM_HEAD)
        return out @ w_out

    def _L0_ffn_ref(x, ln_g, ln_b, Wr, W1, W3, W2, W1s, W3s, W2s):
        import jax, jax.numpy as jnp
        import numpy as np
        import math
        D_MODEL = 128
        D_FF = 512
        NUM_EXPERTS = 8
        NUM_SHARED = 1
        E_ROUTED = NUM_EXPERTS - NUM_SHARED
        TOP_K = 2
        CAP_FACTOR = 1.25
        B, S = (4, 256)
        T = B * S
        CAPACITY = math.ceil(CAP_FACTOR * T * TOP_K / E_ROUTED)
        SHARED_SCALE = 1.0

        def _layernorm(x, g, b, eps=1e-05):
            mu = jnp.mean(x, axis=-1, keepdims=True)
            var = jnp.mean((x - mu) ** 2, axis=-1, keepdims=True)
            return (x - mu) * jax.lax.rsqrt(var + eps) * g + b
        Bx, Sx, D = x.shape
        Tn = Bx * Sx
        h = _layernorm(x, ln_g, ln_b).reshape(Tn, D)
        logits = h @ Wr
        top_vals, top_idx = jax.lax.top_k(logits, TOP_K)
        gates = jax.nn.softmax(top_vals, axis=-1)
        idx = top_idx.T.reshape(-1)
        gat = gates.T.reshape(-1)
        tok = jnp.tile(jnp.arange(Tn), TOP_K)
        onehot = jax.nn.one_hot(idx, E_ROUTED, dtype=jnp.int32)
        pos = jnp.sum(jnp.cumsum(onehot, axis=0) * onehot, axis=-1) - 1
        keep = pos < CAPACITY
        pos_c = jnp.where(keep, pos, CAPACITY)
        xe = jnp.zeros((E_ROUTED, CAPACITY, D), h.dtype).at[idx, pos_c].set(h[tok], mode='drop')
        a = jnp.einsum('ecd,edf->ecf', xe, W1)
        b = jnp.einsum('ecd,edf->ecf', xe, W3)
        ye = jnp.einsum('ecf,efd->ecd', jax.nn.silu(a) * b, W2)
        out_slots = ye[jnp.clip(idx, 0, E_ROUTED - 1), jnp.clip(pos_c, 0, CAPACITY - 1)]
        out_slots = out_slots * (gat * keep.astype(gat.dtype))[:, None]
        routed = jnp.zeros((Tn, D), h.dtype).at[tok].add(out_slots)
        shared = jax.nn.silu(h @ W1s) * (h @ W3s) @ W2s
        out = routed + SHARED_SCALE * shared
        return out.reshape(Bx, Sx, D)

    def _L1_attn_ref(x, W_q, b_q, W_k, b_k, W_v, b_v, W_o, b_o):
        import jax, jax.numpy as jnp
        import numpy as np
        B, T, D = (4, 256, 128)
        N_HEADS = 16
        HEAD_DIM = D // N_HEADS

        def rope(x):
            t, dh = (x.shape[-2], x.shape[-1])
            half = dh // 2
            theta = 1.0 / 10000.0 ** (jnp.arange(half, dtype=jnp.float32) / half)
            ang = jnp.arange(t, dtype=jnp.float32)[:, None] * theta[None, :]
            sin, cos = (jnp.sin(ang), jnp.cos(ang))
            x1 = x[..., 0::2]
            x2 = x[..., 1::2]
            return jnp.concatenate([x1 * cos - x2 * sin, x1 * sin + x2 * cos], axis=-1)
        b, t, d = x.shape
        h, dh = (N_HEADS, d // N_HEADS)

        def heads(y):
            return y.reshape(b, t, h, dh).transpose(0, 2, 1, 3)
        q = rope(heads(x @ W_q.T + b_q))
        k = rope(heads(x @ W_k.T + b_k))
        v = heads(x @ W_v.T + b_v)
        scores = jnp.einsum('bhtd,bhsd->bhts', q, k)
        causal = jnp.tril(jnp.ones((t, t), dtype=bool))
        mask = jnp.where(causal, 0.0, -jnp.inf)
        probs = jax.nn.softmax((scores + mask) / jnp.sqrt(jnp.float32(dh)), axis=-1)
        out = jnp.einsum('bhts,bhsd->bhtd', probs, v)
        out = out.transpose(0, 2, 1, 3).reshape(b, t, d)
        return out @ W_o.T + b_o

    def _L1_ffn_ref(x, Wg, W1, b1, W2, b2):
        import jax, jax.numpy as jnp
        import numpy as np
        B, S, D, F, E, K = (2, 256, 128, 512, 8, 2)
        b, s, d = x.shape
        e = Wg.shape[1]
        T = b * s
        C = 2 * K * T // e
        xt = x.reshape(T, d)
        logits = xt.astype(jnp.float32) @ Wg.astype(jnp.float32)
        gates = jax.nn.softmax(logits, axis=-1)
        idx1 = jnp.argmax(gates, axis=-1)
        mask1 = jax.nn.one_hot(idx1, e, dtype=gates.dtype)
        gate1 = jnp.sum(gates * mask1, axis=-1)
        logits2 = jnp.where(mask1 > 0, -jnp.inf, logits)
        idx2 = jnp.argmax(logits2, axis=-1)
        mask2 = jax.nn.one_hot(idx2, e, dtype=gates.dtype)
        gate2 = jnp.sum(gates * mask2, axis=-1)
        denom = gate1 + gate2 + 1e-09
        w1 = gate1 / denom
        w2 = gate2 / denom
        p1 = jnp.cumsum(mask1, axis=0) - mask1
        pos1 = jnp.sum(p1 * mask1, axis=-1).astype(jnp.int32)
        off = jnp.sum(mask1, axis=0)
        p2 = jnp.cumsum(mask2, axis=0) - mask2 + off[None, :]
        pos2 = jnp.sum(p2 * mask2, axis=-1).astype(jnp.int32)
        keep1 = (pos1 < C).astype(xt.dtype)
        keep2 = (pos2 < C).astype(xt.dtype)
        pos1 = jnp.clip(pos1, 0, C - 1)
        pos2 = jnp.clip(pos2, 0, C - 1)
        xe = jnp.zeros((e, C, d), dtype=xt.dtype)
        xe = xe.at[idx1, pos1].add(xt * keep1[:, None])
        xe = xe.at[idx2, pos2].add(xt * keep2[:, None])
        h = jax.nn.gelu(jnp.einsum('ecd,edf->ecf', xe, W1) + b1[:, None, :], approximate=False)
        ye = jnp.einsum('ecf,efd->ecd', h, W2) + b2[:, None, :]
        out = ye[idx1, pos1] * (w1 * keep1)[:, None] + ye[idx2, pos2] * (w2 * keep2)[:, None]
        return out.reshape(b, s, d)
    x = L0_attn_x
    xn = _layernorm(x, axis=-1)
    x = x + _L0_attn_ref(xn, L0_attn_gamma, L0_attn_w_q, L0_attn_w_kv, L0_attn_null_kv, L0_attn_q_scale, L0_attn_k_scale, L0_attn_w_out) + _L0_ffn_ref(xn, L0_ffn_ln_g, L0_ffn_ln_b, L0_ffn_Wr, L0_ffn_W1, L0_ffn_W3, L0_ffn_W2, L0_ffn_W1s, L0_ffn_W3s, L0_ffn_W2s)
    xn = _layernorm(x, axis=-1)
    x = x + _L1_attn_ref(xn, L1_attn_W_q, L1_attn_b_q, L1_attn_W_k, L1_attn_b_k, L1_attn_W_v, L1_attn_b_v, L1_attn_W_o, L1_attn_b_o) + _L1_ffn_ref(xn, L1_ffn_Wg, L1_ffn_W1, L1_ffn_b1, L1_ffn_W2, L1_ffn_b2)
    return x

_drawn_inputs = setup_inputs


def setup_inputs(seed=0):
    import zlib

    import numpy as np

    out = dict(_drawn_inputs(seed))
    spreads = {'L0_attn_gamma': (1.0, 0.6),
     'L0_attn_q_scale': (1.0, 0.6),
     'L0_attn_k_scale': (1.0, 0.6),
     'L0_ffn_ln_g': (1.0, 0.6),
     'L0_ffn_ln_b': (0.0, 0.8),
     'L1_attn_b_q': (0.0, 2.0),
     'L1_attn_b_k': (0.0, 2.0),
     'L1_attn_b_v': (0.0, 2.0),
     'L1_attn_b_o': (0.0, 0.522),
     'L1_ffn_b1': (0.0, 2.0),
     'L1_ffn_b2': (0.0, 0.72)}
    factors = {'L0_attn_null_kv': 17.618,
     'L0_ffn_Wr': 6.037,
     'L0_ffn_W1': 5.93,
     'L0_ffn_W3': 5.704,
     'L0_ffn_W2': 5.512,
     'L0_ffn_W1s': 3.69,
     'L0_ffn_W3s': 3.717,
     'L0_ffn_W2s': 3.688,
     'L1_attn_W_q': 8.0,
     'L1_attn_W_k': 8.0,
     'L1_attn_W_v': 8.0,
     'L0_attn_w_q': 3.211,
     'L0_attn_w_kv': 3.104,
     'L0_attn_w_out': 2.747,
     'L1_ffn_Wg': 3.437,
     'L1_ffn_W1': 8.0,
     'L1_ffn_W2': 3.837}
    for name, (base, spread) in spreads.items():
        noise = np.random.default_rng([zlib.crc32(name.encode()), seed]).standard_normal(out[name].shape)
        drawn = base * np.exp(spread * noise) if base else spread * noise
        out[name] = jnp.asarray(drawn.astype(out[name].dtype))
    for name, factor in factors.items():
        out[name] = (out[name] * factor).astype(out[name].dtype)
    return out
```

```python
from contextlib import ExitStack

import numpy as np

import concourse.bass as bass
from concourse import mybir

ALU = mybir.AluOpType
ACT = mybir.ActivationFunctionType
F32 = mybir.dt.float32
F16 = mybir.dt.float16
BF16 = mybir.dt.bfloat16
AX_X = mybir.AxisListType.X

P = 128
D = 128
T = 2048
NT = T // P
QW = 512
NQB = T // QW
TPQ = QW // P
EPS = 1e-5
BIG = 1e30
E = 8
F = 512
FC = F // P
CAP0 = 366
CAP1 = 2 * 2 * T // E

H0 = 16
DH0 = 64
PAIRS = H0 // 2
NULLS = 2
KW = NULLS + T
ROW_ONE = 64
ROW_POS = 96
ALIBI_REF = QW // 2

H1 = 16
DH1 = 8
GROUPS = H1 // 2
PARTS = 3
STACK = PARTS * PARTS * DH1
ROW_SHIFT = 96


def flat(ap):
    return ap.rearrange("o a b -> (o a) b")


def chain(eng, sem):
    count = [0]

    def link(ins):
        count[0] += 1
        ins.then_inc(sem, 1)
        eng.wait_ge(sem, count[0])
    return link



BLOCKS0 = [(-1, -1)] + [(qb, kb) for qb in range(NQB) for kb in range(TPQ * qb + TPQ)]
NB0 = len(BLOCKS0)
REAL0 = NB0 - 1


def chunks0():
    out = []
    for qt in range(NT):
        end, at, n = NULLS + P * (qt + 1), 0, 0
        while at < end:
            stop = min(end, at + (NULLS + 3 * P if at == 0 else QW))
            out.append((qt, n, at, stop))
            at, n = stop, n + 1
    return out


CHUNKS0 = chunks0()
NC0 = len(CHUNKS0)
MAXCH = max(n for _, n, _, _ in CHUNKS0) + 1
CHUNKS1 = [(qt, c, QW * c, min(QW * (c + 1), P * (qt + 1))) for qt in range(NT) for c in range(qt // TPQ + 1)]
NC1 = len(CHUNKS1)


def spread(items, first, last, slots):
    out = [[] for _ in range(slots)]
    n = last - first + 1
    for k, it in enumerate(items):
        out[first + k * n // len(items)].append(it)
    return out


class Memory:
    pass


def layer_norm(link, dve, src, dst, cen, sq, col, last, var_ready, rstd_ready, turn):
    wide = [P, NT, D]
    link(dve.reduce_sum(col[:, 0, :], src, AX_X))
    link(dve.tensor_scalar(col[:, 1, :], col[:, 0, :], 1.0 / D, None, ALU.mult))
    link(dve.tensor_tensor(cen, src, col[:, 1, :].unsqueeze(2).to_broadcast(wide), ALU.subtract))
    link(dve.tensor_tensor(sq, cen, cen, ALU.mult))
    link(dve.reduce_sum(col[:, 2, :], sq, AX_X))
    dve.tensor_scalar(col[:, 3, :], col[:, 2, :], 1.0 / D, EPS, ALU.mult, ALU.add).then_inc(var_ready, 1)
    dve.wait_ge(rstd_ready, turn)
    last(dve.tensor_tensor(dst, cen, col[:, 4, :].unsqueeze(2).to_broadcast(wide), ALU.mult))


def pick_top(link, dve, logits, best, eq, cand, first, mask, expert_less):
    wide = [P, NT, E]
    link(dve.reduce_max(best, logits, AX_X))
    link(dve.tensor_tensor(eq, logits, best.unsqueeze(2).to_broadcast(wide), ALU.is_equal))
    link(dve.tensor_scalar(cand, eq, -100.0, None, ALU.mult))
    link(dve.tensor_tensor(cand, cand, expert_less, ALU.add))
    link(dve.tensor_reduce(first, cand, AX_X, ALU.min))
    link(dve.tensor_scalar(first, first, 100.0, None, ALU.add))
    link(dve.tensor_tensor(mask, expert_less, first.unsqueeze(2).to_broadcast(wide), ALU.is_equal))


def prepare(nc, mem, layer, dram):
    routed = E - 1 if layer == 0 else E
    capacity = CAP0 if layer == 0 else CAP1
    with ExitStack() as ctx:
        def sb(name, shape, dt=F32):
            return ctx.enter_context(nc.sbuf_tensor(f"{name}_{layer}", shape, dt))

        def sem(name):
            return ctx.enter_context(nc.semaphore(f"{name}_{layer}"))

        xn = sb("xn", [P, NT, D])
        cen = sb("cen", [P, NT, D])
        sq = sb("sq", [P, NT, D])
        col = sb("col", [P, 5, NT])
        w_router = sb("w_router", [P, E])
        vecs = sb("vecs", [P, 3])
        expert_less = sb("expert_less", [P, NT, E])
        logits = sb("logits", [P, NT, E])
        logits2 = sb("logits2", [P, NT, E])
        soft = sb("soft", [P, NT, E])
        eq = sb("eq", [P, NT, E])
        cand = sb("cand", [P, NT, E])
        mask = sb("mask", [P, 2, NT, E])
        maskb = sb("maskb", [P, 2, NT, E], BF16)
        pos = sb("pos", [P, 2, NT, E])
        total = sb("total", [P, 2 * NT, E])
        before = sb("before", [P, 2 * NT, E])
        small = sb("small", [P, 12, NT])
        pair = sb("pair", [P, 2, NT])
        ones_row = sb("ones_row", [P, 2 * NT])
        turned = [ctx.enter_context(nc.psum_tensor(f"turned{n}_{layer}", [P, QW], F32)) for n in range(NQB)]
        ps_log = ctx.enter_context(nc.psum_tensor(f"ps_log_{layer}", [P, NT, 32], F32))
        ps_cnt = ctx.enter_context(nc.psum_tensor(f"ps_cnt_{layer}", [P, 2 * NT * E], F32))
        ps_tot = ctx.enter_context(nc.psum_tensor(f"ps_tot_{layer}", [P, 2 * NT * E], F32))

        x_loaded = sem("x_loaded")
        consts_loaded = sem("consts_loaded")
        step = sem("step")
        var_ready = sem("var_ready")
        rstd_ready = sem("rstd_ready")
        normed = sem("normed")
        tiles_turned = sem("tiles_turned")
        act_read = sem("act_read")
        hT_ready = sem("hT_ready")
        logits_ready = sem("logits_ready")
        masks_ready = sem("masks_ready")
        counted = sem("counted")
        diff_ready = sem("diff_ready")
        exp_ready = sem("exp_ready")
        xT_ready = sem("xT_ready")
        if layer == 0:
            nk = sb("nk", [2 * H0, DH0])
            nk2 = sb("nk2", [2 * H0, DH0])
            nkcol = sb("nkcol", [2 * H0, 2])
            nk_hi = sb("nk_hi", [DH0, 2 * H0], F16)
            nk_lo = sb("nk_lo", [DH0, 2 * H0], F16)
            ps_null = ctx.enter_context(nc.psum_tensor("ps_null", [DH0, 2 * H0], F32))
            nk_ready = sem("nk_ready")
            nk_turned = sem("nk_turned")
        else:
            gates_flat = sb("gates_flat", [P, NT * E])
            gates_T = sb("gates_T", [P, P])
            b2 = sb("b2", [P, NT * D])
            b_o = sb("b_o", [P, D])
            gates_ready = sem("gates_ready")
            gates_turned = sem("gates_turned")
            bias_ready = sem("bias_ready")
        block = ctx.enter_context(nc.Block())

        @block.sync
        def _(sp):
            if layer == 0:
                sp.dma_start(mem.acc[:, :, :], dram["x"].rearrange("(t p) d -> p t d", p=P)).then_inc(x_loaded, 16)
                sp.dma_start(mem.ident[:, :], dram["ident"]).then_inc(consts_loaded, 16)
                sp.dma_start(mem.mask_q[:, :], dram["mask_q"]).then_inc(consts_loaded, 16)
                sp.dma_start(mem.mask_k[:, :], dram["mask_k"]).then_inc(consts_loaded, 16)
                sp.dma_start(mem.lower[:, :], dram["lower"]).then_inc(consts_loaded, 16)
                sp.dma_start(vecs[:, :], dram["vecs"]).then_inc(consts_loaded, 16)
                sp.dma_start(nk[:, :], dram["null_k"]).then_inc(consts_loaded, 16)
                sp.dma_start(mem.scales[:, :], dram["scales"]).then_inc(consts_loaded, 16)
            else:
                sp.dma_start(b2[:, :], dram["b2_1"]).then_inc(consts_loaded, 16)
                sp.dma_start(b_o[:, :], dram["b_o"].to_broadcast([P, D])).then_inc(consts_loaded, 16)
            sp.dma_start(w_router[:, 0:routed], dram["router0" if layer == 0 else "router1"]).then_inc(consts_loaded, 16)
            sp.dma_start(expert_less[:, :, :], dram["expert_less"].rearrange("p (t e) -> p t e", e=E)).then_inc(consts_loaded, 16)

        loads = 16 * (9 if layer == 0 else 4)

        @block.vector
        def _(dve):
            link = chain(dve, step)
            link(dve.memset(ones_row[:, :], 1.0))
            if layer == 0:
                link(dve.memset(mem.minus_half[:, :], -0.5))
            if layer == 0:
                dve.wait_ge(x_loaded, 16)
                layer_norm(link, dve, mem.acc[:, :, :], xn[:, :, :], cen[:, :, :], sq[:, :, :], col, link,
                           var_ready, rstd_ready, 1)
                layer_norm(link, dve, xn[:, :, :], mem.y[:, :, :], cen[:, :, :], sq[:, :, :], col,
                           lambda ins: ins.then_inc(normed, 1), var_ready, rstd_ready, 2)
            else:
                layer_norm(link, dve, mem.acc[:, :, :], mem.y[:, :, :], cen[:, :, :], sq[:, :, :], col,
                           lambda ins: ins.then_inc(normed, 1), var_ready, rstd_ready, 1)
            dve.wait_ge(consts_loaded, loads)
            if layer == 0:
                link(dve.tensor_copy(mem.ident_b[:, :], mem.ident[:, :]))
                link(dve.tensor_copy(mem.ident_h[:, :], mem.ident[:, :]))
                link(dve.tensor_copy(mem.mask_qb[:, :], mem.mask_q[:, :]))
                link(dve.tensor_copy(mem.mask_kb[:, :], mem.mask_k[:, :]))
                link(dve.tensor_copy(mem.lower_b[:, :], mem.lower[:, :]))
                link(dve.memset(mem.ones_b[:, :], 1.0))
                link(dve.tensor_scalar(mem.scales[:, 0:1], mem.scales[:, 0:1], 8.0, None, ALU.mult))
            if layer == 0:
                link(dve.tensor_tensor(nk2[:, :], nk[:, :], nk[:, :], ALU.mult))
                link(dve.reduce_sum(nkcol[:, 0:1], nk2[:, :], AX_X))
                dve.tensor_scalar(nkcol[:, 0:1], nkcol[:, 0:1], 1e-24, None, ALU.max).then_inc(var_ready, 1)
                dve.wait_ge(rstd_ready, 3)
                dve.tensor_scalar(nk[:, :], nk[:, :], nkcol[:, 1:2], None, ALU.mult).then_inc(nk_ready, 1)
                link(dve.memset(mem.null_ops[:, :, :], 0.0))
                dve.wait_ge(nk_turned, 1)
                ks = mem.scales[0:DH0, 1:2]
                link(dve.tensor_scalar(nk_hi[:, :], ps_null[:, :], ks, None, ALU.mult))
                link(dve.scalar_tensor_tensor(out=nk_lo[:, :], in0=ps_null[:, :], scalar=ks, in1=nk_hi[:, :],
                                              op0=ALU.mult, op1=ALU.subtract))
                hi = nk_hi[:, :].rearrange("p (h n) -> p h n", n=NULLS)
                lo = nk_lo[:, :].rearrange("p (h n) -> p h n", n=NULLS)
                link(dve.tensor_copy(mem.null_ops[0:DH0, :, 0:2], hi))
                link(dve.tensor_copy(mem.null_ops[DH0:P, :, 0:2], lo))
                link(dve.tensor_copy(mem.null_ops[0:DH0, :, 32:34], hi))
                link(dve.tensor_copy(mem.null_ops[0:DH0, :, 64:66], hi))
                one = slice(ROW_ONE, ROW_ONE + 1)
                link(dve.memset(mem.null_ops[one, :, 32:34], 1.0))
                link(dve.memset(mem.null_ops[one, :, 64:66], 1.0))
                for n in range(NULLS):
                    link(dve.memset(mem.null_ops[ROW_POS:ROW_POS + 1, :, 64 + n:65 + n], float(n - NULLS)))
            for n in range(NQB):
                cols = slice(QW * n, QW * n + QW)
                dve.wait_ge(tiles_turned, TPQ * n + TPQ)
                if layer == 0:
                    dve.wait_ge(act_read, n + 1)
                    dve.tensor_scalar(mem.hT[:, cols], turned[n][:, :], vecs[:, 1:2], vecs[:, 2:3],
                                      ALU.mult, ALU.add).then_inc(hT_ready, 1)
                else:
                    dve.tensor_copy(mem.hT[:, cols], turned[n][:, :]).then_inc(hT_ready, 1)
            if routed < E:
                link(dve.memset(logits[:, :, routed:E], -3e38))
            dve.wait_ge(logits_ready, 1)
            link(dve.tensor_copy(logits[:, :, 0:routed], ps_log[:, :, 0:routed]))
            best1, first1, best2, first2, diff = (small[:, n, :] for n in range(1, 6))
            less = expert_less[:, :, :]
            pick_top(link, dve, logits[:, :, :], best1, eq[:, :, :], cand[:, :, :], first1, mask[:, 0, :, :], less)
            link(dve.tensor_scalar(logits2[:, :, :], mask[:, 0, :, :], -3e38, None, ALU.mult))
            link(dve.tensor_tensor(logits2[:, :, :], logits2[:, :, :], logits[:, :, :], ALU.add))
            pick_top(link, dve, logits2[:, :, :], best2, eq[:, :, :], cand[:, :, :], first2, mask[:, 1, :, :], less)
            dve.tensor_copy(maskb[:, :, :, :], mask[:, :, :, :]).then_inc(masks_ready, 1)
            link(dve.tensor_tensor(diff, best2, best1, ALU.subtract))
            if layer == 1:
                link(dve.tensor_tensor(soft[:, :, :], logits[:, :, :], best1.unsqueeze(2).to_broadcast([P, NT, E]),
                                       ALU.subtract))
            dve.tensor_copy(small[:, 6, :], diff).then_inc(diff_ready, 1)
            dve.wait_ge(exp_ready, 2)
            ediff, den, inv = small[:, 7, :], small[:, 8, :], small[:, 9, :]
            if layer == 0:
                link(dve.tensor_scalar(den, ediff, 1.0, None, ALU.add))
                link(dve.reciprocal(pair[:, 0, :], den))
                link(dve.tensor_tensor(pair[:, 1, :], ediff, pair[:, 0, :], ALU.mult))
            else:
                link(dve.reduce_sum(den, soft[:, :, :], AX_X))
                link(dve.reciprocal(pair[:, 0, :], den))
                link(dve.tensor_tensor(pair[:, 1, :], ediff, pair[:, 0, :], ALU.mult))
                link(dve.tensor_tensor(inv, pair[:, 0, :], pair[:, 1, :], ALU.add))
                link(dve.tensor_scalar(inv, inv, 1e-9, None, ALU.add))
                link(dve.reciprocal(inv, inv))
                link(dve.tensor_tensor(pair[:, :, :], pair[:, :, :], inv.unsqueeze(1).to_broadcast([P, 2, NT]), ALU.mult))
            dve.wait_ge(counted, 2)
            link(dve.tensor_copy(total[:, :, :], ps_tot[:, :].rearrange("p (t e) -> p t e", e=E)))
            for e in range(E):
                link(dve.tensor_tensor_scan(before[:, :, e], ones_row[:, :], total[:, :, e], 0.0, ALU.mult, ALU.add))
            link(dve.tensor_tensor(before[:, :, :], before[:, :, :], total[:, :, :], ALU.subtract))
            pos_t = pos[:, :, :, :].rearrange("p k t e -> p (k t) e")
            mask_t = mask[:, :, :, :].rearrange("p k t e -> p (k t) e")
            link(dve.tensor_tensor(pos_t, before[:, :, :], ps_cnt[:, :].rearrange("p (t e) -> p t e", e=E), ALU.add))
            link(dve.tensor_tensor(pos_t, pos_t, mask_t, ALU.mult))
            place = small[:, 10:12, :].rearrange("p k t -> p (k t)")
            link(dve.reduce_sum(place, pos_t, AX_X))
            link(dve.tensor_scalar(place, place, float(capacity), None, ALU.is_lt))
            pair_t = pair[:, :, :].rearrange("p k t -> p (k t)")
            link(dve.tensor_tensor(pair_t, pair_t, place, ALU.mult))
            link(dve.tensor_tensor(pos_t, mask_t, pair_t.unsqueeze(2).to_broadcast([P, 2 * NT, E]), ALU.mult))
            link(dve.tensor_tensor(mem.gates[:, :, :], pos[:, 0, :, :], pos[:, 1, :, :], ALU.add))
            if layer == 0:
                link(dve.memset(mem.gates[:, :, E - 1:E], 1.0))
            else:
                dve.tensor_copy(gates_flat[:, :], mem.gates[:, :, :].rearrange("p t e -> p (t e)")).then_inc(gates_ready, 1)
                dve.wait_ge(gates_turned, 1)
                dve.tensor_copy(gates_T[:, :], ps_cnt[:, 0:P]).then_inc(gates_ready, 1)
                link(dve.tensor_tensor(mem.acc[:, :, :], mem.acc[:, :, :],
                                       b_o[:, :].unsqueeze(1).to_broadcast([P, NT, D]), ALU.add))
                for n in range(NQB):
                    dve.wait_ge(bias_ready, n + 1)
                    acc = mem.acc[:, TPQ * n:TPQ * n + TPQ, :].rearrange("p t d -> p (t d)")
                    link(dve.tensor_tensor(acc, acc, turned[n][:, :], ALU.add))

        @block.gpsimd
        def _(pool):
            for turn in range(2 if layer == 0 else 1):
                pool.wait_ge(var_ready, turn + 1)
                pool.tensor_tensor(col[:, 4, :], col[:, 3, :], mem.minus_half[:, 0:NT], ALU.pow).then_inc(rstd_ready, 1)
            if layer == 0:
                pool.wait_ge(var_ready, 3)
                pool.tensor_tensor(nkcol[:, 1:2], nkcol[:, 0:1], mem.minus_half[0:2 * H0, 0:1], ALU.pow).then_inc(rstd_ready, 1)

        @block.scalar
        def _(act):
            if layer == 0:
                act.wait_ge(consts_loaded, loads)
            for n in range(NQB):
                cols = slice(QW * n, QW * n + QW)
                act.wait_ge(tiles_turned, TPQ * n + TPQ)
                if layer == 0:
                    act.activation(mem.yaT[:, cols], turned[n][:, :], ACT.Copy, scale=vecs[:, 0:1]).then_inc(act_read, 1)
            act.wait_ge(diff_ready, 1)
            act.activation(small[:, 7, :], small[:, 6, :], ACT.Exp).then_inc(exp_ready, 1)
            if layer == 1:
                act.activation(soft[:, :, :], soft[:, :, :], ACT.Exp).then_inc(exp_ready, 1)
            else:
                act.activation(soft[:, 0, :], small[:, 6, 0:E], ACT.Copy).then_inc(exp_ready, 1)

        @block.tensor
        def _(pe):
            pe.wait_ge(normed, 1)
            if layer == 0:
                pe.wait_ge(consts_loaded, loads)
            for t in range(NT):
                at = P * (t % TPQ)
                pe.transpose(turned[t // TPQ][:, at:at + P], mem.y[:, t, :], mem.ident[:, :]).then_inc(tiles_turned, 1)
            if layer == 0:
                pe.wait_ge(nk_ready, 1)
                pe.transpose(ps_null[:, :], nk[:, :], mem.ident[0:2 * H0, 0:2 * H0]).then_inc(nk_turned, 1)
            for t in range(NT):
                pe.wait_ge(hT_ready, t // TPQ + 1)
                last = pe.matmul(ps_log[:, t, 0:routed], mem.hT[:, P * t:P * t + P], w_router[:, 0:routed],
                                 start=True, stop=True)
            last.then_inc(logits_ready, 1)
            pe.wait_ge(masks_ready, 1)
            chosen = maskb[:, :, :, :].rearrange("p k t e -> p (k t e)")
            pe.matmul(ps_cnt[:, :], mem.lower_b[:, :], chosen, start=True, stop=True).then_inc(counted, 1)
            pe.matmul(ps_tot[:, :], mem.ones_b[:, :], chosen, start=True, stop=True).then_inc(counted, 1)
            if layer == 1:
                pe.wait_ge(gates_ready, 1)
                pe.transpose(ps_cnt[:, 0:P], gates_flat[:, :], mem.ident[:, :]).then_inc(gates_turned, 1)
                pe.wait_ge(gates_ready, 2)
                for n in range(NQB):
                    pe.matmul(turned[n][:, :], gates_T[:, :], b2[:, QW * n:QW * n + QW],
                              start=True, stop=True).then_inc(bias_ready, 1)


def experts(nc, mem, layer, dram):
    with ExitStack() as ctx:
        def sb(name, shape, dt=F32):
            return ctx.enter_context(nc.sbuf_tensor(f"f_{name}_{layer}", shape, dt))

        def sem(name):
            return ctx.enter_context(nc.semaphore(f"f_{name}_{layer}"))

        def banks(name, n):
            return [ctx.enter_context(nc.psum_tensor(f"f_{name}{k}_{layer}", [P, QW], F32)) for k in range(n)]

        gated = layer == 0
        w1 = [sb(f"w1{k}", [P, F]) for k in range(2)]
        w2 = [sb(f"w2{k}", [P, FC, D]) for k in range(2)]
        if gated:
            w3 = [sb(f"w3{k}", [P, F]) for k in range(2)]
            act_out = sb("act_out", [P, 2, QW])
            ps_b = banks("ps_b", 2)
        else:
            b1 = [sb(f"b1{k}", [P, FC]) for k in range(2)]
        ps_a = banks("ps_a", 2)
        ps_y = banks("ps_y", 2)
        hidden = sb("hidden", [P, 2, FC, QW])
        gate = sb("gate", [P, 2, NT])

        loaded = [sem(f"loaded{k}") for k in range(2)]
        up_done = sem("up_done")
        act_done = sem("act_done")
        hidden_ready = sem("hidden_ready")
        down_done = sem("down_done")
        added = sem("added")
        gate_ready = sem("gate_ready")
        block = ctx.enter_context(nc.Block())
        per_load = 16 * 3
        UPS = NQB * FC
        d_w1 = dram["w1_0" if gated else "w1_1"]
        d_w2 = dram["w2_0" if gated else "w2_1"]

        @block.sync
        def _(sp):
            def load(k, e):
                sp.dma_start(w1[k][:, :], flat(d_w1[bass.ds(e, 1), :, :])).then_inc(loaded[k], 16)
                sp.dma_start(w2[k][:, :, :].rearrange("p c d -> p (c d)"), flat(d_w2[bass.ds(e, 1), :, :])).then_inc(loaded[k], 16)
                if gated:
                    sp.dma_start(w3[k][:, :], flat(dram["w3_0"][bass.ds(e, 1), :, :])).then_inc(loaded[k], 16)
                else:
                    sp.dma_start(b1[k][:, :], flat(dram["b1_1"][bass.ds(e, 1), :, :])).then_inc(loaded[k], 16)

            load(0, 0)
            load(1, 1)
            with sp.Fori(0, E // 2 - 1) as i:
                for k in range(2):
                    sp.wait_ge(down_done, (2 * i + k + 1) * NQB)
                    load(k, 2 * i + k + 2)

        @block.tensor
        def _(pe):
            def up(k, q, f, unit):
                if unit is not None:
                    pe.wait_ge(hidden_ready, unit)
                bank = f % 2
                rows = slice(P * f, P * f + P)
                cols = slice(QW * q, QW * q + QW)
                mm = pe.matmul(ps_a[bank][:, :], w1[k][:, rows], mem.hT[:, cols], start=True, stop=True)
                if gated:
                    mm = pe.matmul(ps_b[bank][:, :], w3[k][:, rows], mem.hT[:, cols], start=True, stop=True)
                mm.then_inc(up_done, 1)

            def down(k, q, ready, free):
                pe.wait_ge(hidden_ready, ready)
                pe.wait_ge(added, free)
                for j in range(TPQ):
                    for f in range(FC):
                        mm = pe.matmul(ps_y[q % 2][:, P * j:P * j + P], hidden[:, q % 2, f, P * j:P * j + P],
                                       w2[k][:, f, :], start=(f == 0), stop=(f == FC - 1))
                mm.then_inc(down_done, 1)

            with pe.Fori(0, E // 2) as i:
                for k in range(2):
                    pe.wait_ge(loaded[k], i * per_load + per_load)
                    for q in range(NQB):
                        n = UPS * k + FC * q
                        for f in range(FC):
                            up(k, q, f, i * (2 * UPS) + n + f - 1 if n + f >= 2 else None)
                            if f == 1 and q > 0:
                                down(k, q - 1, i * (2 * UPS) + n, i * (2 * NQB) + max(NQB * k + q - 2, 0) + 1)
                    down(k, NQB - 1, i * (2 * UPS) + UPS * (k + 1), i * (2 * NQB) + NQB * k + NQB - 2 + 1)

        @block.scalar
        def _(act):
            with act.Fori(0, E // 2) as i:
                for k in range(2):
                    for q in range(NQB):
                        for f in range(FC):
                            n = UPS * k + FC * q + f
                            act.wait_ge(up_done, i * (2 * UPS) + n + 1)
                            if gated:
                                if n >= 2:
                                    act.wait_ge(hidden_ready, i * (2 * UPS) + n - 1)
                                act.activation(act_out[:, f % 2, :], ps_a[f % 2][:, :], ACT.Silu).then_inc(act_done, 1)
                            else:
                                act.wait_ge(loaded[k], i * per_load + per_load)
                                act.activation(hidden[:, q % 2, f, :], ps_a[f % 2][:, :], ACT.Gelu,
                                               bias=b1[k][:, f:f + 1]).then_inc(hidden_ready, 1)

        @block.vector
        def _(dve):
            def add_up(k, q, done, at):
                dve.wait_ge(down_done, done)
                for j in range(TPQ):
                    t = TPQ * q + j
                    ins = dve.scalar_tensor_tensor(out=mem.acc[:, t, :], in0=ps_y[q % 2][:, P * j:P * j + P],
                                                   scalar=gate[:, k, t:t + 1], in1=mem.acc[:, t, :],
                                                   op0=ALU.mult, op1=ALU.add)
                ins.then_inc(added, 1)

            dve.memset(gate[:, :, :], 0.0).then_inc(added, 1)
            with dve.Fori(0, E // 2) as i:
                for k in range(2):
                    dve.wait_ge(added, i * (2 * NQB) + NQB * k + 1)
                    dve.tensor_copy(gate[:, k, :].unsqueeze(2), mem.gates[:, :, bass.ds(2 * i + k, 1)]).then_inc(gate_ready, 1)
                    dve.wait_ge(gate_ready, i * 2 + k + 1)
                    for q in range(NQB):
                        for f in range(FC):
                            n = UPS * k + FC * q + f
                            if gated:
                                dve.wait_ge(act_done, i * (2 * UPS) + n + 1)
                                dve.tensor_tensor(hidden[:, q % 2, f, :], act_out[:, f % 2, :], ps_b[f % 2][:, :],
                                                  ALU.mult).then_inc(hidden_ready, 1)
                            if f == FC - 1 and q > 0:
                                add_up(k, q - 1, i * (2 * NQB) + NQB * k + q, None)
                    add_up(k, NQB - 1, i * (2 * NQB) + NQB * (k + 1), None)


SLOT_HEAD = 8
MAX_AT = spread(range(NC0), SLOT_HEAD, 33, NB0)
TURN_AT = 35
PROJ_AT = spread(range(NT), SLOT_HEAD, 23, NB0)
TRANS_AT = spread(range(2 * NQB), 28, TURN_AT, NB0)
OUT_AT = {8: 0, 16: 1, 28: 2}


def misc_units(x, more):
    out = [[] for _ in range(NB0)]
    for b in range(NB0):
        if x == 0 and more:
            out[b] += [("proj", t) for t in PROJ_AT[b]] + [("trans", c) for c in TRANS_AT[b]]
        if b == TURN_AT and (x == 0 or more):
            out[b].append(("turn", 0))
        if x == 1 and b in OUT_AT:
            out[b].append(("out", OUT_AT[b]))
    return out


def turn_done(x, more):
    done = 0
    for part in range(x + 1):
        for units in misc_units(part, more):
            for kind, _ in units:
                done += 1
                if part == x and kind == "turn":
                    return done


def upto(x, qb):
    return REAL0 * x + sum(TPQ * q + TPQ for q in range(qb + 1))


PROJECT = NT + 2 * NQB
MISC_FIRST = PROJECT + 1
MISC_PER = PROJECT + 2 + NQB
HEAD_LOADS = 12


def attention0(nc, mem, dram):
    with ExitStack() as ctx:
        def sb(name, shape, dt=F32):
            return ctx.enter_context(nc.sbuf_tensor(f"a0_{name}", shape, dt))

        def sem(name):
            return ctx.enter_context(nc.semaphore(f"a0_{name}"))

        def banks(name, n):
            return [ctx.enter_context(nc.psum_tensor(f"a0_{name}{k}", [P, QW], F32)) for k in range(n)]

        w_qkv = sb("w_qkv", [P, 3 * P])
        w_out = sb("w_out", [P, D])
        raw = sb("raw", [P, NT, 3 * P])
        sq = sb("sq", [P, 2, TPQ, 2 * P])
        ssq = sb("ssq", [P, NT * 4])
        ssm = sb("ssm", [P, NT * 4])
        rnorm = sb("rnorm", [P, NT * 4])
        q_hi = sb("q_hi", [P, T], F16)
        q_lo = sb("q_lo", [P, T], F16)
        k_hi = sb("k_hi", [P, T], F16)
        k_lo = sb("k_lo", [P, T], F16)
        q_both = [sb(f"q_both{x}", [P, T], F16) for x in range(2)]
        k_both = [sb(f"k_both{x}", [P, T], F16) for x in range(2)]
        q_rest = [sb(f"q_rest{x}", [P, T], F16) for x in range(2)]
        q_max = [sb(f"q_max{x}", [P, T], F16) for x in range(2)]
        k_ext = [sb(f"k_ext{x}", [P, KW], F16) for x in range(2)]
        values = [sb(f"values{x}", [P, NT, P]) for x in range(2)]
        null_k = [sb(f"null_k{x}", [P, 64], F16) for x in range(2)]
        null_v = [sb(f"null_v{x}", [P, P]) for x in range(2)]
        table = [sb(f"table{x}", [P, 17 + NT]) for x in range(2)]
        prob = sb("prob", [P, 4, QW])
        null_p = [sb(f"null_p{x}", [P, QW]) for x in range(2)]
        rden = sb("rden", [P, QW])
        out_t = sb("out_t", [P, T])
        maxima = sb("maxima", [P, NT, MAXCH])
        max_all = sb("max_all", [P, NT])
        neg_max = sb("neg_max", [P, NT], F16)
        max_row = sb("max_row", [NT, P], F16)
        scratch = nc.dram_tensor("max_rows", (2, NT, P), F16).ap()

        ps_st = banks("ps_st", 2)
        ps_ot = banks("ps_ot", 2)
        ps_mx = banks("ps_mx", 2)
        ps_misc = banks("ps_misc", 2)

        w_loaded = sem("w_loaded")
        wo_loaded = sem("wo_loaded")
        zeroed = sem("zeroed")
        rows_loaded = sem("rows_loaded")
        head_loaded = [sem(f"head_loaded{x}") for x in range(2)]
        v_copied = sem("v_copied")
        st_full = sem("st_full")
        exp_done = sem("exp_done")
        pv_done = sem("pv_done")
        ot_read = sem("ot_read")
        cleared = sem("cleared")
        mx_full = sem("mx_full")
        mx_done = sem("mx_done")
        max_step = sem("max_step")
        misc_full = sem("misc_full")
        misc_done = sem("misc_done")
        row_stored = sem("row_stored")
        row_loaded = sem("row_loaded")
        sq_done = sem("sq_done")
        ss_done = sem("ss_done")
        ssm_ready = sem("ssm_ready")
        rn_ready = sem("rn_ready")
        qn_done = sem("qn_done")
        hi_done = sem("hi_done")
        den_step = sem("den_step")
        block = ctx.enter_context(nc.Block())

        def steps(more):
            for x in range(2):
                units = misc_units(x, more)
                for b in range(NB0):
                    yield x, b, BLOCKS0[b], (MAX_AT[b] if x == 0 or more else []), units[b]

        @block.sync
        def _(sp):
            def load_head(x, h):
                half = slice(DH0 * x, DH0 * x + DH0)
                low, high = slice(0, DH0), slice(DH0, P)
                done = head_loaded[x]
                sp.dma_start(k_ext[x][low, NULLS:KW], k_hi[half, :]).then_inc(done, 16)
                sp.dma_start(q_max[x][low, :], q_hi[half, :]).then_inc(done, 16)
                sp.dma_start(k_both[x][low, :], k_hi[half, :]).then_inc(done, 16)
                sp.dma_start(k_both[x][high, :], k_lo[half, :]).then_inc(done, 16)
                sp.dma_start(q_both[x][low, :], q_hi[half, :]).then_inc(done, 16)
                sp.dma_start(q_both[x][high, :], q_hi[half, :]).then_inc(done, 16)
                sp.dma_start(q_rest[x][low, :], q_lo[half, :]).then_inc(done, 16)
                sp.dma_start(q_max[x][ROW_POS:ROW_POS + 1, :], dram["slope_rows"][bass.ds(h, 1), :, :]
                             .rearrange("h t o -> h (t o)")).then_inc(done, 16)
                sp.dma_start(table[x][:, :], flat(dram["head_table"][bass.ds(h, 1), :, :])).then_inc(done, 16)
                sp.dma_start(null_k[x][:, :].unsqueeze(1), mem.null_ops[:, bass.ds(h, 1), 0:64]).then_inc(done, 16)
                sp.dma_start(k_ext[x][:, 0:NULLS].unsqueeze(1), mem.null_ops[:, bass.ds(h, 1), 64:66]).then_inc(done, 16)
                sp.dma_start(null_v[x][:, DH0 * x:DH0 * x + DH0], flat(dram["null_v"][bass.ds(h, 1), :, :])).then_inc(done, 16)

            def turn_row(x, n, done):
                sp.wait_ge(misc_done, done)
                sp.dma_start(scratch[x, :, :], max_row[:, :]).then_inc(row_stored, 16)
                sp.wait_ge(row_stored, 16 * n + 16)
                sp.dma_start(q_rest[x][ROW_ONE:ROW_ONE + 1, :],
                             scratch[x:x + 1, :, :].rearrange("o t p -> o (t p)")).then_inc(row_loaded, 16)

            def step(i, more):
                if more:
                    sp.wait_ge(misc_full, MISC_FIRST + i * MISC_PER)
                    sp.dma_start(w_qkv[:, :], flat(dram["w_qkv"][bass.ds(i + 1, 1), :, :])).then_inc(w_loaded, 16)
                else:
                    sp.wait_ge(misc_full, MISC_FIRST + i * MISC_PER)
                sp.dma_start(w_out[:, :], flat(dram["w_out"][bass.ds(i, 1), :, :])).then_inc(wo_loaded, 16)
                turn_row(1, 2 * i + 1, MISC_FIRST + i * MISC_PER + turn_done(0, more))
                if more:
                    sp.wait_ge(pv_done, i * (2 * REAL0) + REAL0)
                    load_head(0, 2 * i + 2)
                    turn_row(0, 2 * i + 2, MISC_FIRST + i * MISC_PER + turn_done(1, more))
                    sp.wait_ge(pv_done, i * (2 * REAL0) + 2 * REAL0)
                    load_head(1, 2 * i + 3)

            sp.dma_start(w_qkv[:, :], dram["w_qkv"][0]).then_inc(w_loaded, 16)
            sp.wait_ge(zeroed, 8)
            for x in range(2):
                for n, row in enumerate((ROW_ONE, ROW_POS)):
                    sp.dma_start(k_ext[x][row:row + 1, :], dram["key_rows"][n:n + 1, :]).then_inc(rows_loaded, 16)
                ones_at = DH0 * (1 - x)
                sp.dma_start(null_v[x][:, ones_at:ones_at + DH0], dram["null_ones"]).then_inc(rows_loaded, 16)
            sp.wait_ge(rows_loaded, 16 * 6)
            sp.wait_ge(misc_done, PROJECT)
            load_head(0, 0)
            load_head(1, 1)
            turn_row(0, 0, MISC_FIRST)
            with sp.Fori(0, PAIRS - 1) as i:
                step(i, True)
            step(PAIRS - 1, False)

        @block.tensor
        def _(pe):
            def transpose(c, bank):
                at = P * (c // NQB)
                for j in range(TPQ):
                    mm = pe.transpose(ps_misc[bank][:, P * j:P * j + P], raw[:, TPQ * (c % NQB) + j, at:at + P],
                                      mem.ident[:, :])
                mm.then_inc(misc_full, 1)

            def unit(kind, n, free, bank, turns, pairs):
                if free is not None:
                    pe.wait_ge(misc_done, free)
                if kind == "proj":
                    if n == 0:
                        pe.wait_ge(w_loaded, 16 * pairs + 16)
                    pe.matmul(ps_misc[bank][:, 0:3 * P], mem.yaT[:, P * n:P * n + P], w_qkv[:, :],
                              start=True, stop=True).then_inc(misc_full, 1)
                elif kind == "trans":
                    pe.wait_ge(qn_done, pairs * NQB + n % NQB + 1)
                    transpose(n, bank)
                elif kind == "turn":
                    pe.wait_ge(max_step, 2 * turns + 2)
                    pe.transpose(ps_misc[bank][:, :].bitcast(F16)[0:NT, 0:P], neg_max[:, :],
                                 mem.ident_h[:, :]).then_inc(misc_full, 1)

            def output(i, qb, bank, free):
                pe.wait_ge(misc_done, free)
                pe.wait_ge(ot_read, i * (2 * NQB) + NQB + qb + 1)
                if qb == 0:
                    pe.wait_ge(wo_loaded, 16 * i + 16)
                for j in range(TPQ):
                    at = QW * qb + P * j
                    mm = pe.matmul(ps_misc[bank][:, P * j:P * j + P], out_t[:, at:at + P], w_out[:, :],
                                   start=True, stop=True)
                mm.then_inc(misc_full, 1)

            def chunk(x, c, free):
                qt, _, a, z = CHUNKS0[c]
                if free is not None:
                    pe.wait_ge(mx_done, free)
                bank = ps_mx[c % 2]
                diag = z == NULLS + P * (qt + 1)
                mm = pe.matmul(bank[:, 0:z - a], q_max[x][:, P * qt:P * qt + P], k_ext[x][:, a:z],
                               start=True, stop=not diag)
                if diag:
                    mm = pe.matmul(bank[:, z - a - P:z - a], mem.ident_b[:, :], mem.mask_qb[:, :],
                                   start=False, stop=True)
                mm.then_inc(mx_full, 1)

            def scores(x, b):
                qb, kb = BLOCKS0[b]
                bank = ps_st[(NB0 * x + b) % 2]
                if b == 0:
                    for q in range(NQB):
                        cols = slice(QW * q, QW * q + QW)
                        rows = slice(32 * q, 32 * q + 32)
                        pe.matmul(bank[rows, :], null_k[x][:, 0:32], q_both[x][:, cols], start=True, stop=False)
                        mm = pe.matmul(bank[rows, :], null_k[x][:, 32:64], q_rest[x][:, cols], start=False, stop=True)
                else:
                    c0 = max(P * (kb - TPQ * qb), 0)
                    cols = slice(QW * qb + c0, QW * qb + QW)
                    keys = slice(P * kb, P * kb + P)
                    diag = kb >= TPQ * qb
                    pe.matmul(bank[:, c0:QW], k_both[x][:, keys], q_both[x][:, cols], start=True, stop=False)
                    mm = pe.matmul(bank[:, c0:QW], k_ext[x][:, NULLS + P * kb:NULLS + P * kb + P], q_rest[x][:, cols],
                                   start=False, stop=not diag)
                    if diag:
                        mm = pe.matmul(bank[:, c0:c0 + P], mem.ident_b[:, :], mem.mask_kb[:, P:2 * P],
                                       start=False, stop=True)
                mm.then_inc(st_full, 1)

            def weighted(i, x, b):
                if b == 0:
                    return
                qb, kb = BLOCKS0[b]
                bank = ps_ot[qb % 2]
                n = REAL0 * x + b - 1
                pe.wait_ge(exp_done, i * (2 * NB0) + NB0 * x + b + 1)
                if kb == 0:
                    if NQB * x + qb >= 2:
                        pe.wait_ge(ot_read, i * (2 * NQB) + NQB * x + qb - 1)
                    rows = slice(32 * qb, 32 * qb + 32)
                    pe.matmul(bank[:, :], null_v[x][rows, :], null_p[x][rows, :], start=True, stop=False)
                c0 = max(P * (kb - TPQ * qb), 0)
                last = kb == TPQ * qb + TPQ - 1
                mm = pe.matmul(bank[:, c0:QW], values[x][:, kb, :], prob[:, n % 4, c0:QW], start=False, stop=last)
                mm.then_inc(pv_done, 1)

            def step(i, more):
                done = 0
                chunks = 0
                before = None
                for x, b, _, maxes, units in steps(more):
                    if b == 0:
                        pe.wait_ge(head_loaded[x], i * (16 * HEAD_LOADS) + 16 * HEAD_LOADS)
                        pe.wait_ge(v_copied, 2 * i + x + 1)
                        pe.wait_ge(row_loaded, i * 32 + 16 * x + 16)
                    if NB0 * x + b >= 2:
                        pe.wait_ge(exp_done, i * (2 * NB0) + NB0 * x + b - 1)
                    scores(x, b)
                    for c in maxes:
                        if c == 0:
                            pe.wait_ge(head_loaded[1 - x], (i + x) * (16 * HEAD_LOADS) + 16 * HEAD_LOADS)
                        chunk(1 - x, c, NC0 + i * (2 * NC0) + chunks - 1)
                        chunks += 1
                    for kind, n in units:
                        free = MISC_FIRST + i * MISC_PER + done - 1
                        bank = (MISC_FIRST + done) % 2
                        if kind == "out":
                            output(i, n, bank, free)
                        else:
                            unit(kind, n, free, bank, 2 * i + 1 + x, i + 1)
                        done += 1
                    if before is not None:
                        weighted(i, *before)
                    before = (x, b)
                weighted(i, *before)
                output(i, NQB - 1, (MISC_FIRST + done) % 2, MISC_FIRST + i * MISC_PER + done - 1)

            for u, (kind, n) in enumerate([("proj", t) for t in range(NT)] + [("trans", c) for c in range(2 * NQB)]):
                unit(kind, n, u - 1 if u >= 2 else None, u % 2, 0, 0)
            pe.wait_ge(head_loaded[0], 16 * HEAD_LOADS)
            for c in range(NC0):
                chunk(0, c, c - 1 if c >= 2 else None)
            unit("turn", 0, PROJECT - 1, PROJECT % 2, 0, 0)
            with pe.Fori(0, PAIRS - 1) as i:
                step(i, True)
            step(PAIRS - 1, False)

        @block.scalar
        def _(act):
            def high(c, full, bank, pairs):
                cols = slice(QW * (c % NQB), QW * (c % NQB) + QW)
                act.wait_ge(misc_full, full)
                if pairs is not None:
                    act.wait_ge(head_loaded[1], pairs)
                k = c // NQB
                dst = (q_hi, k_hi)[k]
                act.activation(dst[:, cols], ps_misc[bank][:, :], ACT.Copy, scale=mem.scales[:, k:k + 1]).then_inc(hi_done, 1)

            def copy_values(x):
                at = 2 * P + DH0 * x
                act.activation(values[x][:, :, DH0 * x:DH0 * x + DH0], raw[:, :, at:at + DH0], ACT.Copy).then_inc(v_copied, 1)

            def step(i, more):
                done = 0
                for x, b, (qb, kb), _, units in steps(more):
                    if (x, b) == (0, 3):
                        act.wait_ge(misc_done, MISC_FIRST + i * MISC_PER)
                        copy_values(1)
                    if (x, b) == (1, 6) and more:
                        act.wait_ge(pv_done, i * (2 * REAL0) + REAL0)
                        act.wait_ge(misc_done, MISC_FIRST + i * MISC_PER + PROJECT)
                        copy_values(0)
                    act.wait_ge(st_full, i * (2 * NB0) + NB0 * x + b + 1)
                    bank = ps_st[(NB0 * x + b) % 2]
                    if b == 0:
                        act.activation(null_p[x][:, :], bank[:, :], ACT.Exp, bias=table[x][:, 16:17]).then_inc(exp_done, 1)
                    else:
                        n = REAL0 * x + b - 1
                        c0 = max(P * (kb - TPQ * qb), 0)
                        at = kb - TPQ * qb + TPQ * (NQB - 1)
                        if n >= 4:
                            act.wait_ge(pv_done, i * (2 * REAL0) + n - 3)
                        act.activation(prob[:, n % 4, c0:QW], bank[:, c0:QW], ACT.Exp,
                                       bias=table[x][:, at:at + 1]).then_inc(exp_done, 1)
                    for kind, n in units:
                        done += 1
                        if kind == "trans":
                            high(n, MISC_FIRST + i * MISC_PER + done, (MISC_FIRST + done - 1) % 2, (i + 1) * (16 * HEAD_LOADS))

            for c in range(2 * NQB):
                high(c, NT + c + 1, (NT + c) % 2, None)
            act.wait_ge(misc_done, NT)
            act.wait_ge(zeroed, 8)
            copy_values(0)
            with act.Fori(0, PAIRS - 1) as i:
                step(i, True)
            step(PAIRS - 1, False)

        @block.gpsimd
        def _(pool):
            def norms(pairs, misc):
                for g in range(NQB):
                    if g >= 2:
                        pool.wait_ge(ss_done, pairs * NQB + g - 1)
                    pool.wait_ge(misc_done, misc + TPQ * g + TPQ)
                    rows = raw[:, TPQ * g:TPQ * g + TPQ, 0:2 * P]
                    pool.tensor_tensor(sq[:, g % 2, :, :], rows, rows, ALU.mult).then_inc(sq_done, 1)
                pool.wait_ge(ssm_ready, pairs + 1)
                pool.tensor_tensor(rnorm[:, :], ssm[:, :], mem.minus_half[:, :], ALU.pow).then_inc(rn_ready, 1)
                pool.wait_ge(rn_ready, pairs + 1)
                for g in range(NQB):
                    rows = raw[:, TPQ * g:TPQ * g + TPQ, 0:2 * P].rearrange("p t (g d) -> p t g d", d=DH0)
                    r = rnorm[:, 4 * TPQ * g:4 * TPQ * (g + 1)].rearrange("p (t g) -> p t g", g=4)
                    pool.tensor_tensor(rows, rows, r.unsqueeze(3).to_broadcast([P, TPQ, 4, DH0]),
                                       ALU.mult).then_inc(qn_done, 1)

            link = chain(pool, zeroed)
            for x in range(2):
                ones_at = DH0 * (1 - x)
                link(pool.memset(q_rest[x][DH0:P, :], 0.0))
                link(pool.memset(q_max[x][DH0:P, :], 0.0))
                link(pool.memset(k_ext[x][DH0:P, :], 0.0))
                link(pool.memset(values[x][:, :, ones_at:ones_at + DH0], 1.0))
            norms(0, 0)
            with pool.Fori(0, PAIRS - 1) as i:
                norms(i + 1, MISC_FIRST + i * MISC_PER)

        @block.vector
        def _(dve):
            def unit(kind, n, full, bank, pairs, turns):
                ps = ps_misc[bank]
                dve.wait_ge(misc_full, full)
                if kind == "proj":
                    if n == 0 and pairs is not None:
                        dve.wait_ge(v_copied, 2 * pairs)
                    dve.tensor_copy(raw[:, n, :], ps[:, 0:3 * P]).then_inc(misc_done, 1)
                elif kind == "trans":
                    cols = slice(QW * (n % NQB), QW * (n % NQB) + QW)
                    k = n // NQB
                    hi, lo = ((q_hi, q_lo), (k_hi, k_lo))[k]
                    dve.wait_ge(hi_done, (0 if pairs is None else pairs * (2 * NQB)) + n + 1)
                    dve.scalar_tensor_tensor(out=lo[:, cols], in0=ps[:, :], scalar=mem.scales[:, k:k + 1],
                                             in1=hi[:, cols], op0=ALU.mult, op1=ALU.subtract).then_inc(misc_done, 1)
                elif kind == "turn":
                    if turns is not None:
                        dve.wait_ge(row_stored, 16 * turns)
                    dve.tensor_copy(max_row[:, :], ps[:, :].bitcast(F16)[0:NT, 0:P]).then_inc(misc_done, 1)
                elif kind == "out":
                    acc = mem.acc[:, TPQ * n:TPQ * n + TPQ, :].rearrange("p t d -> p (t d)")
                    dve.tensor_tensor(acc, ps[:, :], acc, ALU.add).then_inc(misc_done, 1)

            def sums(g, base):
                dve.wait_ge(sq_done, base + g + 1)
                view = sq[:, g % 2, :, :].rearrange("p t (g d) -> p (t g) d", d=DH0)
                dve.reduce_sum(ssq[:, 4 * TPQ * g:4 * TPQ * (g + 1)], view, AX_X).then_inc(ss_done, 1)
                if g == NQB - 1:
                    dve.wait_ge(ss_done, base + NQB)
                    dve.tensor_scalar(ssm[:, :], ssq[:, :], 1e-24, None, ALU.max).then_inc(ssm_ready, 1)

            def chunk(c, full):
                qt, n, a, z = CHUNKS0[c]
                dve.wait_ge(mx_full, full)
                dve.reduce_max(maxima[:, qt, n:n + 1], ps_mx[c % 2][:, 0:z - a], AX_X).then_inc(mx_done, 1)

            def finish_max(x, all_done, turns):
                dve.wait_ge(mx_done, all_done)
                dve.reduce_max(max_all[:, :], maxima[:, :, :], AX_X).then_inc(max_step, 1)
                dve.wait_ge(max_step, 2 * turns + 1)
                dve.tensor_tensor(neg_max[:, :], table[x][:, 17:17 + NT], max_all[:, :], ALU.subtract).then_inc(max_step, 1)

            def normalise(i, x, qb):
                n = NQB * x + qb
                own, other = slice(DH0 * x, DH0 * x + DH0), slice(DH0 * (1 - x), DH0 * (1 - x) + DH0)
                bank = ps_ot[qb % 2]
                dve.wait_ge(pv_done, i * (2 * REAL0) + upto(x, qb))
                dve.reciprocal(rden[own, :], bank[other, :]).then_inc(den_step, 1)
                dve.wait_ge(den_step, i * (2 * NQB) + n + 1)
                dve.tensor_tensor(out_t[own, QW * qb:QW * qb + QW], bank[own, :], rden[own, :], ALU.mult).then_inc(ot_read, 1)

            def step(i, more):
                done = 0
                chunks = 0
                groups = 0
                before = None
                for x, b, _, maxes, units in steps(more):
                    for c in maxes:
                        chunks += 1
                        chunk(c, NC0 + i * (2 * NC0) + chunks)
                        if c == NC0 - 1:
                            finish_max(1 - x, NC0 + i * (2 * NC0) + chunks, 2 * i + 1 + x)
                    for kind, n in units:
                        unit(kind, n, MISC_FIRST + i * MISC_PER + done + 1, (MISC_FIRST + done) % 2, i + 1, 2 * i + 1 + x)
                        done += 1
                        if kind == "proj" and n >= 5 and n % TPQ == 1:
                            sums(groups, (i + 1) * NQB)
                            groups += 1
                    if groups == NQB - 1 and x == 0 and b == 25:
                        sums(groups, (i + 1) * NQB)
                        groups += 1
                    if before is not None and before[1] >= 0 and before[2] == TPQ * before[1] + TPQ - 1:
                        normalise(i, before[0], before[1])
                    before = (x, *BLOCKS0[b])
                normalise(i, before[0], before[1])
                unit("out", NQB - 1, MISC_FIRST + i * MISC_PER + done + 1, (MISC_FIRST + done) % 2, None, None)

            dve.memset(maxima[:, :, :], -BIG).then_inc(cleared, 1)
            dve.wait_ge(cleared, 1)
            for t in range(NT):
                unit("proj", t, t + 1, t % 2, None, None)
            for g in range(NQB):
                sums(g, 0)
            for c in range(2 * NQB):
                unit("trans", c, NT + c + 1, (NT + c) % 2, None, None)
            dve.wait_ge(head_loaded[0], 16 * HEAD_LOADS)
            for c in range(NC0):
                chunk(c, c + 1)
            finish_max(0, NC0, 0)
            unit("turn", 0, PROJECT + 1, PROJECT % 2, None, None)
            with dve.Fori(0, PAIRS - 1) as i:
                step(i, True)
            step(PAIRS - 1, False)


SLOTS1 = [(qb, m) for qb in range(NQB) for m in range(TPQ * (qb + 1) // 2)]
NS1 = len(SLOTS1)
MAX_AT1 = spread([(a, c) for a in range(2) for c in range(NC1)], 4, 16, NS1)
TURN_AT1 = 17
SCALE1 = float(1 / np.sqrt(np.float32(DH1)))


def units1(more):
    out = [[] for _ in range(2 * NS1 + 5)]
    for x in range(2):
        if x == 0 or more:
            out[NS1 * x + TURN_AT1].append(("turn", x, 0))
        for s, (qb, m) in enumerate(SLOTS1):
            if m == TPQ * (qb + 1) // 2 - 1:
                out[NS1 * x + s + 2].append(("den", x, qb))
                out[NS1 * x + s + 4].append(("out", x, qb))
    return out


def before1(kind, x, qb, more):
    n = 0
    for units in units1(more):
        for u in units:
            n += 1
            if u == (kind, x, qb):
                return n


MISC_PER1 = 2 + 4 * NQB
HEAD_LOADS1 = 6
GROUP_LOADS = 2 * HEAD_LOADS1 + 1


def project1(nc, mem, dram, parts, values_all):
    with ExitStack() as ctx:
        def sb(name, shape, dt=F32):
            return ctx.enter_context(nc.sbuf_tensor(f"p1_{name}", shape, dt))

        def sem(name):
            return ctx.enter_context(nc.semaphore(f"p1_{name}"))

        w = sb("w", [P, 3 * P])
        bias = sb("bias", [P, 3 * P])
        rope = sb("rope", [P, 2, NT, 64])
        raw = sb("raw", [P, NT, 3 * P])
        a_cos = sb("a_cos", [P, NT, 64])
        b_sin = sb("b_sin", [P, NT, 64])
        a_sin = sb("a_sin", [P, NT, 64])
        b_cos = sb("b_cos", [P, NT, 64])
        turned = sb("turned", [P, NT, P])
        part = sb("part", [P, 2, PARTS, NT, P], BF16)
        part_t = sb("part_t", [P, 2, T], BF16)
        ps = [ctx.enter_context(nc.psum_tensor(f"p1_ps{k}", [P, QW], F32)) for k in range(2)]
        ps_t = [ctx.enter_context(nc.psum_tensor(f"p1_pt{k}", [P, 2 * QW], BF16)) for k in range(4)]

        loaded = sem("loaded")
        projected = sem("projected")
        step = sem("step")
        raw_ready = sem("raw_ready")
        v_step = sem("v_step")
        parts_ready = sem("parts_ready")
        turned_full = sem("turned_full")
        turned_read = sem("turned_read")
        stored = [sem(f"stored{k}") for k in range(2)]
        block = ctx.enter_context(nc.Block())

        @block.sync
        def _(sp):
            sp.dma_start(w[:, :], dram["w_qkv1"]).then_inc(loaded, 16)
            sp.dma_start(bias[:, :], dram["b_qkv1"].to_broadcast([P, 3 * P])).then_inc(loaded, 16)
            sp.dma_start(rope[:, :, :, :].rearrange("p c t f -> p (c t f)"), dram["rope"]).then_inc(loaded, 16)
            for n in range(2 * PARTS):
                sp.wait_ge(turned_read, 2 * n + 2)
                sp.dma_start(parts[n // PARTS, n % PARTS, :, :], part_t[:, n % 2, :]).then_inc(stored[n % 2], 16)
            for k in range(2):
                sp.wait_ge(stored[k], 16 * PARTS)

        @block.tensor
        def _(pe):
            pe.wait_ge(loaded, 48)
            for t in range(NT):
                if t >= 2:
                    pe.wait_ge(raw_ready, t - 1)
                pe.matmul(ps[t % 2][:, 0:3 * P], mem.hT[:, P * t:P * t + P], w[:, :], start=True, stop=True)\
                  .then_inc(projected, 1)
            for n in range(2 * PARTS):
                pe.wait_ge(parts_ready, n + 1)
                for half in range(2):
                    u = 2 * n + half
                    if u >= 4:
                        pe.wait_ge(turned_read, u - 3)
                    for j in range(NT // 2):
                        mm = pe.transpose(ps_t[u % 4][:, P * j:P * j + P],
                                          part[:, n // PARTS, n % PARTS, NT // 2 * half + j, :], mem.ident_b[:, :])
                    mm.then_inc(turned_full, 1)

        @block.scalar
        def _(act):
            for n in range(2 * PARTS):
                for half in range(2):
                    u = 2 * n + half
                    act.wait_ge(turned_full, u + 1)
                    if n >= 2:
                        act.wait_ge(stored[n % 2], 16 * (n // 2))
                    act.copy(part_t[:, n % 2, 2 * QW * half:2 * QW * (half + 1)], ps_t[u % 4][:, :]).then_inc(turned_read, 1)

        @block.gpsimd
        def _(pool):
            pool.memset(values_all[:, :, :, :, :], 1.0).then_inc(v_step, 1)
            pool.wait_ge(v_step, 1)
            pool.wait_ge(raw_ready, NT)
            for a in range(2):
                v = raw[:, :, 2 * P:3 * P].rearrange("p t (g a d) -> p g t a d", a=2, d=DH1)
                pool.tensor_copy(values_all[:, :, :, a, 0:DH1], v[:, :, :, a, :]).then_inc(v_step, 1)
                pool.wait_ge(v_step, a + 2)

        @block.vector
        def _(dve):
            link = chain(dve, step)
            for t in range(NT):
                dve.wait_ge(projected, t + 1)
                dve.tensor_tensor(raw[:, t, :], ps[t % 2][:, 0:3 * P], bias[:, :], ALU.add).then_inc(raw_ready, 1)
            dve.wait_ge(raw_ready, NT)
            cos, sin = rope[:, 0, :, :], rope[:, 1, :, :]
            for k in range(2):
                even, odd = raw[:, :, P * k:P * k + 64], raw[:, :, P * k + 64:P * k + P]
                link(dve.tensor_tensor(a_cos[:, :, :], even, cos, ALU.mult))
                link(dve.tensor_tensor(b_sin[:, :, :], odd, sin, ALU.mult))
                link(dve.tensor_tensor(a_sin[:, :, :], even, sin, ALU.mult))
                link(dve.tensor_tensor(b_cos[:, :, :], odd, cos, ALU.mult))
                view = turned[:, :, :].rearrange("p t (h c f) -> p t h c f", h=H1, c=2)

                def by_head(m):
                    return m[:, :, :].rearrange("p t (h f) -> p t h f", h=H1)

                link(dve.tensor_tensor(view[:, :, :, 0, :], by_head(a_cos), by_head(b_sin), ALU.subtract))
                link(dve.tensor_tensor(view[:, :, :, 1, :], by_head(a_sin), by_head(b_cos), ALU.add))
                for n in range(PARTS):
                    ins = dve.tensor_copy(part[:, k, n, :, :], turned[:, :, :])
                    ins.then_inc(parts_ready, 1)
                    dve.wait_ge(parts_ready, PARTS * k + n + 1)
                    if n < PARTS - 1:
                        link(dve.tensor_tensor(turned[:, :, :], turned[:, :, :], part[:, k, n, :, :], ALU.subtract))


def attention1(nc, mem, dram):
    with ExitStack() as outer:
        parts = nc.dram_tensor("parts1", (2, PARTS, P, T), BF16).ap()
        values_all = outer.enter_context(nc.sbuf_tensor("values_all", [P, GROUPS, NT, 2, 32], F32))
        project1(nc, mem, dram, parts, values_all)
        attend1(nc, mem, dram, parts, values_all)


def attend1(nc, mem, dram, parts, values_all):
    with ExitStack() as ctx:
        def sb(name, shape, dt=F32):
            return ctx.enter_context(nc.sbuf_tensor(f"a1_{name}", shape, dt))

        def sem(name):
            return ctx.enter_context(nc.semaphore(f"a1_{name}"))

        qs = [[sb(f"qs{x}{a}", [P, T], BF16) for a in range(2)] for x in range(2)]
        ks = [[sb(f"ks{x}{a}", [P, T], BF16) for a in range(2)] for x in range(2)]
        values = [sb(f"values{x}", [P, NT, 2, 32]) for x in range(2)]
        w_out = [sb(f"w_out{x}", [P, D]) for x in range(2)]
        select = sb("select", [P, P])
        prob = sb("prob", [P, 2, 2, 2, QW])
        sums = sb("sums", [P, 2, QW])
        rden = sb("rden", [P, QW])
        out_t = sb("out_t", [P, QW])
        maxima = sb("maxima", [P, 2 * NT, NQB])
        max_all = sb("max_all", [P, 2 * NT])
        neg_max = sb("neg_max", [P, 2 * NT], BF16)
        max_row = sb("max_row", [2 * NT, P], BF16)
        scratch = nc.dram_tensor("max_rows1", (2, 2 * NT, P), BF16).ap()
        ps_st = [ctx.enter_context(nc.psum_tensor(f"a1_st{k}", [P, 2, QW], F32)) for k in range(2)]
        ps_ot = ctx.enter_context(nc.psum_tensor("a1_ot", [P, QW], F32))
        ps_mx = [ctx.enter_context(nc.psum_tensor(f"a1_mx{k}", [P, QW], F32)) for k in range(2)]
        ps_misc = ctx.enter_context(nc.psum_tensor("a1_misc", [P, QW], F32))

        zeroed = sem("zeroed")
        select_loaded = sem("select_loaded")
        loaded = [sem(f"loaded{x}") for x in range(2)]
        out_loaded = [sem(f"out_loaded{x}") for x in range(2)]
        st_full = sem("st_full")
        exp_done = sem("exp_done")
        pv_done = sem("pv_done")
        ot_read = sem("ot_read")
        cleared = sem("cleared")
        mx_full = sem("mx_full")
        mx_done = sem("mx_done")
        max_step = sem("max_step")
        misc_full = sem("misc_full")
        misc_done = sem("misc_done")
        den_step = sem("den_step")
        row_stored = sem("row_stored")
        row_loaded = sem("row_loaded")
        block = ctx.enter_context(nc.Block())

        def slots(more):
            units = units1(more)
            for n in range(2 * NS1 + 5):
                x, s = n // NS1, n % NS1
                maxes = MAX_AT1[s] if x == 0 or (x == 1 and more) else []
                yield n, x, s, maxes, units[n]

        def upto1(x, qb):
            return NS1 * x + sum(TPQ * (q + 1) // 2 for q in range(qb + 1))

        @block.sync
        def _(sp):
            def load_group(x, g):
                for a in range(2):
                    for n in range(PARTS):
                        rows = slice(PARTS * DH1 * n, PARTS * DH1 * (n + 1))
                        sp.dma_start(qs[x][a][rows, :],
                                     parts[0].rearrange("n (g f) t -> g n f t", f=DH1)[bass.ds(2 * g + a, 1), :, :, :]
                                     .rearrange("o n f t -> (o n) f t")).then_inc(loaded[x], 16)
                        key = parts[1, n].rearrange("(g f) t -> g f t", f=DH1)[bass.ds(2 * g + a, 1), :, :]
                        sp.dma_start(ks[x][a][rows, :], key.to_broadcast([PARTS, DH1, T])).then_inc(loaded[x], 16)
                sp.dma_start(values[x][:, :, :, :].rearrange("p t a f -> p (t a f)").unsqueeze(1),
                             values_all[:, bass.ds(g, 1), :, :, :].rearrange("p g t a f -> p g (t a f)")).then_inc(loaded[x], 16)

            def load_out(x, g):
                sp.dma_start(w_out[x][:, :], flat(dram["w_out1"][bass.ds(g, 1), :, :])).then_inc(out_loaded[x], 16)

            def turn_row(x, n, done):
                sp.wait_ge(misc_done, done)
                sp.dma_start(scratch[x, :, :], max_row[:, :]).then_inc(row_stored, 16)
                sp.wait_ge(row_stored, 16 * n + 16)
                for a in range(2):
                    sp.dma_start(qs[x][a][ROW_SHIFT:ROW_SHIFT + 1, :],
                                 scratch[x:x + 1, NT * a:NT * (a + 1), :].rearrange("o t p -> o (t p)")).then_inc(row_loaded, 16)

            def step(i, more):
                turn_row(1, 2 * i + 1, 1 + i * MISC_PER1 + before1("turn", 1 - 1, 0, more))
                if more:
                    sp.wait_ge(pv_done, i * (2 * NS1) + NS1)
                    load_group(0, 2 * i + 2)
                    sp.wait_ge(misc_done, 1 + i * MISC_PER1 + before1("out", 0, NQB - 1, more))
                    load_out(0, 2 * i + 2)
                    turn_row(0, 2 * i + 2, 1 + i * MISC_PER1 + before1("turn", 1, 0, more))
                    sp.wait_ge(pv_done, i * (2 * NS1) + 2 * NS1)
                    load_group(1, 2 * i + 3)
                    sp.wait_ge(misc_done, 1 + i * MISC_PER1 + MISC_PER1)
                    load_out(1, 2 * i + 3)

            sp.dma_start(select[:, :], dram["den_select"]).then_inc(select_loaded, 16)
            sp.wait_ge(zeroed, 12)
            for x in range(2):
                load_group(x, x)
                load_out(x, x)
            turn_row(0, 0, 1)
            with sp.Fori(0, GROUPS // 2 - 1) as i:
                step(i, True)
            step(GROUPS // 2 - 1, False)

        @block.gpsimd
        def _(pool):
            link = chain(pool, zeroed)
            for x in range(2):
                for a in range(2):
                    link(pool.memset(qs[x][a][:, :], 0.0))
                    link(pool.memset(ks[x][a][:, :], 0.0))
                    link(pool.memset(ks[x][a][ROW_SHIFT:ROW_SHIFT + 1, :], 1.0))

        @block.tensor
        def _(pe):
            def chunk(x, a, c, static, free):
                qt, _, lo, hi = CHUNKS1[c]
                if free is not None:
                    pe.wait_ge(mx_done, free)
                bank = ps_mx[static % 2]
                diag = hi == P * (qt + 1)
                mm = pe.matmul(bank[:, 0:hi - lo], qs[x][a][0:STACK, P * qt:P * qt + P], ks[x][a][0:STACK, lo:hi],
                               start=True, stop=not diag)
                if diag:
                    mm = pe.matmul(bank[:, hi - lo - P:hi - lo], mem.ident_b[:, :], mem.mask_qb[:, :], start=False, stop=True)
                mm.then_inc(mx_full, 1)

            def turn(turns, free):
                pe.wait_ge(max_step, 2 * turns + 2)
                if free is not None:
                    pe.wait_ge(misc_done, free)
                pe.transpose(ps_misc[:, :].bitcast(BF16)[0:2 * NT, 0:P], neg_max[:, :], mem.ident_b[:, :]).then_inc(misc_full, 1)

            def scores(x, a, s):
                qb, m = SLOTS1[s]
                bank = ps_st[a]
                c0 = max(P * (2 * m - TPQ * qb), 0)
                diag = 2 * m >= TPQ * qb
                cols = slice(QW * qb + c0, QW * qb + QW)
                for k in range(2):
                    keys = slice(P * (2 * m + k), P * (2 * m + k) + P)
                    masked = diag or (2 * m + k >= TPQ * qb)
                    mm = pe.matmul(bank[:, k, c0:QW], ks[x][a][0:ROW_SHIFT + 1, keys], qs[x][a][0:ROW_SHIFT + 1, cols],
                                   start=True, stop=not masked)
                    if masked:
                        mm = pe.matmul(bank[:, k, c0:c0 + P * (k + 1)], mem.ident_b[:, :],
                                       mem.mask_kb[:, P * (1 - k):2 * P], start=False, stop=True)
                mm.then_inc(st_full, 1)

            def weighted(i, n, x, s):
                qb, m = SLOTS1[s]
                c0 = max(P * (2 * m - TPQ * qb), 0)
                pe.wait_ge(exp_done, i * (4 * NS1) + 2 * n + 2)
                if m == 0 and NQB * x + qb >= 1:
                    pe.wait_ge(ot_read, i * (2 * NQB) + NQB * x + qb)
                for a in range(2):
                    for k in range(2):
                        rows = slice(64 * a + 32 * k, 64 * a + 32 * k + 32)
                        mm = pe.matmul(ps_ot[rows, c0:QW], values[x][:, 2 * m + k, a, :], prob[:, n % 2, a, k, c0:QW],
                                       start=(m == 0), stop=(m == TPQ * (qb + 1) // 2 - 1))
                mm.then_inc(pv_done, 1)

            def step(i, more):
                done = 0
                chunks = 0
                for n, x, s, maxes, units in slots(more):
                    if n < 2 * NS1:
                        if s == 0:
                            pe.wait_ge(loaded[x], i * (16 * GROUP_LOADS) + 16 * GROUP_LOADS)
                            pe.wait_ge(row_loaded, i * 64 + 32 * x + 32)
                        half = len(maxes) // 2
                        for a in range(2):
                            if n >= 1:
                                pe.wait_ge(exp_done, i * (4 * NS1) + 2 * n + a - 1)
                            scores(x, a, s)
                            for head, c in (maxes[:half], maxes[half:])[a]:
                                if (head, c) == (0, 0):
                                    pe.wait_ge(loaded[1 - x], (i + x) * (16 * GROUP_LOADS) + 16 * GROUP_LOADS)
                                chunk(1 - x, head, c, chunks, 2 * NC1 + i * (4 * NC1) + chunks - 1)
                                chunks += 1
                    for kind, gx, qb in units:
                        free = 1 + i * MISC_PER1 + done
                        if kind == "turn":
                            turn(2 * i + 1 + gx, free)
                        elif kind == "den":
                            pe.wait_ge(misc_done, free)
                            pe.wait_ge(ot_read, i * (2 * NQB) + NQB * gx + qb + 1)
                            pe.matmul(ps_misc[:, :], select[:, :], sums[:, qb % 2, :], start=True, stop=True).then_inc(misc_full, 1)
                        else:
                            pe.wait_ge(misc_done, free)
                            pe.wait_ge(out_loaded[gx], 16 * i + 16)
                            for j in range(TPQ):
                                mm = pe.matmul(ps_misc[:, P * j:P * j + P], out_t[:, P * j:P * j + P], w_out[gx][:, :],
                                               start=True, stop=True)
                            mm.then_inc(misc_full, 1)
                        done += 1
                    if 1 <= n <= 2 * NS1:
                        weighted(i, n - 1, (n - 1) // NS1, (n - 1) % NS1)

            pe.wait_ge(select_loaded, 16)
            pe.wait_ge(loaded[0], 16 * GROUP_LOADS)
            n = 0
            for a in range(2):
                for c in range(NC1):
                    chunk(0, a, c, n, n - 1 if n >= 2 else None)
                    n += 1
            turn(0, None)
            with pe.Fori(0, GROUPS // 2 - 1) as i:
                step(i, True)
            step(GROUPS // 2 - 1, False)

        @block.scalar
        def _(act):
            def step(i):
                for n in range(2 * NS1):
                    s = n % NS1
                    qb, m = SLOTS1[s]
                    c0 = max(P * (2 * m - TPQ * qb), 0)
                    for a in range(2):
                        act.wait_ge(st_full, i * (4 * NS1) + 2 * n + a + 1)
                        if n >= 2:
                            act.wait_ge(pv_done, i * (2 * NS1) + n - 1)
                        act.activation(prob[:, n % 2, a, :, c0:QW], ps_st[a][:, :, c0:QW], ACT.Exp,
                                       scale=SCALE1).then_inc(exp_done, 1)

            with act.Fori(0, GROUPS // 2) as i:
                step(i)

        @block.vector
        def _(dve):
            def chunk(a, c, static, full):
                qt, n, lo, hi = CHUNKS1[c]
                dve.wait_ge(mx_full, full)
                dve.reduce_max(maxima[:, NT * a + qt, n:n + 1], ps_mx[static % 2][:, 0:hi - lo], AX_X).then_inc(mx_done, 1)

            def finish_max(all_done, turns):
                dve.wait_ge(mx_done, all_done)
                dve.reduce_max(max_all[:, :], maxima[:, :, :], AX_X).then_inc(max_step, 1)
                dve.wait_ge(max_step, 2 * turns + 1)
                dve.tensor_scalar(neg_max[:, :], max_all[:, :], -1.0, None, ALU.mult).then_inc(max_step, 1)

            def turn(turns, full):
                dve.wait_ge(misc_full, full)
                if turns is not None:
                    dve.wait_ge(row_stored, 16 * turns)
                dve.tensor_copy(max_row[:, :], ps_misc[:, :].bitcast(BF16)[0:2 * NT, 0:P]).then_inc(misc_done, 1)

            def step(i, more):
                done = 0
                chunks = 0
                ends = {upto1(x, qb) - 1: (x, qb) for x in range(2) for qb in range(NQB)}
                for n, x, s, maxes, units in slots(more):
                    if n < 2 * NS1:
                        for head, c in maxes:
                            chunk(head, c, chunks, 2 * NC1 + i * (4 * NC1) + chunks + 1)
                            chunks += 1
                            if (head, c) == (1, NC1 - 1):
                                finish_max(2 * NC1 + i * (4 * NC1) + chunks, 2 * i + 1 + x)
                    for kind, gx, qb in units:
                        full = 1 + i * MISC_PER1 + done + 1
                        if kind == "turn":
                            turn(2 * i + 1 + gx, full)
                        elif kind == "den":
                            nth = i * (2 * NQB) + NQB * gx + qb
                            dve.wait_ge(misc_full, full)
                            dve.reciprocal(rden[:, :], ps_misc[:, :]).then_inc(den_step, 1)
                            dve.wait_ge(den_step, nth + 1)
                            dve.tensor_tensor(out_t[:, :], sums[:, qb % 2, :], rden[:, :], ALU.mult).then_inc(misc_done, 1)
                        else:
                            dve.wait_ge(misc_full, full)
                            acc = mem.acc[:, TPQ * qb:TPQ * qb + TPQ, :].rearrange("p t d -> p (t d)")
                            dve.tensor_tensor(acc, ps_misc[:, :], acc, ALU.add).then_inc(misc_done, 1)
                        done += 1
                    if n - 1 in ends:
                        gx, qb = ends[n - 1]
                        dve.wait_ge(pv_done, i * (2 * NS1) + n)
                        dve.tensor_copy(sums[:, qb % 2, :], ps_ot[:, :]).then_inc(ot_read, 1)

            dve.memset(maxima[:, :, :], -BIG).then_inc(cleared, 1)
            dve.wait_ge(cleared, 1)
            n = 0
            for a in range(2):
                for c in range(NC1):
                    chunk(a, c, n, n + 1)
                    n += 1
            finish_max(n, 0)
            turn(None, 1)
            with dve.Fori(0, GROUPS // 2 - 1) as i:
                step(i, True)
            step(GROUPS // 2 - 1, False)


def store(nc, mem, out):
    with ExitStack() as ctx:
        stored = ctx.enter_context(nc.semaphore("stored"))
        block = ctx.enter_context(nc.Block())

        @block.sync
        def _(sp):
            sp.dma_start(out.rearrange("(t p) d -> p t d", p=P), mem.acc[:, :, :]).then_inc(stored, 16)
            sp.wait_ge(stored, 16)


def build(nc, dram, out, phases="0af1AFs"):
    mem = Memory()
    with ExitStack() as ctx:
        def sb(name, shape, dt=F32):
            return ctx.enter_context(nc.sbuf_tensor(name, shape, dt))

        mem.acc = sb("acc", [P, NT, D])
        mem.y = sb("y", [P, NT, D])
        mem.hT = sb("hT", [P, T])
        mem.yaT = sb("yaT", [P, T])
        mem.gates = sb("gates", [P, NT, E])
        mem.ident = sb("ident_f", [P, P])
        mem.ident_b = sb("ident_b", [P, P], BF16)
        mem.ident_h = sb("ident_h", [P, P], F16)
        mem.mask_q = sb("mask_qf", [P, P])
        mem.mask_k = sb("mask_kf", [P, 2 * P])
        mem.mask_qb = sb("mask_qb", [P, P], BF16)
        mem.mask_kb = sb("mask_kb", [P, 2 * P], BF16)
        mem.lower = sb("lower_f", [P, P])
        mem.lower_b = sb("lower_b", [P, P], BF16)
        mem.ones_b = sb("ones_b", [P, P], BF16)
        mem.minus_half = sb("minus_half", [P, 4 * NT])
        mem.scales = sb("scales_s", [P, 2])
        mem.null_ops = sb("null_ops", [P, H0, 66], F16)
        if "0" in phases:
            prepare(nc, mem, 0, dram)
        if "a" in phases:
            attention0(nc, mem, dram)
        if "f" in phases:
            experts(nc, mem, 0, dram)
        if "1" in phases:
            prepare(nc, mem, 1, dram)
        if "A" in phases:
            attention1(nc, mem, dram)
        if "F" in phases:
            experts(nc, mem, 1, dram)
        store(nc, mem, out)



def slopes():
    start = 2.0 ** (-2.0 ** (-(np.log2(H0) - 3.0)))
    return np.array([start * start ** n for n in range(H0)], np.float32)


def constants():
    f = np.float32
    p = np.arange(P)
    c = {"ident": np.eye(P, dtype=f)}
    later = p[None, :] > p[:, None]
    c["mask_q"] = np.where(later, f(-BIG), f(0)).astype(f)
    c["mask_k"] = np.concatenate([np.full((P, P), -BIG, f),
                                  np.where(later.T, f(-BIG), f(0)).astype(f)], 1)
    c["lower"] = later.astype(f)
    c["expert_less"] = np.tile(np.arange(E, dtype=f) - 100, (P, NT)).astype(f)
    s = slopes()
    blocks = np.arange(-(TPQ * (NQB - 1)), TPQ)
    table = np.zeros((H0, P, len(blocks) + 1 + NT), f)
    dist = (P * blocks[None, :] + p[:, None] - ALIBI_REF).astype(f)
    s16 = s.astype(np.float16).astype(f)
    for h in range(H0):
        table[h, :, :len(blocks)] = s[h] * dist
        for q in range(NQB):
            for n in range(NULLS):
                table[h, 32 * q + n, len(blocks)] = s[h] * f(n - NULLS - QW * q - ALIBI_REF)
        table[h, :, len(blocks) + 1:] = (s16[h] * (QW * (np.arange(NT) // TPQ) + ALIBI_REF).astype(f))[None, :]
    c["head_table"] = table
    c["slope_rows"] = np.repeat(s.astype(np.float16)[:, None, None], T, 2)
    c["key_rows"] = np.stack([np.ones(KW), np.arange(KW) - NULLS]).astype(np.float16)
    ones = np.zeros((P, DH0), f)
    for q in range(NQB):
        ones[32 * q:32 * q + NULLS] = 1
    c["null_ones"] = ones
    theta = f(1) / (f(10000.0) ** (np.arange(DH1 // 2, dtype=f) / f(DH1 // 2)))
    ang = (np.arange(T, dtype=f)[:, None] * theta[None, :]).astype(f)
    cs = np.stack([np.cos(ang.astype(np.float64)), np.sin(ang.astype(np.float64))]).astype(f)
    c["rope"] = np.ascontiguousarray(np.tile(cs, (1, 1, H1)).reshape(2, NT, P, 64).transpose(2, 0, 1, 3)).reshape(P, -1)
    sel = np.zeros((P, P), f)
    for a in range(2):
        for k in range(2):
            sel[64 * a + 32 * k + DH1, 64 * a:64 * a + 64] = 1
    c["den_select"] = sel
    return c


def laid_out(v):
    w = {"x": v["L0_attn_x"].reshape(T, D)}
    w["vecs"] = np.stack([v["L0_attn_gamma"], v["L0_ffn_ln_g"], v["L0_ffn_ln_b"]], 1)
    w["scales"] = np.stack([np.tile(v["L0_attn_q_scale"], 2), np.tile(v["L0_attn_k_scale"], 2)], 1)
    nkv = v["L0_attn_null_kv"].reshape(H0, NULLS, 2, DH0)
    w["null_k"] = nkv[:, :, 0].reshape(H0 * NULLS, DH0)
    nv = np.zeros((H0, P, DH0), np.float32)
    for q in range(NQB):
        nv[:, 32 * q:32 * q + NULLS] = nkv[:, :, 1]
    w["null_v"] = nv
    wq = v["L0_attn_w_q"].reshape(D, PAIRS, P)
    wk, wv = v["L0_attn_w_kv"].reshape(D, 2, PAIRS, P).transpose(1, 0, 2, 3)
    w["w_qkv"] = np.concatenate([wq, wk, wv], 2).transpose(1, 0, 2)
    w["w_out"] = v["L0_attn_w_out"].reshape(PAIRS, P, D)
    w["router0"] = v["L0_ffn_Wr"]
    w["router1"] = v["L1_ffn_Wg"]
    w["w1_0"] = np.concatenate([v["L0_ffn_W1"], v["L0_ffn_W1s"][None]])
    w["w3_0"] = np.concatenate([v["L0_ffn_W3"], v["L0_ffn_W3s"][None]])
    w2 = np.concatenate([v["L0_ffn_W2"], v["L0_ffn_W2s"][None]])
    w["w2_0"] = w2.reshape(E, FC, P, D).transpose(0, 2, 1, 3).reshape(E, P, FC * D)
    w["w1_1"] = v["L1_ffn_W1"]
    w["w2_1"] = v["L1_ffn_W2"].reshape(E, FC, P, D).transpose(0, 2, 1, 3).reshape(E, P, FC * D)
    w["b1_1"] = v["L1_ffn_b1"].reshape(E, FC, P).transpose(0, 2, 1)
    b2 = np.zeros((NT, E, NT, D), np.float32)
    for t in range(NT):
        b2[t, :, t] = v["L1_ffn_b2"]
    w["b2_1"] = b2.reshape(P, NT * D)
    def turned(m):
        return m.reshape(H1, DH1 // 2, 2, -1).transpose(2, 0, 1, 3).reshape(D, -1)
    w["w_qkv1"] = np.concatenate([turned(v["L1_attn_W_q"]).T, turned(v["L1_attn_W_k"]).T, v["L1_attn_W_v"].T], 1)
    w["b_qkv1"] = np.concatenate([turned(v["L1_attn_b_q"])[:, 0], turned(v["L1_attn_b_k"])[:, 0], v["L1_attn_b_v"]])[None]
    wo = np.zeros((GROUPS, 2, 2, 32, D), np.float32)
    wo[:, :, :, 0:DH1] = v["L1_attn_W_o"].T.reshape(GROUPS, 2, 1, DH1, D)
    w["w_out1"] = wo.reshape(GROUPS, P, D)
    w["b_o"] = v["L1_attn_b_o"][None]
    return w


def kernel(**inputs):
    import concourse.bacc as bacc
    from concourse.bass_utils import run_bass_kernel_spmd

    nc = bacc.Bacc("TRN2", target_bir_lowering=False, num_devices=1)
    arrays, dram = {}, {}
    every = laid_out({k: np.asarray(a) for k, a in inputs.items()}) | constants()
    for name, a in every.items():
        a = np.ascontiguousarray(a)
        arrays[f"in_{name}"] = a
        dram[name] = nc.dram_tensor(f"in_{name}", a.shape, mybir.dt.from_np(a.dtype), kind="ExternalInput").ap()
    out = nc.dram_tensor("out_0", (T, D), F32, kind="ExternalOutput").ap()
    build(nc, dram, out)
    r = run_bass_kernel_spmd(nc, [arrays], core_ids=[0])
    return r.results[0]["out_0"].reshape(1, T, D)
```

```python
from contextlib import ExitStack

import numpy as np

import concourse.bass as bass
from concourse import mybir

ALU = mybir.AluOpType
ACT = mybir.ActivationFunctionType
F32 = mybir.dt.float32
F16 = mybir.dt.float16
BF16 = mybir.dt.bfloat16
U32 = mybir.dt.uint32
AX_X = mybir.AxisListType.X

P = 128
D = 128
T = 2048
NT = T // P
QW = 512
NQB = T // QW
TPQ = QW // P
EPS = 1e-5
BIG = 1e30
E = 8
F = 512
FC = F // P
CAP0 = 366
CAP1 = 2 * 2 * T // E
ROUTED = (E - 1, E)
CAPACITY = (CAP0, CAP1)
BLOCK_W = (CAP0, QW)
BLOCKS_PER = (1, CAP1 // QW)
SLOTS = (ROUTED[0] * CAP0, ROUTED[1] * CAP1)
ZERO_W = 2048
CHOICES = 2 * NT

H0 = 16
DH0 = 64
PAIRS = H0 // 2
NULLS = 2
KW = NULLS + T
ROW_ONE = 64
ROW_POS = 96
ALIBI_REF = QW // 2

H1 = 16
DH1 = 8
GROUPS = H1 // 2
PARTS = 3
STACK = PARTS * PARTS * DH1
ROW_SHIFT = 96


def flat(ap):
    return ap.rearrange("o a b -> (o a) b")


def chain(eng, sem):
    count = [0]

    def link(ins):
        count[0] += 1
        ins.then_inc(sem, 1)
        eng.wait_ge(sem, count[0])
    return link



BLOCKS0 = [(-1, -1)] + [(qb, kb) for qb in range(NQB) for kb in range(TPQ * qb + TPQ)]
NB0 = len(BLOCKS0)
REAL0 = NB0 - 1


def chunks0():
    out = []
    for qt in range(NT):
        end, at, n = NULLS + P * (qt + 1), 0, 0
        while at < end:
            stop = min(end, at + (NULLS + 3 * P if at == 0 else QW))
            out.append((qt, n, at, stop))
            at, n = stop, n + 1
    return out


CHUNKS0 = chunks0()
NC0 = len(CHUNKS0)
MAXCH = max(n for _, n, _, _ in CHUNKS0) + 1
CHUNKS1 = [(qt, c, QW * c, min(QW * (c + 1), P * (qt + 1))) for qt in range(NT) for c in range(qt // TPQ + 1)]
NC1 = len(CHUNKS1)


def spread(items, first, last, slots):
    out = [[] for _ in range(slots)]
    n = last - first + 1
    for k, it in enumerate(items):
        out[first + k * n // len(items)].append(it)
    return out


def spread_weighed(items, costs, first, last, room):
    out = [[] for _ in room]
    total, have = sum(costs), sum(room[first:last + 1])
    slot, used, limit = first, 0, room[first]
    for item, cost in zip(items, costs):
        used += cost
        while slot < last and (used - cost / 2) / total > limit / have:
            slot += 1
            limit += room[slot]
        out[slot].append(item)
    return out


class Memory:
    pass


def layer_norm(link, dve, src, dst, cen, sq, col, last, var_ready, rstd_ready, turn):
    wide = [P, NT, D]
    link(dve.reduce_sum(col[:, 0, :], src, AX_X))
    link(dve.tensor_scalar(col[:, 1, :], col[:, 0, :], 1.0 / D, None, ALU.mult))
    link(dve.tensor_tensor(cen, src, col[:, 1, :].unsqueeze(2).to_broadcast(wide), ALU.subtract))
    link(dve.tensor_tensor(sq, cen, cen, ALU.mult))
    link(dve.reduce_sum(col[:, 2, :], sq, AX_X))
    dve.tensor_scalar(col[:, 3, :], col[:, 2, :], 1.0 / D, EPS, ALU.mult, ALU.add).then_inc(var_ready, 1)
    dve.wait_ge(rstd_ready, turn)
    last(dve.tensor_tensor(dst, cen, col[:, 4, :].unsqueeze(2).to_broadcast(wide), ALU.mult))


def pick_top(link, dve, logits, best, eq, cand, first, mask, expert_less):
    wide = [P, NT, E]
    link(dve.reduce_max(best, logits, AX_X))
    link(dve.tensor_tensor(eq, logits, best.unsqueeze(2).to_broadcast(wide), ALU.is_equal))
    link(dve.tensor_scalar(cand, eq, -100.0, None, ALU.mult))
    link(dve.tensor_tensor(cand, cand, expert_less, ALU.add))
    link(dve.tensor_reduce(first, cand, AX_X, ALU.min))
    link(dve.tensor_scalar(first, first, 100.0, None, ALU.add))
    link(dve.tensor_tensor(mask, expert_less, first.unsqueeze(2).to_broadcast(wide), ALU.is_equal))


def prepare(nc, mem, layer, dram):
    routed = E - 1 if layer == 0 else E
    capacity = CAP0 if layer == 0 else CAP1
    with ExitStack() as ctx:
        def sb(name, shape, dt=F32):
            return ctx.enter_context(nc.sbuf_tensor(f"{name}_{layer}", shape, dt))

        def sem(name):
            return ctx.enter_context(nc.semaphore(f"{name}_{layer}"))

        xn = sb("xn", [P, NT, D])
        cen = sb("cen", [P, NT, D])
        sq = sb("sq", [P, NT, D])
        col = sb("col", [P, 5, NT])
        w_router = sb("w_router", [P, E])
        vecs = mem.vecs
        expert_less = sb("expert_less", [P, NT, E])
        logits = sb("logits", [P, NT, E])
        logits2 = sb("logits2", [P, NT, E])
        soft = sb("soft", [P, NT, E])
        eq = sb("eq", [P, NT, E])
        cand = sb("cand", [P, NT, E])
        mask = sb("mask", [P, 2, NT, E])
        maskb = sb("maskb", [P, 2, NT, E], BF16)
        pos = sb("pos", [P, 2, NT, E])
        total = sb("total", [P, 2 * NT, E])
        before = sb("before", [P, 2 * NT, E])
        small = sb("small", [P, 14, NT])
        keep_slot = sb("keep_slot", [P, 2, CHOICES])
        spare = sb("spare", [P, CHOICES])
        pair = sb("pair", [P, 2, NT])
        ones_row = sb("ones_row", [P, 2 * NT])
        turned = [ctx.enter_context(nc.psum_tensor(f"turned{n}_{layer}", [P, QW], F32)) for n in range(NQB)]
        ps_log = ctx.enter_context(nc.psum_tensor(f"ps_log_{layer}", [P, NT, 32], F32))
        ps_cnt = ctx.enter_context(nc.psum_tensor(f"ps_cnt_{layer}", [P, 2 * NT * E], F32))
        ps_tot = ctx.enter_context(nc.psum_tensor(f"ps_tot_{layer}", [P, 2 * NT * E], F32))

        x_loaded = sem("x_loaded")
        consts_loaded = sem("consts_loaded")
        step = sem("step")
        var_ready = sem("var_ready")
        rstd_ready = sem("rstd_ready")
        normed = sem("normed")
        tiles_turned = sem("tiles_turned")
        act_read = sem("act_read")
        hT_ready = sem("hT_ready")
        logits_ready = sem("logits_ready")
        masks_ready = sem("masks_ready")
        counted = sem("counted")
        diff_ready = sem("diff_ready")
        exp_ready = sem("exp_ready")
        xT_ready = sem("xT_ready")
        if layer == 0:
            nk = sb("nk", [2 * H0, DH0])
            nk2 = sb("nk2", [2 * H0, DH0])
            nkcol = sb("nkcol", [2 * H0, 2])
            nk_hi = sb("nk_hi", [DH0, 2 * H0], F16)
            nk_lo = sb("nk_lo", [DH0, 2 * H0], F16)
            ps_null = ctx.enter_context(nc.psum_tensor("ps_null", [DH0, 2 * H0], F32))
            nk_ready = sem("nk_ready")
            nk_turned = sem("nk_turned")
            zeros = sb("zeros", [P, ZERO_W])
            zeros_ready = sem("zeros_ready")
            zeros_stored = sem("zeros_stored")
        else:
            gates = sb("gates", [P, NT, E])
            gates_flat = sb("gates_flat", [P, NT * E])
            gates_T = sb("gates_T", [P, P])
            b2 = sb("b2", [P, NT * D])
            b_o = sb("b_o", [P, D])
            gates_ready = sem("gates_ready")
            gates_turned = sem("gates_turned")
            bias_ready = sem("bias_ready")
        block = ctx.enter_context(nc.Block())

        @block.sync
        def _(sp):
            if layer == 0:
                sp.dma_start(mem.acc[:, :, :], dram["x"].rearrange("(t p) d -> p t d", p=P)).then_inc(x_loaded, 16)
                sp.dma_start(mem.ident[:, :], dram["ident"]).then_inc(consts_loaded, 16)
                sp.dma_start(mem.mask_q[:, :], dram["mask_q"]).then_inc(consts_loaded, 16)
                sp.dma_start(mem.mask_k[:, :], dram["mask_k"]).then_inc(consts_loaded, 16)
                sp.dma_start(mem.lower[:, :], dram["lower"]).then_inc(consts_loaded, 16)
                sp.dma_start(vecs[:, :], dram["vecs"]).then_inc(consts_loaded, 16)
                sp.dma_start(nk[:, :], dram["null_k"]).then_inc(consts_loaded, 16)
                sp.dma_start(mem.scales[:, :], dram["scales"]).then_inc(consts_loaded, 16)
            else:
                sp.dma_start(b2[:, :], dram["b2_1"]).then_inc(consts_loaded, 16)
                sp.dma_start(b_o[:, :], dram["b_o"].to_broadcast([P, D])).then_inc(consts_loaded, 16)
            sp.dma_start(w_router[:, 0:routed], dram["router0" if layer == 0 else "router1"]).then_inc(consts_loaded, 16)
            sp.dma_start(spare[:, :], dram[f"spare{layer}"]).then_inc(consts_loaded, 16)
            sp.dma_start(expert_less[:, :, :], dram["expert_less"].rearrange("p (t e) -> p t e", e=E)).then_inc(consts_loaded, 16)

            if layer == 0:
                sp.wait_ge(zeros_ready, 1)
                fills = 0
                for n in range(2):
                    rows = mem.expert_in[n][0:SLOTS[n], :].rearrange("r d -> (r d)").rearrange("(p a) -> p a", p=P)
                    for at in range(0, SLOTS[n], ZERO_W):
                        end = min(at + ZERO_W, SLOTS[n])
                        sp.dma_start(rows[:, at:end], zeros[:, 0:end - at]).then_inc(zeros_stored, 16)
                        fills += 1
                sp.wait_ge(zeros_stored, 16 * fills)

        loads = 16 * (10 if layer == 0 else 5)

        @block.vector
        def _(dve):
            link = chain(dve, step)
            link(dve.memset(ones_row[:, :], 1.0))
            if layer == 0:
                link(dve.memset(mem.minus_half[:, :], -0.5))
            if layer == 0:
                dve.wait_ge(x_loaded, 16)
                layer_norm(link, dve, mem.acc[:, :, :], xn[:, :, :], cen[:, :, :], sq[:, :, :], col, link,
                           var_ready, rstd_ready, 1)
                layer_norm(link, dve, xn[:, :, :], mem.y[:, :, :], cen[:, :, :], sq[:, :, :], col,
                           lambda ins: ins.then_inc(normed, 1), var_ready, rstd_ready, 2)
            else:
                layer_norm(link, dve, mem.acc[:, :, :], mem.y[:, :, :], cen[:, :, :], sq[:, :, :], col,
                           lambda ins: ins.then_inc(normed, 1), var_ready, rstd_ready, 1)
            dve.wait_ge(consts_loaded, loads)
            if layer == 0:
                link(dve.tensor_copy(mem.ident_b[:, :], mem.ident[:, :]))
                link(dve.tensor_copy(mem.ident_h[:, :], mem.ident[:, :]))
                link(dve.tensor_copy(mem.mask_qb[:, :], mem.mask_q[:, :]))
                link(dve.tensor_copy(mem.mask_kb[:, :], mem.mask_k[:, :]))
                link(dve.tensor_copy(mem.lower_b[:, :], mem.lower[:, :]))
                link(dve.memset(mem.ones_b[:, :], 1.0))
                link(dve.tensor_scalar(mem.scales[:, 0:1], mem.scales[:, 0:1], 8.0, None, ALU.mult))
            if layer == 0:
                link(dve.tensor_tensor(nk2[:, :], nk[:, :], nk[:, :], ALU.mult))
                link(dve.reduce_sum(nkcol[:, 0:1], nk2[:, :], AX_X))
                dve.tensor_scalar(nkcol[:, 0:1], nkcol[:, 0:1], 1e-24, None, ALU.max).then_inc(var_ready, 1)
                dve.wait_ge(rstd_ready, 3)
                dve.tensor_scalar(nk[:, :], nk[:, :], nkcol[:, 1:2], None, ALU.mult).then_inc(nk_ready, 1)
                link(dve.memset(mem.null_ops[:, :, :], 0.0))
                dve.wait_ge(nk_turned, 1)
                ks = mem.scales[0:DH0, 1:2]
                link(dve.tensor_scalar(nk_hi[:, :], ps_null[:, :], ks, None, ALU.mult))
                link(dve.scalar_tensor_tensor(out=nk_lo[:, :], in0=ps_null[:, :], scalar=ks, in1=nk_hi[:, :],
                                              op0=ALU.mult, op1=ALU.subtract))
                hi = nk_hi[:, :].rearrange("p (h n) -> p h n", n=NULLS)
                lo = nk_lo[:, :].rearrange("p (h n) -> p h n", n=NULLS)
                link(dve.tensor_copy(mem.null_ops[0:DH0, :, 0:2], hi))
                link(dve.tensor_copy(mem.null_ops[DH0:P, :, 0:2], lo))
                link(dve.tensor_copy(mem.null_ops[0:DH0, :, 32:34], hi))
                link(dve.tensor_copy(mem.null_ops[0:DH0, :, 64:66], hi))
                one = slice(ROW_ONE, ROW_ONE + 1)
                link(dve.memset(mem.null_ops[one, :, 32:34], 1.0))
                link(dve.memset(mem.null_ops[one, :, 64:66], 1.0))
                for n in range(NULLS):
                    link(dve.memset(mem.null_ops[ROW_POS:ROW_POS + 1, :, 64 + n:65 + n], float(n - NULLS)))
            for n in range(NQB):
                cols = slice(QW * n, QW * n + QW)
                dve.wait_ge(tiles_turned, TPQ * n + TPQ)
                if layer == 0:
                    dve.wait_ge(act_read, n + 1)
                    dve.tensor_scalar(mem.hT[:, cols], turned[n][:, :], vecs[:, 1:2], vecs[:, 2:3],
                                      ALU.mult, ALU.add).then_inc(hT_ready, 1)
                else:
                    dve.tensor_copy(mem.hT[:, cols], turned[n][:, :]).then_inc(hT_ready, 1)
            if routed < E:
                link(dve.memset(logits[:, :, routed:E], -3e38))
            dve.wait_ge(logits_ready, 1)
            link(dve.tensor_copy(logits[:, :, 0:routed], ps_log[:, :, 0:routed]))
            best1, first1, best2, first2, diff = (small[:, n, :] for n in range(1, 6))
            less = expert_less[:, :, :]
            pick_top(link, dve, logits[:, :, :], best1, eq[:, :, :], cand[:, :, :], first1, mask[:, 0, :, :], less)
            link(dve.tensor_scalar(logits2[:, :, :], mask[:, 0, :, :], -3e38, None, ALU.mult))
            link(dve.tensor_tensor(logits2[:, :, :], logits2[:, :, :], logits[:, :, :], ALU.add))
            pick_top(link, dve, logits2[:, :, :], best2, eq[:, :, :], cand[:, :, :], first2, mask[:, 1, :, :], less)
            dve.tensor_copy(maskb[:, :, :, :], mask[:, :, :, :]).then_inc(masks_ready, 1)
            link(dve.tensor_tensor(diff, best2, best1, ALU.subtract))
            if layer == 1:
                link(dve.tensor_tensor(soft[:, :, :], logits[:, :, :], best1.unsqueeze(2).to_broadcast([P, NT, E]),
                                       ALU.subtract))
            dve.tensor_copy(small[:, 6, :], diff).then_inc(diff_ready, 1)
            dve.wait_ge(exp_ready, 2)
            ediff, den, inv = small[:, 7, :], small[:, 8, :], small[:, 9, :]
            if layer == 0:
                link(dve.tensor_scalar(den, ediff, 1.0, None, ALU.add))
                link(dve.reciprocal(pair[:, 0, :], den))
                link(dve.tensor_tensor(pair[:, 1, :], ediff, pair[:, 0, :], ALU.mult))
            else:
                link(dve.reduce_sum(den, soft[:, :, :], AX_X))
                link(dve.reciprocal(pair[:, 0, :], den))
                link(dve.tensor_tensor(pair[:, 1, :], ediff, pair[:, 0, :], ALU.mult))
                link(dve.tensor_tensor(inv, pair[:, 0, :], pair[:, 1, :], ALU.add))
                link(dve.tensor_scalar(inv, inv, 1e-9, None, ALU.add))
                link(dve.reciprocal(inv, inv))
                link(dve.tensor_tensor(pair[:, :, :], pair[:, :, :], inv.unsqueeze(1).to_broadcast([P, 2, NT]), ALU.mult))
            dve.wait_ge(counted, 2)
            link(dve.tensor_copy(total[:, :, :], ps_tot[:, :].rearrange("p (t e) -> p t e", e=E)))
            for e in range(E):
                link(dve.tensor_tensor_scan(before[:, :, e], ones_row[:, :], total[:, :, e], 0.0, ALU.mult, ALU.add))
            link(dve.tensor_tensor(before[:, :, :], before[:, :, :], total[:, :, :], ALU.subtract))
            pos_t = pos[:, :, :, :].rearrange("p k t e -> p (k t) e")
            mask_t = mask[:, :, :, :].rearrange("p k t e -> p (k t) e")
            link(dve.tensor_tensor(pos_t, before[:, :, :], ps_cnt[:, :].rearrange("p (t e) -> p t e", e=E), ALU.add))
            link(dve.tensor_tensor(pos_t, pos_t, mask_t, ALU.mult))
            place = small[:, 10:12, :].rearrange("p k t -> p (k t)")
            link(dve.reduce_sum(place, pos_t, AX_X))
            keep, slot = keep_slot[:, 0, :], keep_slot[:, 1, :]
            link(dve.tensor_scalar(keep, place, float(capacity), None, ALU.is_lt))
            chosen = small[:, 12:14, :].rearrange("p k t -> p (k t)")
            for k, first in enumerate((first1, first2)):
                link(dve.tensor_scalar(small[:, 12 + k, :], first, 100.0, float(capacity), ALU.add, ALU.mult))
            link(dve.tensor_tensor(slot, chosen, place, ALU.add))
            link(dve.tensor_tensor(slot, slot, keep, ALU.mult))
            link(dve.tensor_copy(mem.slot_from[layer][:, :], slot))
            link(dve.tensor_scalar(place, keep, -1.0, 1.0, ALU.mult, ALU.add))
            link(dve.tensor_tensor(place, place, spare[:, :], ALU.mult))
            link(dve.tensor_tensor(slot, slot, place, ALU.add))
            link(dve.tensor_copy(mem.slot_to[layer][:, :], slot))
            pair_t = pair[:, :, :].rearrange("p k t -> p (k t)")
            link(dve.tensor_tensor(mem.weights[layer][:, :], pair_t, keep, ALU.mult))
            if layer == 1:
                link(dve.tensor_tensor(pos_t, mask_t, mem.weights[layer][:, :].unsqueeze(2).to_broadcast([P, 2 * NT, E]), ALU.mult))
                link(dve.tensor_tensor(gates[:, :, :], pos[:, 0, :, :], pos[:, 1, :, :], ALU.add))
                dve.tensor_copy(gates_flat[:, :], gates[:, :, :].rearrange("p t e -> p (t e)")).then_inc(gates_ready, 1)
                dve.wait_ge(gates_turned, 1)
                dve.tensor_copy(gates_T[:, :], ps_cnt[:, 0:P]).then_inc(gates_ready, 1)
                link(dve.tensor_tensor(mem.acc[:, :, :], mem.acc[:, :, :],
                                       b_o[:, :].unsqueeze(1).to_broadcast([P, NT, D]), ALU.add))
                for n in range(NQB):
                    dve.wait_ge(bias_ready, n + 1)
                    acc = mem.acc[:, TPQ * n:TPQ * n + TPQ, :].rearrange("p t d -> p (t d)")
                    link(dve.tensor_tensor(acc, acc, turned[n][:, :], ALU.add))

        @block.gpsimd
        def _(pool):
            if layer == 0:
                pool.memset(zeros[:, :], 0.0).then_inc(zeros_ready, 1)
            for turn in range(2 if layer == 0 else 1):
                pool.wait_ge(var_ready, turn + 1)
                pool.tensor_tensor(col[:, 4, :], col[:, 3, :], mem.minus_half[:, 0:NT], ALU.pow).then_inc(rstd_ready, 1)
            if layer == 0:
                pool.wait_ge(var_ready, 3)
                pool.tensor_tensor(nkcol[:, 1:2], nkcol[:, 0:1], mem.minus_half[0:2 * H0, 0:1], ALU.pow).then_inc(rstd_ready, 1)

        @block.scalar
        def _(act):
            if layer == 0:
                act.wait_ge(consts_loaded, loads)
            for n in range(NQB):
                cols = slice(QW * n, QW * n + QW)
                act.wait_ge(tiles_turned, TPQ * n + TPQ)
                if layer == 0:
                    act.activation(mem.yaT[:, cols], turned[n][:, :], ACT.Copy, scale=vecs[:, 0:1]).then_inc(act_read, 1)
            act.wait_ge(diff_ready, 1)
            act.activation(small[:, 7, :], small[:, 6, :], ACT.Exp).then_inc(exp_ready, 1)
            if layer == 1:
                act.activation(soft[:, :, :], soft[:, :, :], ACT.Exp).then_inc(exp_ready, 1)
            else:
                act.activation(soft[:, 0, :], small[:, 6, 0:E], ACT.Copy).then_inc(exp_ready, 1)

        @block.tensor
        def _(pe):
            pe.wait_ge(normed, 1)
            if layer == 0:
                pe.wait_ge(consts_loaded, loads)
            for t in range(NT):
                at = P * (t % TPQ)
                pe.transpose(turned[t // TPQ][:, at:at + P], mem.y[:, t, :], mem.ident[:, :]).then_inc(tiles_turned, 1)
            if layer == 0:
                pe.wait_ge(nk_ready, 1)
                pe.transpose(ps_null[:, :], nk[:, :], mem.ident[0:2 * H0, 0:2 * H0]).then_inc(nk_turned, 1)
            for t in range(NT):
                pe.wait_ge(hT_ready, t // TPQ + 1)
                last = pe.matmul(ps_log[:, t, 0:routed], mem.hT[:, P * t:P * t + P], w_router[:, 0:routed],
                                 start=True, stop=True)
            last.then_inc(logits_ready, 1)
            pe.wait_ge(masks_ready, 1)
            chosen = maskb[:, :, :, :].rearrange("p k t e -> p (k t e)")
            pe.matmul(ps_cnt[:, :], mem.lower_b[:, :], chosen, start=True, stop=True).then_inc(counted, 1)
            pe.matmul(ps_tot[:, :], mem.ones_b[:, :], chosen, start=True, stop=True).then_inc(counted, 1)
            if layer == 1:
                pe.wait_ge(gates_ready, 1)
                pe.transpose(ps_cnt[:, 0:P], gates_flat[:, :], mem.ident[:, :]).then_inc(gates_turned, 1)
                pe.wait_ge(gates_ready, 2)
                for n in range(NQB):
                    pe.matmul(turned[n][:, :], gates_T[:, :], b2[:, QW * n:QW * n + QW],
                              start=True, stop=True).then_inc(bias_ready, 1)


def scatter(pool, mem, layer, scattered):
    for c in range(CHOICES):
        pool.indirect_dma_start(mem.expert_in[layer][:, :], bass.IndirectOffsetOnAxis(ap=mem.slot_to[layer][:, c:c + 1], axis=0),
                                mem.y[:, c % NT, :], None).then_inc(scattered, 16)
    pool.wait_ge(scattered, 16 * CHOICES)


def gather(pool, mem, layer, back, gathered):
    for c in range(CHOICES):
        pool.indirect_dma_start(back[:, c, :], None, mem.expert_out[layer][:, :],
                                bass.IndirectOffsetOnAxis(ap=mem.slot_from[layer][:, c:c + 1], axis=0)).then_inc(gathered, 16)
    pool.wait_ge(gathered, 16 * CHOICES)


def combine(dve, mem, layer, back, gathered, combined):
    dve.wait_ge(gathered, 16 * CHOICES)
    for c in range(CHOICES):
        t = c % NT
        if c == NT:
            dve.wait_ge(combined, NT)
        dve.scalar_tensor_tensor(out=mem.acc[:, t, :], in0=back[:, c, :], scalar=mem.weights[layer][:, c:c + 1],
                                 in1=mem.acc[:, t, :], op0=ALU.mult, op1=ALU.add).then_inc(combined, 1)
    dve.wait_ge(combined, CHOICES)


def experts(nc, mem, layer, dram):
    with ExitStack() as ctx:
        def sb(name, shape, dt=F32):
            return ctx.enter_context(nc.sbuf_tensor(f"f_{name}_{layer}", shape, dt))

        def sem(name):
            return ctx.enter_context(nc.semaphore(f"f_{name}_{layer}"))

        def banks(name, n):
            return [ctx.enter_context(nc.psum_tensor(f"f_{name}{k}_{layer}", [P, QW], F32)) for k in range(n)]

        gated = layer == 0
        routed, width, per = ROUTED[layer], BLOCK_W[layer], BLOCKS_PER[layer]
        tiles = [(at, min(P, width - at)) for at in range(0, width, P)]
        shared = NQB if gated else 0
        step_blocks = 2 * per
        w1 = [sb(f"w1{k}", [P, F]) for k in range(2)]
        w2 = [sb(f"w2{k}", [P, FC, D]) for k in range(2)]
        if gated:
            w3 = [sb(f"w3{k}", [P, F]) for k in range(2)]
            act_out = sb("act_out", [P, 2, QW])
            ps_b = banks("ps_b", 2)
        else:
            b1 = [sb(f"b1{k}", [P, FC]) for k in range(2)]
        rows = [sb(f"rows{k}", [P, TPQ, D]) for k in range(2)]
        x_t = [sb(f"x_t{k}", [P, QW]) for k in range(2)]
        hidden = sb("hidden", [P, 2, FC, QW])
        result = [sb(f"result{k}", [P, TPQ, D]) for k in range(2)]
        ps_x = banks("ps_x", 2)
        ps_a = banks("ps_a", 2)
        ps_y = banks("ps_y", 2)

        moved = sem("moved")
        loaded = [sem(f"loaded{k}") for k in range(2)]
        rows_loaded = [sem(f"rows_loaded{k}") for k in range(2)]
        turned = sem("turned")
        x_ready = sem("x_ready")
        up_done = sem("up_done")
        act_done = sem("act_done")
        hidden_ready = sem("hidden_ready")
        down_done = sem("down_done")
        y_read = sem("y_read")
        stored = [sem(f"stored{k}") for k in range(2)]
        block = ctx.enter_context(nc.Block())
        per_load = 16 * 3
        whole, odd = divmod(width, P)
        row_dmas = 16 * (2 if odd else 1)
        d_w1 = dram["w1_0" if gated else "w1_1"]
        d_w2 = dram["w2_0" if gated else "w2_1"]
        in_rows = mem.expert_in[layer][0:SLOTS[layer], :].rearrange("(g r) d -> g r d", r=width)
        out_rows = mem.expert_out[layer].rearrange("(g r) d -> g r d", r=width)

        all_blocks = routed * per

        def run(eng, step):
            loops = (routed - 2) // 2
            with eng.Fori(0, loops) as i:
                step(i, step_blocks)
            for i in range(loops, (routed + 1) // 2):
                step(i, min(step_blocks, all_blocks - i * step_blocks))

        def is_block(g):
            return not isinstance(g, int) or g < all_blocks

        def pieces(sb_rows, dram_block):
            flat_block = dram_block.rearrange("o r d -> (o r) d")
            yield sb_rows[:, 0:whole, :], flat_block[0:P * whole, :].rearrange("(c p) d -> p c d", p=P)
            if odd:
                yield sb_rows[0:odd, whole, :], flat_block[P * whole:width, :]

        @block.sync
        def _(sp):
            def load(k, e):
                sp.dma_start(w1[k][:, :], flat(d_w1[bass.ds(e, 1), :, :])).then_inc(loaded[k], 16)
                sp.dma_start(w2[k][:, :, :].rearrange("p c d -> p (c d)"), flat(d_w2[bass.ds(e, 1), :, :])).then_inc(loaded[k], 16)
                if gated:
                    sp.dma_start(w3[k][:, :], flat(dram["w3_0"][bass.ds(e, 1), :, :])).then_inc(loaded[k], 16)
                else:
                    sp.dma_start(b1[k][:, :], flat(dram["b1_1"][bass.ds(e, 1), :, :])).then_inc(loaded[k], 16)

            def load_rows(k, g):
                for here, there in pieces(rows[k], in_rows[bass.ds(g, 1), :, :]):
                    sp.dma_start(here, there).then_inc(rows_loaded[k], 16)

            def store_rows(n, g):
                sp.wait_ge(y_read, g + (shared + 1 + 2))
                for here, there in pieces(result[n % 2], out_rows[bass.ds(g, 1), :, :]):
                    sp.dma_start(there, here).then_inc(stored[n % 2], 16)

            def step(i, blocks):
                for n in range(blocks):
                    g = i * step_blocks + n
                    if is_block(g + 2):
                        sp.wait_ge(turned, g + 1)
                        load_rows(n % 2, g + 2)
                    if n % per == per - 1 and is_block(g + per * 2):
                        sp.wait_ge(down_done, g + (shared + 1))
                        load(n // per, i * 2 + (n // per + 2))
                    if n > 0:
                        store_rows(n - 1, g - 1)
                store_rows(blocks - 1, g)

            if gated:
                load(1, E - 1)
            load(0, 0)
            if gated:
                sp.wait_ge(down_done, shared)
            load(1, 1)
            if gated:
                sp.wait_ge(moved, 16 * CHOICES)
            load_rows(0, 0)
            load_rows(1, 1)
            run(sp, step)
            for n in range(2):
                sp.wait_ge(stored[n], row_dmas * ((all_blocks + 1 - n) // 2 + 1))

        if gated:
            @block.gpsimd
            def _(pool):
                scatter(pool, mem, layer, moved)

        @block.tensor
        def _(pe):
            def turn_rows(i, n):
                k = n % 2
                pe.wait_ge(rows_loaded[k], i * (per * row_dmas) + (n // 2 + 1) * row_dmas)
                for c, (at, count) in enumerate(tiles):
                    mm = pe.transpose(ps_x[k][:, at:at + count], rows[k][0:count, c, :], mem.ident[0:count, 0:count])
                mm.then_inc(turned, 1)

            def up(k, src, w, f, free):
                if free is not None:
                    pe.wait_ge(hidden_ready, free)
                at = slice(P * f, P * f + P)
                mm = pe.matmul(ps_a[f % 2][:, 0:w], w1[k][:, at], src, start=True, stop=True)
                if gated:
                    mm = pe.matmul(ps_b[f % 2][:, 0:w], w3[k][:, at], src, start=True, stop=True)
                mm.then_inc(up_done, 1)

            def down(k, b, where, ready, free):
                pe.wait_ge(hidden_ready, ready)
                pe.wait_ge(y_read, free)
                for at, count in where:
                    for f in range(FC):
                        mm = pe.matmul(ps_y[b][0:count, at:at + D], hidden[:, b, f, at:at + count],
                                       w2[k][:, f, :], start=(f == 0), stop=(f == FC - 1))
                mm.then_inc(down_done, 1)

            def step(i, blocks):
                for n in range(blocks):
                    g = i * step_blocks + n
                    k = n // per
                    src = x_t[n % 2][:, 0:width]
                    if n % per == 0:
                        pe.wait_ge(loaded[k], (i + (k if gated else 0)) * per_load + per_load)
                    pe.wait_ge(x_ready, g + 1)
                    for f in range(FC):
                        up(k, src, width, f, g * FC + (shared * FC + f - 1) if n > 0 or f >= 2 else None)
                        if f == 0 and is_block(g + 1):
                            turn_rows(*((i, n + 1) if n + 1 < step_blocks else (i + 1, 0)))
                        if f == 1 and n > 0:
                            down((n - 1) // per, (n - 1) % 2, tiles, (g + shared) * FC, g + shared)
                down((blocks - 1) // per, (blocks - 1) % 2, tiles, g * FC + (shared + 1) * FC, g + (shared + 1))

            if gated:
                pe.wait_ge(loaded[1], per_load)
                full_tiles = [(P * j, P) for j in range(TPQ)]
                for q in range(NQB):
                    for f in range(FC):
                        unit = FC * q + f
                        up(1, mem.hT[:, QW * q:QW * q + QW], QW, f, unit - 1 if unit >= 2 else None)
                        if f == 1 and q > 0:
                            down(1, (q - 1) % 2, full_tiles, FC * q, q)
                down(1, (NQB - 1) % 2, full_tiles, FC * NQB, NQB)
            turn_rows(0, 0)
            run(pe, step)

        @block.scalar
        def _(act):
            def unit(k, b, w, f, done, n):
                act.wait_ge(up_done, done)
                if gated:
                    if n is not None:
                        act.wait_ge(hidden_ready, n)
                    act.activation(act_out[:, f % 2, 0:w], ps_a[f % 2][:, 0:w], ACT.Silu).then_inc(act_done, 1)
                else:
                    act.activation(hidden[:, b, f, 0:w], ps_a[f % 2][:, 0:w], ACT.Gelu,
                                   bias=b1[k][:, f:f + 1]).then_inc(hidden_ready, 1)

            def step(i, blocks):
                for n in range(blocks):
                    g = i * step_blocks + n
                    k = n // per
                    if not gated and n % per == 0:
                        act.wait_ge(loaded[k], i * per_load + per_load)
                    for f in range(FC):
                        unit(k, n % 2, width, f, g * FC + (shared * FC + f + 1), g * FC + (shared * FC + f - 1))

            for q in range(shared):
                for f in range(FC):
                    u = FC * q + f
                    unit(1, q % 2, QW, f, u + 1, u - 1 if u >= 2 else None)
            run(act, step)

        @block.vector
        def _(dve):
            def gate_unit(b, w, f, done):
                dve.wait_ge(act_done, done)
                dve.tensor_tensor(hidden[:, b, f, 0:w], act_out[:, f % 2, 0:w], ps_b[f % 2][:, 0:w],
                                  ALU.mult).then_inc(hidden_ready, 1)

            def turn_x(g, b):
                dve.wait_ge(turned, g + 1)
                if gated:
                    dve.tensor_scalar(x_t[b][:, 0:width], ps_x[b][:, 0:width], mem.vecs[:, 1:2], mem.vecs[:, 2:3],
                                      ALU.mult, ALU.add).then_inc(x_ready, 1)
                else:
                    dve.tensor_copy(x_t[b][:, 0:width], ps_x[b][:, 0:width]).then_inc(x_ready, 1)

            def take(b, done, before):
                dve.wait_ge(down_done, done)
                dve.wait_ge(stored[b], before)
                for here, there in ([(result[b][:, 0:whole, :], ps_y[b][:, 0:P * whole])] +
                                    ([(result[b][0:odd, whole:whole + 1, :], ps_y[b][0:odd, P * whole:P * whole + D])] if odd else [])):
                    ins = dve.tensor_copy(here.rearrange("p c d -> p (c d)"), there)
                ins.then_inc(y_read, 1)

            def add_shared(q):
                dve.wait_ge(down_done, q + 1)
                acc = mem.acc[:, TPQ * q:TPQ * q + TPQ, :].rearrange("p t d -> p (t d)")
                dve.tensor_tensor(acc, ps_y[q % 2][:, :], acc, ALU.add).then_inc(y_read, 1)

            def step(i, blocks):
                for n in range(blocks):
                    g = i * step_blocks + n
                    for f in range(FC):
                        if f == 1 and is_block(g + 1):
                            turn_x(g + 1, (n + 1) % 2)
                        if gated:
                            gate_unit(n % 2, width, f, g * FC + (shared * FC + f + 1))
                        if f == FC - 1 and n > 0:
                            take((n - 1) % 2, g + shared, i * (per * row_dmas) + ((n - 1) // 2 + 1) * row_dmas)
                take((blocks - 1) % 2, g + (shared + 1), i * (per * row_dmas) + ((blocks - 1) // 2 + 1) * row_dmas)

            dve.memset(result[0][:, 0, 0:1], 0.0).then_inc(y_read, 2)
            dve.memset(result[0][:, 0, 1:2], 0.0).then_inc(stored[0], row_dmas)
            dve.memset(result[1][:, 0, 0:1], 0.0).then_inc(stored[1], row_dmas)
            for q in range(shared):
                for f in range(FC):
                    gate_unit(q % 2, QW, f, FC * q + f + 1)
                    if f == FC - 1 and q > 0:
                        add_shared(q - 1)
            if gated:
                add_shared(NQB - 1)
            turn_x(0, 0)
            run(dve, step)


FLAT0 = 5000
SLOT_HEAD = 8
ROOM0 = [FLAT0 + QW - max(P * (kb - TPQ * qb), 0) for qb, kb in BLOCKS0]
MAX_AT = spread_weighed(range(NC0), [64 + end - at for _, _, at, end in CHUNKS0], SLOT_HEAD, 33, ROOM0)
TURN_AT = 35
PROJ_AT = spread(range(NT), SLOT_HEAD, 23, NB0)
TRANS_AT = spread(range(2 * NQB), 28, TURN_AT, NB0)
OUT_AT = {9: 0, 17: 1, 29: 2}
OUT_LATE = 6
SQUARE_AT, POWER_AT, NORM_AT = ({first + TPQ * g: g for g in range(NQB)} for first in (12, 15, 18))
TAKE_AT = {sum(TPQ * q + TPQ for q in range(qb + 1)) + 3: (0, qb) for qb in range(NQB - 1)} | {3: (-1, NQB - 1)}
NPROB = 8


PROJECT = NT + 2 * NQB
MISC_FIRST = PROJECT + 1
MISC_PER = PROJECT + 2 + 4 * NQB


def misc_units(x, more, first):
    out = [[] for _ in range(NB0)]
    for b in range(NB0):
        if x == 0 and more:
            out[b] += [("proj", t) for t in PROJ_AT[b]] + [("trans", c) for c in TRANS_AT[b]]
        if b == TURN_AT and (x == 0 or more):
            out[b].append(("turn", 0))
        if b in OUT_AT:
            out[b] += [("den", (x, OUT_AT[b])), ("out", (x, OUT_AT[b]))]
        if b == OUT_LATE and (x == 1 or not first):
            out[b] += [("den", (x - 1, NQB - 1)), ("out", (x - 1, NQB - 1))]
    return out


def done_by(kind, n, more, first, x=None):
    done = 0
    for part in range(2):
        for units in misc_units(part, more, first):
            for unit in units:
                done += 1
                if unit == (kind, n) and x in (None, part):
                    return done


def before_step(i, first):
    return MISC_FIRST if first else i * MISC_PER + (MISC_FIRST - 2)


AFTER_LAST = before_step(PAIRS, False) - PROJECT - 1


def upto(x, qb):
    return REAL0 * x + sum(TPQ * q + TPQ for q in range(qb + 1))


HEAD_LOADS = 12


def attention0(nc, mem, dram, routed=True):
    with ExitStack() as ctx:
        def sb(name, shape, dt=F32):
            return ctx.enter_context(nc.sbuf_tensor(f"a0_{name}", shape, dt))

        def sem(name):
            return ctx.enter_context(nc.semaphore(f"a0_{name}"))

        def banks(name, n):
            return [ctx.enter_context(nc.psum_tensor(f"a0_{name}{k}", [P, QW], F32)) for k in range(n)]

        w_qkv = sb("w_qkv", [P, 3 * P])
        w_out = sb("w_out", [P, 2, D])
        raw = sb("raw", [P, NT, 3 * P])
        sq = sb("sq", [P, 2, TPQ, 2 * P])
        ssq = sb("ssq", [P, NT * 4])
        ssm = sb("ssm", [P, NT * 4])
        rnorm = sb("rnorm", [P, NT * 4])
        q_hi = sb("q_hi", [P, T], F16)
        q_lo = sb("q_lo", [P, T], F16)
        k_hi = sb("k_hi", [P, T], F16)
        k_lo = sb("k_lo", [P, T], F16)
        q_both = [sb(f"q_both{x}", [P, T], F16) for x in range(2)]
        k_both = [sb(f"k_both{x}", [P, T], F16) for x in range(2)]
        q_rest = [sb(f"q_rest{x}", [P, T], F16) for x in range(2)]
        q_max = [sb(f"q_max{x}", [P, T], F16) for x in range(2)]
        k_ext = [sb(f"k_ext{x}", [P, KW], F16) for x in range(2)]
        values = [sb(f"values{x}", [P, NT, DH0]) for x in range(2)]
        null_k = [sb(f"null_k{x}", [P, 64], F16) for x in range(2)]
        null_v = [sb(f"null_v{x}", [P, DH0]) for x in range(2)]
        table = [sb(f"table{x}", [P, 17 + NT]) for x in range(2)]
        prob = sb("prob", [P, NPROB, QW])
        prob_sum = sb("prob_sum", [P, NQB, QW])
        ones_col = sb("ones_col", [P, 1])
        null_ones = sb("null_ones", [P, DH0])
        null_p = [sb(f"null_p{x}", [P, QW]) for x in range(2)]
        rden = sb("rden", [P, NT])
        out_t = sb("out_t", [P, T])
        maxima = sb("maxima", [P, NT, MAXCH])
        max_all = sb("max_all", [P, NT])
        neg_max = sb("neg_max", [P, NT], F16)
        max_row = sb("max_row", [NT, P], F16)
        scratch = nc.dram_tensor("max_rows", (2, NT, P), F16).ap()

        back = sb("back", [P, CHOICES, D])

        ps_st = banks("ps_st", 2)
        ps_ot = banks("ps_ot", 2)
        ps_mx = banks("ps_mx", 2)
        ps_misc = banks("ps_misc", 2)

        gathered = sem("gathered")
        combined = sem("combined")
        w_loaded = sem("w_loaded")
        wo_loaded = sem("wo_loaded")
        zeroed = sem("zeroed")
        rows_loaded = sem("rows_loaded")
        head_loaded = [sem(f"head_loaded{x}") for x in range(2)]
        v_copied = sem("v_copied")
        st_full = sem("st_full")
        exp_done = sem("exp_done")
        pv_done = sem("pv_done")
        ot_read = sem("ot_read")
        cleared = sem("cleared")
        mx_full = sem("mx_full")
        mx_done = sem("mx_done")
        max_step = sem("max_step")
        misc_full = sem("misc_full")
        misc_done = sem("misc_done")
        row_stored = sem("row_stored")
        row_loaded = sem("row_loaded")
        sq_done = sem("sq_done")
        ss_done = sem("ss_done")
        ssm_ready = sem("ssm_ready")
        rn_ready = sem("rn_ready")
        qn_done = sem("qn_done")
        hi_done = sem("hi_done")
        added = sem("added")
        block = ctx.enter_context(nc.Block())

        def steps(more, first):
            for x in range(2):
                units = misc_units(x, more, first)
                for b in range(NB0):
                    yield x, b, BLOCKS0[b], (MAX_AT[b] if x == 0 or more else []), units[b]

        @block.sync
        def _(sp):
            def load_head(x, h):
                half = slice(DH0 * x, DH0 * x + DH0)
                low, high = slice(0, DH0), slice(DH0, P)
                done = head_loaded[x]
                sp.dma_start(k_ext[x][low, NULLS:KW], k_hi[half, :]).then_inc(done, 16)
                sp.dma_start(q_max[x][low, :], q_hi[half, :]).then_inc(done, 16)
                sp.dma_start(k_both[x][low, :], k_hi[half, :]).then_inc(done, 16)
                sp.dma_start(k_both[x][high, :], k_lo[half, :]).then_inc(done, 16)
                sp.dma_start(q_both[x][low, :], q_hi[half, :]).then_inc(done, 16)
                sp.dma_start(q_both[x][high, :], q_hi[half, :]).then_inc(done, 16)
                sp.dma_start(q_rest[x][low, :], q_lo[half, :]).then_inc(done, 16)
                sp.dma_start(q_max[x][ROW_POS:ROW_POS + 1, :], dram["slope_rows"][bass.ds(h, 1), :, :]
                             .rearrange("h t o -> h (t o)")).then_inc(done, 16)
                sp.dma_start(table[x][:, :], flat(dram["head_table"][bass.ds(h, 1), :, :])).then_inc(done, 16)
                sp.dma_start(null_k[x][:, :].unsqueeze(1), mem.null_ops[:, bass.ds(h, 1), 0:64]).then_inc(done, 16)
                sp.dma_start(k_ext[x][:, 0:NULLS].unsqueeze(1), mem.null_ops[:, bass.ds(h, 1), 64:66]).then_inc(done, 16)
                sp.dma_start(null_v[x][:, :], flat(dram["null_v"][bass.ds(h, 1), :, :])).then_inc(done, 16)

            def turn_row(x, n, done):
                sp.wait_ge(misc_done, done)
                sp.dma_start(scratch[x, :, :], max_row[:, :]).then_inc(row_stored, 16)
                sp.wait_ge(row_stored, 16 * n + 16)
                sp.dma_start(q_rest[x][ROW_ONE:ROW_ONE + 1, :],
                             scratch[x:x + 1, :, :].rearrange("o t p -> o (t p)")).then_inc(row_loaded, 16)

            def step(i, more, first=False):
                base = before_step(i, first)
                if more:
                    sp.wait_ge(misc_full, base)
                    sp.dma_start(w_qkv[:, :], flat(dram["w_qkv"][bass.ds(i + 1, 1), :, :])).then_inc(w_loaded, 16)
                if not first:
                    sp.wait_ge(misc_full, base + done_by("out", (-1, NQB - 1), more, first))
                sp.dma_start(w_out[:, :, :], dram["w_out"][bass.ds(2 * i, 2), :, :].rearrange("x p d -> p x d")).then_inc(wo_loaded, 16)
                turn_row(1, 2 * i + 1, base + done_by("turn", 0, more, first))
                if more:
                    sp.wait_ge(exp_done, i * (2 * NB0) + NB0)
                    load_head(0, 2 * i + 2)
                    turn_row(0, 2 * i + 2, base + done_by("turn", 0, more, first, x=1))
                    sp.wait_ge(exp_done, i * (2 * NB0) + 2 * NB0)
                    load_head(1, 2 * i + 3)

            sp.dma_start(w_qkv[:, :], dram["w_qkv"][0]).then_inc(w_loaded, 16)
            sp.dma_start(null_ones[:, :], dram["null_ones"]).then_inc(rows_loaded, 16)
            sp.wait_ge(zeroed, 7)
            for x in range(2):
                for n, row in enumerate((ROW_ONE, ROW_POS)):
                    sp.dma_start(k_ext[x][row:row + 1, :], dram["key_rows"][n:n + 1, :]).then_inc(rows_loaded, 16)
            sp.wait_ge(rows_loaded, 16 * 5)
            sp.wait_ge(misc_done, PROJECT)
            load_head(0, 0)
            load_head(1, 1)
            turn_row(0, 0, MISC_FIRST)
            step(0, True, first=True)
            with sp.Fori(1, PAIRS - 1) as i:
                step(i, True)
            step(PAIRS - 1, False)

        @block.tensor
        def _(pe):
            def transpose(c, bank):
                at = P * (c // NQB)
                for j in range(TPQ):
                    mm = pe.transpose(ps_misc[bank][:, P * j:P * j + P], raw[:, TPQ * (c % NQB) + j, at:at + P],
                                      mem.ident[:, :])
                mm.then_inc(misc_full, 1)

            def unit(kind, n, free, bank, turns, pairs):
                if free is not None:
                    pe.wait_ge(misc_done, free)
                if kind == "proj":
                    if n == 0:
                        pe.wait_ge(w_loaded, 16 * pairs + 16)
                    pe.matmul(ps_misc[bank][:, 0:3 * P], mem.yaT[:, P * n:P * n + P], w_qkv[:, :],
                              start=True, stop=True).then_inc(misc_full, 1)
                elif kind == "trans":
                    pe.wait_ge(qn_done, pairs * NQB + n % NQB + 1)
                    transpose(n, bank)
                elif kind == "turn":
                    pe.wait_ge(max_step, 2 * turns + 2)
                    pe.transpose(ps_misc[bank][:, :].bitcast(F16)[0:NT, 0:P], neg_max[:, :],
                                 mem.ident_h[:, :]).then_inc(misc_full, 1)

            def sums(i, x, qb, bank, free):
                pe.wait_ge(misc_done, free)
                pe.wait_ge(added, i * (2 * REAL0) + upto(x, qb))
                x = x % 2
                null = slice(32 * qb, 32 * qb + 32)
                for j in range(TPQ):
                    tile = slice(P * j, P * j + P)
                    pe.matmul(ps_misc[bank][:, j:j + 1], prob_sum[:, qb, tile], ones_col[:, :], start=True, stop=False)
                    mm = pe.matmul(ps_misc[bank][:, j:j + 1], null_p[x][null, tile], null_ones[null, 0:1],
                                   start=False, stop=True)
                mm.then_inc(misc_full, 1)

            def output(i, x, qb, bank, free):
                pe.wait_ge(misc_done, free)
                pe.wait_ge(ot_read, i * (2 * NQB) + NQB * x + qb + 1)
                x = x % 2
                if (x, qb) == (0, 0):
                    pe.wait_ge(wo_loaded, 16 * i + 16)
                for j in range(TPQ):
                    at = QW * qb + P * j
                    mm = pe.matmul(ps_misc[bank][:, P * j:P * j + P], out_t[:, at:at + P], w_out[:, x, :],
                                   start=True, stop=True)
                mm.then_inc(misc_full, 1)

            def chunk(x, c, free):
                qt, _, a, z = CHUNKS0[c]
                if free is not None:
                    pe.wait_ge(mx_done, free)
                bank = ps_mx[c % 2]
                diag = z == NULLS + P * (qt + 1)
                mm = pe.matmul(bank[:, 0:z - a], q_max[x][:, P * qt:P * qt + P], k_ext[x][:, a:z],
                               start=True, stop=not diag)
                if diag:
                    mm = pe.matmul(bank[:, z - a - P:z - a], mem.ident_b[:, :], mem.mask_qb[:, :],
                                   start=False, stop=True)
                mm.then_inc(mx_full, 1)

            def scores(x, b):
                qb, kb = BLOCKS0[b]
                bank = ps_st[(NB0 * x + b) % 2]
                if b == 0:
                    for q in range(NQB):
                        cols = slice(QW * q, QW * q + QW)
                        rows = slice(32 * q, 32 * q + 32)
                        pe.matmul(bank[rows, :], null_k[x][:, 0:32], q_both[x][:, cols], start=True, stop=False)
                        mm = pe.matmul(bank[rows, :], null_k[x][:, 32:64], q_rest[x][:, cols], start=False, stop=True)
                else:
                    c0 = max(P * (kb - TPQ * qb), 0)
                    cols = slice(QW * qb + c0, QW * qb + QW)
                    keys = slice(P * kb, P * kb + P)
                    diag = kb >= TPQ * qb
                    pe.matmul(bank[:, c0:QW], k_both[x][:, keys], q_both[x][:, cols], start=True, stop=False)
                    mm = pe.matmul(bank[:, c0:QW], k_ext[x][:, NULLS + P * kb:NULLS + P * kb + P], q_rest[x][:, cols],
                                   start=False, stop=not diag)
                    if diag:
                        mm = pe.matmul(bank[:, c0:c0 + P], mem.ident_b[:, :], mem.mask_kb[:, P:2 * P],
                                       start=False, stop=True)
                mm.then_inc(st_full, 1)

            def weighted(i, x, b, first):
                qb, kb = BLOCKS0[b]
                bank = ps_ot[qb % 2]
                pe.wait_ge(exp_done, i * (2 * NB0) + NB0 * x + b + 1)
                x = x % 2
                if kb == 1:
                    if NQB * x + qb >= 2 or not first:
                        pe.wait_ge(ot_read, i * (2 * NQB) + NQB * x + qb - 1)
                    rows = slice(32 * qb, 32 * qb + 32)
                    pe.matmul(bank[0:DH0, :], null_v[x][rows, :], null_p[x][rows, :], start=True, stop=False)
                last = kb == TPQ * qb + TPQ - 1
                for back, half in ((1, slice(DH0, P)), (0, slice(0, DH0))):
                    c0 = max(P * (kb - back - TPQ * qb), 0)
                    n = REAL0 * x + b - 1 - back
                    mm = pe.matmul(bank[half, c0:QW], values[x][:, kb - back, :], prob[:, n % NPROB, c0:QW],
                                   start=kb - back == 0, stop=last)
                mm.then_inc(pv_done, 2)

            def step(i, more, first=False):
                base = before_step(i, first)
                done = 0
                chunks = 0
                before = None if first else (-1, NB0 - 1)
                for x, b, _, maxes, units in steps(more, first):
                    if b == 0:
                        pe.wait_ge(head_loaded[x], i * (16 * HEAD_LOADS) + 16 * HEAD_LOADS)
                        pe.wait_ge(v_copied, 2 * i + x + 1)
                        pe.wait_ge(row_loaded, i * 32 + 16 * x + 16)
                    if NB0 * x + b >= 2 or not first:
                        pe.wait_ge(exp_done, i * (2 * NB0) + NB0 * x + b - 1)
                    scores(x, b)
                    for c in maxes:
                        if c == 0:
                            pe.wait_ge(head_loaded[1 - x], (i + x) * (16 * HEAD_LOADS) + 16 * HEAD_LOADS)
                        chunk(1 - x, c, NC0 + i * (2 * NC0) + chunks - 1)
                        chunks += 1
                    for kind, n in units:
                        free = base + done - 1
                        bank = (MISC_FIRST + done) % 2
                        if kind == "den":
                            sums(i, *n, bank, free)
                        elif kind == "out":
                            output(i, *n, bank, free)
                        else:
                            unit(kind, n, free, bank, 2 * i + 1 + x, i + 1)
                        done += 1
                    if b % 2 == 0:
                        if before is not None:
                            weighted(i, *before, first)
                        before = (x, b) if b > 0 else None

            for u, (kind, n) in enumerate([("proj", t) for t in range(NT)] + [("trans", c) for c in range(2 * NQB)]):
                unit(kind, n, u - 1 if u >= 2 else None, u % 2, 0, 0)
            pe.wait_ge(head_loaded[0], 16 * HEAD_LOADS)
            for c in range(NC0):
                chunk(0, c, c - 1 if c >= 2 else None)
            unit("turn", 0, PROJECT - 1, PROJECT % 2, 0, 0)
            step(0, True, first=True)
            with pe.Fori(1, PAIRS - 1) as i:
                step(i, True)
            step(PAIRS - 1, False)
            weighted(PAIRS, -1, NB0 - 1, False)
            sums(PAIRS, -1, NQB - 1, AFTER_LAST % 2, AFTER_LAST - 1)
            output(PAIRS, -1, NQB - 1, (AFTER_LAST + 1) % 2, AFTER_LAST)

        @block.scalar
        def _(act):
            def high(c, full, bank, pairs):
                cols = slice(QW * (c % NQB), QW * (c % NQB) + QW)
                act.wait_ge(misc_full, full)
                if pairs is not None:
                    act.wait_ge(head_loaded[1], pairs)
                k = c // NQB
                dst = (q_hi, k_hi)[k]
                act.activation(dst[:, cols], ps_misc[bank][:, :], ACT.Copy, scale=mem.scales[:, k:k + 1]).then_inc(hi_done, 1)

            def copy_values(x):
                at = 2 * P + DH0 * x
                act.activation(values[x][:, :, :], raw[:, :, at:at + DH0], ACT.Copy).then_inc(v_copied, 1)

            def take_out(i, x, qb, base, more, first):
                act.wait_ge(pv_done, i * (2 * REAL0) + upto(x, qb))
                if x == 1 or (x, qb) == (0, NQB - 1) and not first:
                    act.wait_ge(misc_full, base + done_by("out", (x - 1, qb), more, first))
                elif not first:
                    act.wait_ge(misc_full, base)
                act.activation(out_t[:, QW * qb:QW * qb + QW], ps_ot[qb % 2][:, :], ACT.Copy).then_inc(ot_read, 1)

            def squares(pairs, g, projected):
                if g >= 2:
                    act.wait_ge(ss_done, pairs * NQB + g - 1)
                act.wait_ge(misc_done, projected)
                act.activation(sq[:, g % 2, :, :], raw[:, TPQ * g:TPQ * g + TPQ, 0:2 * P], ACT.Square).then_inc(sq_done, 1)

            def step(i, more, first=False):
                base = before_step(i, first)
                done = 0
                for x, b, (qb, kb), _, units in steps(more, first):
                    if (x, b) == (0, 3):
                        if not first:
                            act.wait_ge(pv_done, i * (2 * REAL0))
                        act.wait_ge(misc_done, base)
                        copy_values(1)
                    if (x, b) == (1, 6) and more:
                        act.wait_ge(pv_done, i * (2 * REAL0) + REAL0)
                        act.wait_ge(misc_done, base + done_by("turn", 0, more, first))
                        copy_values(0)
                    act.wait_ge(st_full, i * (2 * NB0) + NB0 * x + b + 1)
                    bank = ps_st[(NB0 * x + b) % 2]
                    if b == 0:
                        act.activation(null_p[x][:, :], bank[:, :], ACT.Exp, bias=table[x][:, 16:17]).then_inc(exp_done, 1)
                    else:
                        n = REAL0 * x + b - 1
                        c0 = max(P * (kb - TPQ * qb), 0)
                        at = kb - TPQ * qb + TPQ * (NQB - 1)
                        if n >= NPROB or not first:
                            act.wait_ge(pv_done, i * (2 * REAL0) + (n - NPROB) // 2 * 2 + 2)
                            act.wait_ge(added, i * (2 * REAL0) + (n - NPROB) // 2 * 2 + 2)
                        act.activation(prob[:, n % NPROB, c0:QW], bank[:, c0:QW], ACT.Exp,
                                       bias=table[x][:, at:at + 1]).then_inc(exp_done, 1)
                    for kind, n in units:
                        done += 1
                        if kind == "trans":
                            high(n, base + done, (MISC_FIRST + done - 1) % 2, (i + 1) * (16 * HEAD_LOADS))
                    if x == 0 and more and b in SQUARE_AT:
                        g = SQUARE_AT[b]
                        squares(i + 1, g, base + done_by("proj", TPQ * g + TPQ - 1, more, first))
                    if b in TAKE_AT and not (first and x + TAKE_AT[b][0] < 0):
                        take_out(i, x + TAKE_AT[b][0], TAKE_AT[b][1], base, more, first)

            for g in range(NQB):
                squares(0, g, TPQ * g + TPQ)
            for c in range(2 * NQB):
                high(c, NT + c + 1, (NT + c) % 2, None)
            copy_values(0)
            step(0, True, first=True)
            with act.Fori(1, PAIRS - 1) as i:
                step(i, True)
            step(PAIRS - 1, False)
            take_out(PAIRS, -1, NQB - 1, AFTER_LAST, False, False)

        @block.gpsimd
        def _(pool):
            def power(pairs, g):
                at = slice(4 * TPQ * g, 4 * TPQ * (g + 1))
                pool.wait_ge(ssm_ready, pairs * NQB + g + 1)
                pool.tensor_tensor(rnorm[:, at], ssm[:, at], mem.minus_half[:, at], ALU.pow).then_inc(rn_ready, 1)

            def add(i, x, b, base, more, first):
                qb, kb = BLOCKS0[b]
                n = REAL0 * x + b - 1
                c0 = max(P * (kb - TPQ * qb), 0)
                into = prob_sum[:, qb, :]
                if kb == 0:
                    return
                pool.wait_ge(exp_done, i * (2 * NB0) + NB0 * x + b + 1)
                if kb == 1:
                    if x == 1 or qb == NQB - 1 and not first:
                        pool.wait_ge(misc_full, base + done_by("den", (x - 1, qb), more, first))
                    elif not first:
                        pool.wait_ge(misc_full, base)
                    if c0 > 0:
                        first = prob[:, (n - 1) % NPROB, 0:c0]
                        pool.tensor_tensor(into[:, 0:c0], first, ones_col[:, :].to_broadcast([P, c0]), ALU.mult).then_inc(added, 1)
                    pool.tensor_tensor(into[:, c0:QW], prob[:, (n - 1) % NPROB, c0:QW], prob[:, n % NPROB, c0:QW],
                                       ALU.add).then_inc(added, 1 if c0 > 0 else 2)
                else:
                    pool.wait_ge(added, i * (2 * REAL0) + n)
                    pool.tensor_tensor(into[:, c0:QW], into[:, c0:QW], prob[:, n % NPROB, c0:QW],
                                       ALU.add).then_inc(added, 1)

            def step(i, more, first=False):
                base = before_step(i, first)
                for x, b, _, _, _ in steps(more, first):
                    if b > 0:
                        add(i, x, b, base, more, first)
                    if x == 0 and more:
                        if b in POWER_AT:
                            power(i + 1, POWER_AT[b])

            link = chain(pool, zeroed)
            link(pool.memset(ones_col[:, :], 1.0))
            for x in range(2):
                link(pool.memset(q_rest[x][DH0:P, :], 0.0))
                link(pool.memset(q_max[x][DH0:P, :], 0.0))
                link(pool.memset(k_ext[x][DH0:P, :], 0.0))
            for g in range(NQB):
                power(0, g)
            if routed:
                gather(pool, mem, 0, back, gathered)
            step(0, True, first=True)
            with pool.Fori(1, PAIRS - 1) as i:
                step(i, True)
            step(PAIRS - 1, False)

        @block.vector
        def _(dve):
            def unit(kind, n, full, bank, pairs, turns):
                ps = ps_misc[bank]
                dve.wait_ge(misc_full, full)
                if kind == "proj":
                    if n == 0 and pairs is not None:
                        dve.wait_ge(v_copied, 2 * pairs)
                    dve.tensor_copy(raw[:, n, :], ps[:, 0:3 * P]).then_inc(misc_done, 1)
                elif kind == "trans":
                    cols = slice(QW * (n % NQB), QW * (n % NQB) + QW)
                    k = n // NQB
                    hi, lo = ((q_hi, q_lo), (k_hi, k_lo))[k]
                    dve.wait_ge(hi_done, (0 if pairs is None else pairs * (2 * NQB)) + n + 1)
                    dve.scalar_tensor_tensor(out=lo[:, cols], in0=ps[:, :], scalar=mem.scales[:, k:k + 1],
                                             in1=hi[:, cols], op0=ALU.mult, op1=ALU.subtract).then_inc(misc_done, 1)
                elif kind == "turn":
                    if turns is not None:
                        dve.wait_ge(row_stored, 16 * turns)
                    dve.tensor_copy(max_row[:, :], ps[:, :].bitcast(F16)[0:NT, 0:P]).then_inc(misc_done, 1)
                elif kind == "den":
                    at = TPQ * n[1]
                    dve.reciprocal(rden[:, at:at + TPQ], ps[:, 0:TPQ]).then_inc(misc_done, 1)
                elif kind == "out":
                    dve.wait_ge(misc_done, full - 1)
                    for j in range(TPQ):
                        t = TPQ * n[1] + j
                        ins = dve.scalar_tensor_tensor(out=mem.acc[:, t, :], in0=ps[:, P * j:P * j + P],
                                                       scalar=rden[:, t:t + 1], in1=mem.acc[:, t, :],
                                                       op0=ALU.mult, op1=ALU.add)
                    ins.then_inc(misc_done, 1)

            def sums(g, base):
                dve.wait_ge(sq_done, base + g + 1)
                view = sq[:, g % 2, :, :].rearrange("p t (g d) -> p (t g) d", d=DH0)
                dve.reduce_sum(ssq[:, 4 * TPQ * g:4 * TPQ * (g + 1)], view, AX_X).then_inc(ss_done, 1)
                dve.wait_ge(ss_done, base + g + 1)
                at = slice(4 * TPQ * g, 4 * TPQ * (g + 1))
                dve.tensor_scalar(ssm[:, at], ssq[:, at], 1e-24, None, ALU.max).then_inc(ssm_ready, 1)

            def chunk(c, full):
                qt, n, a, z = CHUNKS0[c]
                dve.wait_ge(mx_full, full)
                dve.reduce_max(maxima[:, qt, n:n + 1], ps_mx[c % 2][:, 0:z - a], AX_X).then_inc(mx_done, 1)

            def finish_max(x, all_done, turns):
                dve.wait_ge(mx_done, all_done)
                dve.reduce_max(max_all[:, :], maxima[:, :, :], AX_X).then_inc(max_step, 1)
                dve.wait_ge(max_step, 2 * turns + 1)
                dve.tensor_tensor(neg_max[:, :], table[x][:, 17:17 + NT], max_all[:, :], ALU.subtract).then_inc(max_step, 1)

            def normalise(pairs, g):
                dve.wait_ge(rn_ready, pairs * NQB + g + 1)
                rows = raw[:, TPQ * g:TPQ * g + TPQ, 0:2 * P].rearrange("p t (g d) -> p t g d", d=DH0)
                r = rnorm[:, 4 * TPQ * g:4 * TPQ * (g + 1)].rearrange("p (t g) -> p t g", g=4)
                dve.tensor_tensor(rows, rows, r.unsqueeze(3).to_broadcast([P, TPQ, 4, DH0]),
                                  ALU.mult).then_inc(qn_done, 1)

            def step(i, more, first=False):
                base = before_step(i, first)
                done = 0
                chunks = 0
                for x, b, _, maxes, units in steps(more, first):
                    for c in maxes:
                        chunks += 1
                        chunk(c, NC0 + i * (2 * NC0) + chunks)
                        if c == NC0 - 1:
                            finish_max(1 - x, NC0 + i * (2 * NC0) + chunks, 2 * i + 1 + x)
                    for kind, n in units:
                        unit(kind, n, base + done + 1, (MISC_FIRST + done) % 2, i + 1, 2 * i + 1 + x)
                        done += 1
                    if x == 0 and more and b - 1 in SQUARE_AT:
                        sums(SQUARE_AT[b - 1], (i + 1) * NQB)
                    if x == 0 and more and b in NORM_AT:
                        normalise(i + 1, NORM_AT[b])

            dve.memset(maxima[:, :, :], -BIG).then_inc(cleared, 1)
            dve.wait_ge(cleared, 1)
            for t in range(NT):
                unit("proj", t, t + 1, t % 2, None, None)
            for g in range(NQB):
                sums(g, 0)
            for g in range(NQB):
                normalise(0, g)
            for c in range(2 * NQB):
                unit("trans", c, NT + c + 1, (NT + c) % 2, None, None)
            dve.wait_ge(head_loaded[0], 16 * HEAD_LOADS)
            for c in range(NC0):
                chunk(c, c + 1)
            finish_max(0, NC0, 0)
            unit("turn", 0, PROJECT + 1, PROJECT % 2, None, None)
            if routed:
                combine(dve, mem, 0, back, gathered, combined)
            step(0, True, first=True)
            with dve.Fori(1, PAIRS - 1) as i:
                step(i, True)
            step(PAIRS - 1, False)
            for n, kind in enumerate(("den", "out")):
                unit(kind, (-1, NQB - 1), AFTER_LAST + n + 1, (AFTER_LAST + n) % 2, None, None)


FIRST1, LAST1, FLAT1 = 3, 17, 5000
SLOTS1 = [(qb, m) for qb in range(NQB) for m in range(TPQ * (qb + 1) // 2)]
NS1 = len(SLOTS1)
ROOM1 = [FLAT1 + QW - max(P * (2 * m - TPQ * qb), 0) for qb, m in SLOTS1]
MAX_AT1 = spread_weighed([(a, c) for a in range(2) for c in range(NC1)],
                         [64 + hi - lo for _ in range(2) for _, _, lo, hi in CHUNKS1], FIRST1, LAST1, ROOM1)
TURN_AT1 = 18
SCALE1 = float(1 / np.sqrt(np.float32(DH1)))


def units1(more):
    out = [[] for _ in range(2 * NS1 + 5)]
    for x in range(2):
        if x == 0 or more:
            out[NS1 * x + TURN_AT1].append(("turn", x, 0))
        for s, (qb, m) in enumerate(SLOTS1):
            if m == TPQ * (qb + 1) // 2 - 1:
                out[NS1 * x + s + 2].append(("den", x, qb))
                for a in range(2):
                    out[NS1 * x + s + 3 + a].append((("out", a), x, qb))
    return out


def before1(kind, x, qb, more):
    n = 0
    for units in units1(more):
        for u in units:
            n += 1
            if u == (kind, x, qb):
                return n


MISC_PER1 = 2 + 6 * NQB
HEAD_LOADS1 = 6
GROUP_LOADS = 2 * HEAD_LOADS1 + 1


def project1(nc, mem, dram, parts, values_all):
    with ExitStack() as ctx:
        def sb(name, shape, dt=F32):
            return ctx.enter_context(nc.sbuf_tensor(f"p1_{name}", shape, dt))

        def sem(name):
            return ctx.enter_context(nc.semaphore(f"p1_{name}"))

        w = sb("w", [P, 3 * P])
        bias = sb("bias", [P, 3 * P])
        rope = sb("rope", [P, 2, NT, 64])
        raw = sb("raw", [P, NT, 3 * P])
        a_cos = sb("a_cos", [P, NT, 64])
        b_sin = sb("b_sin", [P, NT, 64])
        a_sin = sb("a_sin", [P, NT, 64])
        b_cos = sb("b_cos", [P, NT, 64])
        turned = sb("turned", [P, NT, P])
        part = sb("part", [P, 2, PARTS, NT, P], BF16)
        part_t = sb("part_t", [P, 2, T], BF16)
        ps = [ctx.enter_context(nc.psum_tensor(f"p1_ps{k}", [P, QW], F32)) for k in range(2)]
        ps_t = [ctx.enter_context(nc.psum_tensor(f"p1_pt{k}", [P, 2 * QW], BF16)) for k in range(4)]

        loaded = sem("loaded")
        projected = sem("projected")
        step = sem("step")
        raw_ready = sem("raw_ready")
        v_step = sem("v_step")
        parts_ready = sem("parts_ready")
        turned_full = sem("turned_full")
        turned_read = sem("turned_read")
        stored = [sem(f"stored{k}") for k in range(2)]
        scattered = sem("scattered")
        block = ctx.enter_context(nc.Block())

        @block.sync
        def _(sp):
            sp.dma_start(w[:, :], dram["w_qkv1"]).then_inc(loaded, 16)
            sp.dma_start(bias[:, :], dram["b_qkv1"].to_broadcast([P, 3 * P])).then_inc(loaded, 16)
            sp.dma_start(rope[:, :, :, :].rearrange("p c t f -> p (c t f)"), dram["rope"]).then_inc(loaded, 16)
            for n in range(2 * PARTS):
                sp.wait_ge(turned_read, 2 * n + 2)
                sp.dma_start(parts[n // PARTS, n % PARTS, :, :], part_t[:, n % 2, :]).then_inc(stored[n % 2], 16)
            for k in range(2):
                sp.wait_ge(stored[k], 16 * PARTS)

        @block.tensor
        def _(pe):
            pe.wait_ge(loaded, 48)
            for t in range(NT):
                if t >= 2:
                    pe.wait_ge(raw_ready, t - 1)
                pe.matmul(ps[t % 2][:, 0:3 * P], mem.hT[:, P * t:P * t + P], w[:, :], start=True, stop=True)\
                  .then_inc(projected, 1)
            for n in range(2 * PARTS):
                pe.wait_ge(parts_ready, n + 1)
                for half in range(2):
                    u = 2 * n + half
                    if u >= 4:
                        pe.wait_ge(turned_read, u - 3)
                    for j in range(NT // 2):
                        mm = pe.transpose(ps_t[u % 4][:, P * j:P * j + P],
                                          part[:, n // PARTS, n % PARTS, NT // 2 * half + j, :], mem.ident_b[:, :])
                    mm.then_inc(turned_full, 1)

        @block.scalar
        def _(act):
            for n in range(2 * PARTS):
                for half in range(2):
                    u = 2 * n + half
                    act.wait_ge(turned_full, u + 1)
                    if n >= 2:
                        act.wait_ge(stored[n % 2], 16 * (n // 2))
                    act.copy(part_t[:, n % 2, 2 * QW * half:2 * QW * (half + 1)], ps_t[u % 4][:, :]).then_inc(turned_read, 1)

        @block.gpsimd
        def _(pool):
            pool.memset(values_all[:, :, :, :, :], 1.0).then_inc(v_step, 1)
            pool.wait_ge(v_step, 1)
            pool.wait_ge(raw_ready, NT)
            for a in range(2):
                v = raw[:, :, 2 * P:3 * P].rearrange("p t (g a d) -> p g t a d", a=2, d=DH1)
                pool.tensor_copy(values_all[:, :, :, a, 0:DH1], v[:, :, :, a, :]).then_inc(v_step, 1)
                pool.wait_ge(v_step, a + 2)
            scatter(pool, mem, 1, scattered)

        @block.vector
        def _(dve):
            link = chain(dve, step)
            for t in range(NT):
                dve.wait_ge(projected, t + 1)
                dve.tensor_tensor(raw[:, t, :], ps[t % 2][:, 0:3 * P], bias[:, :], ALU.add).then_inc(raw_ready, 1)
            dve.wait_ge(raw_ready, NT)
            cos, sin = rope[:, 0, :, :], rope[:, 1, :, :]
            for k in range(2):
                even, odd = raw[:, :, P * k:P * k + 64], raw[:, :, P * k + 64:P * k + P]
                link(dve.tensor_tensor(a_cos[:, :, :], even, cos, ALU.mult))
                link(dve.tensor_tensor(b_sin[:, :, :], odd, sin, ALU.mult))
                link(dve.tensor_tensor(a_sin[:, :, :], even, sin, ALU.mult))
                link(dve.tensor_tensor(b_cos[:, :, :], odd, cos, ALU.mult))
                view = turned[:, :, :].rearrange("p t (h c f) -> p t h c f", h=H1, c=2)

                def by_head(m):
                    return m[:, :, :].rearrange("p t (h f) -> p t h f", h=H1)

                link(dve.tensor_tensor(view[:, :, :, 0, :], by_head(a_cos), by_head(b_sin), ALU.subtract))
                link(dve.tensor_tensor(view[:, :, :, 1, :], by_head(a_sin), by_head(b_cos), ALU.add))
                for n in range(PARTS):
                    ins = dve.tensor_copy(part[:, k, n, :, :], turned[:, :, :])
                    ins.then_inc(parts_ready, 1)
                    dve.wait_ge(parts_ready, PARTS * k + n + 1)
                    if n < PARTS - 1:
                        link(dve.tensor_tensor(turned[:, :, :], turned[:, :, :], part[:, k, n, :, :], ALU.subtract))


def attention1(nc, mem, dram):
    with ExitStack() as outer:
        parts = nc.dram_tensor("parts1", (2, PARTS, P, T), BF16).ap()
        values_all = outer.enter_context(nc.sbuf_tensor("values_all", [P, GROUPS, NT, 2, 32], F32))
        project1(nc, mem, dram, parts, values_all)
        experts(nc, mem, 1, dram)
        attend1(nc, mem, dram, parts, values_all)


def attend1(nc, mem, dram, parts, values_all):
    with ExitStack() as ctx:
        def sb(name, shape, dt=F32):
            return ctx.enter_context(nc.sbuf_tensor(f"a1_{name}", shape, dt))

        def sem(name):
            return ctx.enter_context(nc.semaphore(f"a1_{name}"))

        qs = [[sb(f"qs{x}{a}", [P, T], BF16) for a in range(2)] for x in range(2)]
        ks = [[sb(f"ks{x}{a}", [P, T], BF16) for a in range(2)] for x in range(2)]
        values = [sb(f"values{x}", [P, NT, 2, 32]) for x in range(2)]
        w_out = [sb(f"w_out{x}", [P, D]) for x in range(2)]
        select = sb("select", [P, 2])
        prob = sb("prob", [P, 2, 2, 2, QW])
        sums = sb("sums", [P, 2, QW])
        rden = sb("rden", [P, 2 * TPQ])
        maxima = sb("maxima", [P, 2 * NT, NQB])
        max_all = sb("max_all", [P, 2 * NT])
        neg_max = sb("neg_max", [P, 2 * NT], BF16)
        max_row = sb("max_row", [2 * NT, P], BF16)
        scratch = nc.dram_tensor("max_rows1", (2, 2 * NT, P), BF16).ap()
        ps_st = [ctx.enter_context(nc.psum_tensor(f"a1_st{k}", [P, 2, QW], F32)) for k in range(2)]
        ps_ot = ctx.enter_context(nc.psum_tensor("a1_ot", [P, QW], F32))
        ps_mx = [ctx.enter_context(nc.psum_tensor(f"a1_mx{k}", [P, QW], F32)) for k in range(2)]
        ps_misc = ctx.enter_context(nc.psum_tensor("a1_misc", [P, QW], F32))

        back = sb("back", [P, CHOICES, D])
        gathered = sem("gathered")
        combined = sem("combined")
        zeroed = sem("zeroed")
        select_loaded = sem("select_loaded")
        loaded = [sem(f"loaded{x}") for x in range(2)]
        out_loaded = [sem(f"out_loaded{x}") for x in range(2)]
        st_full = sem("st_full")
        exp_done = sem("exp_done")
        pv_done = sem("pv_done")
        ot_read = sem("ot_read")
        cleared = sem("cleared")
        mx_full = sem("mx_full")
        mx_done = sem("mx_done")
        max_step = sem("max_step")
        misc_full = sem("misc_full")
        misc_done = sem("misc_done")
        row_stored = sem("row_stored")
        row_loaded = sem("row_loaded")
        block = ctx.enter_context(nc.Block())

        def slots(more):
            units = units1(more)
            for n in range(2 * NS1 + 5):
                x, s = n // NS1, n % NS1
                maxes = MAX_AT1[s] if x == 0 or (x == 1 and more) else []
                yield n, x, s, maxes, units[n]

        def upto1(x, qb):
            return NS1 * x + sum(TPQ * (q + 1) // 2 for q in range(qb + 1))

        @block.sync
        def _(sp):
            def load_group(x, g, used=None):
                for a in range(2):
                    for n in range(PARTS):
                        rows = slice(PARTS * DH1 * n, PARTS * DH1 * (n + 1))
                        sp.dma_start(qs[x][a][rows, :],
                                     parts[0].rearrange("n (g f) t -> g n f t", f=DH1)[bass.ds(2 * g + a, 1), :, :, :]
                                     .rearrange("o n f t -> (o n) f t")).then_inc(loaded[x], 16)
                        key = parts[1, n].rearrange("(g f) t -> g f t", f=DH1)[bass.ds(2 * g + a, 1), :, :]
                        sp.dma_start(ks[x][a][rows, :], key.to_broadcast([PARTS, DH1, T])).then_inc(loaded[x], 16)
                if used is not None:
                    sp.wait_ge(pv_done, used)
                sp.dma_start(values[x][:, :, :, :].rearrange("p t a f -> p (t a f)").unsqueeze(1),
                             values_all[:, bass.ds(g, 1), :, :, :].rearrange("p g t a f -> p g (t a f)")).then_inc(loaded[x], 16)

            def load_out(x, g):
                sp.dma_start(w_out[x][:, :], flat(dram["w_out1"][bass.ds(g, 1), :, :])).then_inc(out_loaded[x], 16)

            def turn_row(x, n, done):
                sp.wait_ge(misc_done, done)
                sp.dma_start(scratch[x, :, :], max_row[:, :]).then_inc(row_stored, 16)
                sp.wait_ge(row_stored, 16 * n + 16)
                for a in range(2):
                    sp.dma_start(qs[x][a][ROW_SHIFT:ROW_SHIFT + 1, :],
                                 scratch[x:x + 1, NT * a:NT * (a + 1), :].rearrange("o t p -> o (t p)")).then_inc(row_loaded, 16)

            def step(i, more):
                turn_row(1, 2 * i + 1, 1 + i * MISC_PER1 + before1("turn", 1 - 1, 0, more))
                if more:
                    sp.wait_ge(exp_done, i * (4 * NS1) + 2 * NS1)
                    load_group(0, 2 * i + 2, i * (2 * NS1) + NS1)
                    sp.wait_ge(misc_done, 1 + i * MISC_PER1 + before1(("out", 1), 0, NQB - 1, more))
                    load_out(0, 2 * i + 2)
                    turn_row(0, 2 * i + 2, 1 + i * MISC_PER1 + before1("turn", 1, 0, more))
                    sp.wait_ge(exp_done, i * (4 * NS1) + 4 * NS1)
                    load_group(1, 2 * i + 3, i * (2 * NS1) + 2 * NS1)
                    sp.wait_ge(misc_done, 1 + i * MISC_PER1 + MISC_PER1)
                    load_out(1, 2 * i + 3)

            sp.dma_start(select[:, :], dram["den_select"]).then_inc(select_loaded, 16)
            for x in range(2):
                sp.wait_ge(zeroed, 6 * x + 6)
                load_group(x, x)
                load_out(x, x)
            turn_row(0, 0, 1)
            with sp.Fori(0, GROUPS // 2 - 1) as i:
                step(i, True)
            step(GROUPS // 2 - 1, False)

        @block.gpsimd
        def _(pool):
            gather(pool, mem, 1, back, gathered)

        @block.tensor
        def _(pe):
            def chunk(x, a, c, static, free):
                qt, _, lo, hi = CHUNKS1[c]
                if free is not None:
                    pe.wait_ge(mx_done, free)
                bank = ps_mx[static % 2]
                diag = hi == P * (qt + 1)
                mm = pe.matmul(bank[:, 0:hi - lo], qs[x][a][0:STACK, P * qt:P * qt + P], ks[x][a][0:STACK, lo:hi],
                               start=True, stop=not diag)
                if diag:
                    mm = pe.matmul(bank[:, hi - lo - P:hi - lo], mem.ident_b[:, :], mem.mask_qb[:, :], start=False, stop=True)
                mm.then_inc(mx_full, 1)

            def turn(turns, free):
                pe.wait_ge(max_step, 2 * turns + 2)
                if free is not None:
                    pe.wait_ge(misc_done, free)
                pe.transpose(ps_misc[:, :].bitcast(BF16)[0:2 * NT, 0:P], neg_max[:, :], mem.ident_b[:, :]).then_inc(misc_full, 1)

            def scores(x, a, s):
                qb, m = SLOTS1[s]
                bank = ps_st[a]
                c0 = max(P * (2 * m - TPQ * qb), 0)
                diag = 2 * m >= TPQ * qb
                cols = slice(QW * qb + c0, QW * qb + QW)
                for k in range(2):
                    keys = slice(P * (2 * m + k), P * (2 * m + k) + P)
                    masked = diag or (2 * m + k >= TPQ * qb)
                    mm = pe.matmul(bank[:, k, c0:QW], ks[x][a][0:ROW_SHIFT + 1, keys], qs[x][a][0:ROW_SHIFT + 1, cols],
                                   start=True, stop=not masked)
                    if masked:
                        mm = pe.matmul(bank[:, k, c0:c0 + P * (k + 1)], mem.ident_b[:, :],
                                       mem.mask_kb[:, P * (1 - k):2 * P], start=False, stop=True)
                mm.then_inc(st_full, 1)

            def weighted(i, n, x, s):
                qb, m = SLOTS1[s]
                c0 = max(P * (2 * m - TPQ * qb), 0)
                pe.wait_ge(exp_done, i * (4 * NS1) + 2 * n + 2)
                if m == 0 and NQB * x + qb >= 1:
                    pe.wait_ge(ot_read, i * (2 * NQB) + NQB * x + qb)
                for a in range(2):
                    for k in range(2):
                        rows = slice(64 * a + 32 * k, 64 * a + 32 * k + 32)
                        mm = pe.matmul(ps_ot[rows, c0:QW], values[x][:, 2 * m + k, a, :], prob[:, n % 2, a, k, c0:QW],
                                       start=(m == 0), stop=(m == TPQ * (qb + 1) // 2 - 1))
                mm.then_inc(pv_done, 1)

            def step(i, more):
                done = 0
                chunks = 0
                for n, x, s, maxes, units in slots(more):
                    if n < 2 * NS1:
                        if s == 0:
                            pe.wait_ge(loaded[x], i * (16 * GROUP_LOADS) + 16 * GROUP_LOADS)
                            pe.wait_ge(row_loaded, i * 64 + 32 * x + 32)
                        half = len(maxes) // 2
                        for a in range(2):
                            if n >= 1:
                                pe.wait_ge(exp_done, i * (4 * NS1) + 2 * n + a - 1)
                            scores(x, a, s)
                            for head, c in (maxes[:half], maxes[half:])[a]:
                                if (head, c) == (0, 0):
                                    pe.wait_ge(loaded[1 - x], (i + x) * (16 * GROUP_LOADS) + 16 * GROUP_LOADS)
                                chunk(1 - x, head, c, chunks, 2 * NC1 + i * (4 * NC1) + chunks - 1)
                                chunks += 1
                    for kind, gx, qb in units:
                        free = 1 + i * MISC_PER1 + done
                        if kind == "turn":
                            turn(2 * i + 1 + gx, free)
                        elif kind == "den":
                            pe.wait_ge(misc_done, free)
                            pe.wait_ge(ot_read, i * (2 * NQB) + NQB * gx + qb + 1)
                            for j in range(TPQ):
                                mm = pe.matmul(ps_misc[:, 2 * j:2 * j + 2], sums[:, qb % 2, P * j:P * j + P], select[:, :],
                                               start=True, stop=True)
                            mm.then_inc(misc_full, 1)
                        else:
                            pe.wait_ge(misc_done, free)
                            pe.wait_ge(out_loaded[gx], 16 * i + 16)
                            rows = slice(64 * kind[1], 64 * kind[1] + 64)
                            for j in range(TPQ):
                                mm = pe.matmul(ps_misc[:, P * j:P * j + P], sums[rows, qb % 2, P * j:P * j + P],
                                               w_out[gx][rows, :], start=True, stop=True)
                            mm.then_inc(misc_full, 1)
                        done += 1
                    if 1 <= n <= 2 * NS1:
                        weighted(i, n - 1, (n - 1) // NS1, (n - 1) % NS1)

            pe.wait_ge(select_loaded, 16)
            pe.wait_ge(loaded[0], 16 * GROUP_LOADS)
            n = 0
            for a in range(2):
                for c in range(NC1):
                    chunk(0, a, c, n, n - 1 if n >= 2 else None)
                    n += 1
            turn(0, None)
            with pe.Fori(0, GROUPS // 2 - 1) as i:
                step(i, True)
            step(GROUPS // 2 - 1, False)

        @block.scalar
        def _(act):
            def take_out(i, n, qb, more):
                act.wait_ge(pv_done, i * (2 * NS1) + n)
                x, before = divmod(NQB * ((n - 1) // NS1) + qb - 2, NQB)
                act.wait_ge(misc_full, 1 + i * MISC_PER1 + (before1(("out", 1), x, before, more) if x >= 0 else 0))
                act.activation(sums[:, qb % 2, :], ps_ot[:, :], ACT.Copy).then_inc(ot_read, 1)

            ends = {upto1(x, qb): (x, qb) for x in range(2) for qb in range(NQB)}

            def step(i, more):
                for n in range(2 * NS1):
                    s = n % NS1
                    qb, m = SLOTS1[s]
                    c0 = max(P * (2 * m - TPQ * qb), 0)
                    for a in range(2):
                        act.wait_ge(st_full, i * (4 * NS1) + 2 * n + a + 1)
                        if n >= 2:
                            act.wait_ge(pv_done, i * (2 * NS1) + n - 1)
                        act.activation(prob[:, n % 2, a, :, c0:QW], ps_st[a][:, :, c0:QW], ACT.Exp,
                                       scale=SCALE1).then_inc(exp_done, 1)
                    if n in ends:
                        take_out(i, n, ends[n][1], more)
                take_out(i, 2 * NS1, NQB - 1, more)

            with act.Fori(0, GROUPS // 2 - 1) as i:
                step(i, True)
            step(GROUPS // 2 - 1, False)

        @block.vector
        def _(dve):
            def chunk(a, c, static, full):
                qt, n, lo, hi = CHUNKS1[c]
                dve.wait_ge(mx_full, full)
                dve.reduce_max(maxima[:, NT * a + qt, n:n + 1], ps_mx[static % 2][:, 0:hi - lo], AX_X).then_inc(mx_done, 1)

            def finish_max(all_done, turns):
                dve.wait_ge(mx_done, all_done)
                dve.reduce_max(max_all[:, :], maxima[:, :, :], AX_X).then_inc(max_step, 1)
                dve.wait_ge(max_step, 2 * turns + 1)
                dve.tensor_scalar(neg_max[:, :], max_all[:, :], -1.0, None, ALU.mult).then_inc(max_step, 1)

            def turn(turns, full):
                dve.wait_ge(misc_full, full)
                if turns is not None:
                    dve.wait_ge(row_stored, 16 * turns)
                dve.tensor_copy(max_row[:, :], ps_misc[:, :].bitcast(BF16)[0:2 * NT, 0:P]).then_inc(misc_done, 1)

            def step(i, more):
                done = 0
                chunks = 0
                for n, x, s, maxes, units in slots(more):
                    if n < 2 * NS1:
                        for head, c in maxes:
                            chunk(head, c, chunks, 2 * NC1 + i * (4 * NC1) + chunks + 1)
                            chunks += 1
                            if (head, c) == (1, NC1 - 1):
                                finish_max(2 * NC1 + i * (4 * NC1) + chunks, 2 * i + 1 + x)
                    for kind, gx, qb in units:
                        full = 1 + i * MISC_PER1 + done + 1
                        if kind == "turn":
                            turn(2 * i + 1 + gx, full)
                        elif kind == "den":
                            dve.wait_ge(misc_full, full)
                            dve.reciprocal(rden[:, :], ps_misc[:, 0:2 * TPQ]).then_inc(misc_done, 1)
                        else:
                            dve.wait_ge(misc_full, full)
                            dve.wait_ge(misc_done, full - 1)
                            for j in range(TPQ):
                                t = TPQ * qb + j
                                ins = dve.scalar_tensor_tensor(
                                    out=mem.acc[:, t, :], in0=ps_misc[:, P * j:P * j + P],
                                    scalar=rden[:, 2 * j + kind[1]:2 * j + kind[1] + 1], in1=mem.acc[:, t, :],
                                    op0=ALU.mult, op1=ALU.add)
                            ins.then_inc(misc_done, 1)
                        done += 1

            ones_twice = float(np.array([0x3F803F80], np.uint32).view(np.float32)[0])
            for x in range(2):
                for a in range(2):
                    dve.memset(qs[x][a][64:ROW_SHIFT, :], 0.0).then_inc(zeroed, 1)
                    dve.memset(ks[x][a][64:ROW_SHIFT, :], 0.0).then_inc(zeroed, 1)
                    dve.memset(ks[x][a][:, :].bitcast(F32)[ROW_SHIFT:ROW_SHIFT + 1, :], ones_twice).then_inc(zeroed, 1)
            dve.memset(maxima[:, :, :], -BIG).then_inc(cleared, 1)
            dve.wait_ge(cleared, 1)
            n = 0
            for a in range(2):
                for c in range(NC1):
                    chunk(a, c, n, n + 1)
                    n += 1
            finish_max(n, 0)
            turn(None, 1)
            combine(dve, mem, 1, back, gathered, combined)
            with dve.Fori(0, GROUPS // 2 - 1) as i:
                step(i, True)
            step(GROUPS // 2 - 1, False)




def store(nc, mem, out):
    with ExitStack() as ctx:
        stored = ctx.enter_context(nc.semaphore("stored"))
        block = ctx.enter_context(nc.Block())

        @block.sync
        def _(sp):
            sp.dma_start(out.rearrange("(t p) d -> p t d", p=P), mem.acc[:, :, :]).then_inc(stored, 16)
            sp.wait_ge(stored, 16)


def build(nc, dram, out, phases="0af1AFs"):
    mem = Memory()
    with ExitStack() as ctx:
        def sb(name, shape, dt=F32):
            return ctx.enter_context(nc.sbuf_tensor(name, shape, dt))

        mem.acc = sb("acc", [P, NT, D])
        mem.y = sb("y", [P, NT, D])
        mem.hT = sb("hT", [P, T])
        mem.yaT = sb("yaT", [P, T])
        mem.vecs = sb("vecs", [P, 3])
        mem.slot_to = [sb(f"slot_to{n}", [P, CHOICES], U32) for n in range(2)]
        mem.slot_from = [sb(f"slot_from{n}", [P, CHOICES], U32) for n in range(2)]
        mem.weights = [sb(f"weights{n}", [P, CHOICES]) for n in range(2)]
        mem.expert_in = [nc.dram_tensor(f"expert_in{n}", (SLOTS[n] + 2 * T, D), F32).ap() for n in range(2)]
        mem.expert_out = [nc.dram_tensor(f"expert_out{n}", (SLOTS[n], D), F32).ap() for n in range(2)]
        mem.ident = sb("ident_f", [P, P])
        mem.ident_b = sb("ident_b", [P, P], BF16)
        mem.ident_h = sb("ident_h", [P, P], F16)
        mem.mask_q = sb("mask_qf", [P, P])
        mem.mask_k = sb("mask_kf", [P, 2 * P])
        mem.mask_qb = sb("mask_qb", [P, P], BF16)
        mem.mask_kb = sb("mask_kb", [P, 2 * P], BF16)
        mem.lower = sb("lower_f", [P, P])
        mem.lower_b = sb("lower_b", [P, P], BF16)
        mem.ones_b = sb("ones_b", [P, P], BF16)
        mem.minus_half = sb("minus_half", [P, 4 * NT])
        mem.scales = sb("scales_s", [P, 2])
        mem.null_ops = sb("null_ops", [P, H0, 66], F16)
        if "0" in phases:
            prepare(nc, mem, 0, dram)
        if "f" in phases:
            experts(nc, mem, 0, dram)
        if "a" in phases:
            attention0(nc, mem, dram, "f" in phases)
        if "1" in phases:
            prepare(nc, mem, 1, dram)
        if "A" in phases:
            attention1(nc, mem, dram)
        store(nc, mem, out)



def slopes():
    start = 2.0 ** (-2.0 ** (-(np.log2(H0) - 3.0)))
    return np.array([start * start ** n for n in range(H0)], np.float32)


def constants():
    f = np.float32
    p = np.arange(P)
    c = {"ident": np.eye(P, dtype=f)}
    later = p[None, :] > p[:, None]
    c["mask_q"] = np.where(later, f(-BIG), f(0)).astype(f)
    c["mask_k"] = np.concatenate([np.full((P, P), -BIG, f),
                                  np.where(later.T, f(-BIG), f(0)).astype(f)], 1)
    for n in range(2):
        c[f"spare{n}"] = (SLOTS[n] + P * np.arange(CHOICES)[None, :] + p[:, None]).astype(f)
    c["lower"] = later.astype(f)
    c["expert_less"] = np.tile(np.arange(E, dtype=f) - 100, (P, NT)).astype(f)
    s = slopes()
    blocks = np.arange(-(TPQ * (NQB - 1)), TPQ)
    table = np.zeros((H0, P, len(blocks) + 1 + NT), f)
    dist = (P * blocks[None, :] + p[:, None] - ALIBI_REF).astype(f)
    s16 = s.astype(np.float16).astype(f)
    for h in range(H0):
        table[h, :, :len(blocks)] = s[h] * dist
        for q in range(NQB):
            for n in range(NULLS):
                table[h, 32 * q + n, len(blocks)] = s[h] * f(n - NULLS - QW * q - ALIBI_REF)
        table[h, :, len(blocks) + 1:] = (s16[h] * (QW * (np.arange(NT) // TPQ) + ALIBI_REF).astype(f))[None, :]
    c["head_table"] = table
    c["slope_rows"] = np.repeat(s.astype(np.float16)[:, None, None], T, 2)
    c["key_rows"] = np.stack([np.ones(KW), np.arange(KW) - NULLS]).astype(np.float16)
    ones = np.zeros((P, DH0), f)
    for q in range(NQB):
        ones[32 * q:32 * q + NULLS] = 1
    c["null_ones"] = ones
    theta = f(1) / (f(10000.0) ** (np.arange(DH1 // 2, dtype=f) / f(DH1 // 2)))
    ang = (np.arange(T, dtype=f)[:, None] * theta[None, :]).astype(f)
    cs = np.stack([np.cos(ang.astype(np.float64)), np.sin(ang.astype(np.float64))]).astype(f)
    c["rope"] = np.ascontiguousarray(np.tile(cs, (1, 1, H1)).reshape(2, NT, P, 64).transpose(2, 0, 1, 3)).reshape(P, -1)
    sel = np.zeros((P, 2), f)
    for a in range(2):
        for k in range(2):
            sel[64 * a + 32 * k + DH1, a] = 1
    c["den_select"] = sel
    return c


def laid_out(v):
    w = {"x": v["L0_attn_x"].reshape(T, D)}
    w["vecs"] = np.stack([v["L0_attn_gamma"], v["L0_ffn_ln_g"], v["L0_ffn_ln_b"]], 1)
    w["scales"] = np.stack([np.tile(v["L0_attn_q_scale"], 2), np.tile(v["L0_attn_k_scale"], 2)], 1)
    nkv = v["L0_attn_null_kv"].reshape(H0, NULLS, 2, DH0)
    w["null_k"] = nkv[:, :, 0].reshape(H0 * NULLS, DH0)
    nv = np.zeros((H0, P, DH0), np.float32)
    for q in range(NQB):
        nv[:, 32 * q:32 * q + NULLS] = nkv[:, :, 1]
    w["null_v"] = nv
    wq = v["L0_attn_w_q"].reshape(D, PAIRS, P)
    wk, wv = v["L0_attn_w_kv"].reshape(D, 2, PAIRS, P).transpose(1, 0, 2, 3)
    w["w_qkv"] = np.concatenate([wq, wk, wv], 2).transpose(1, 0, 2)
    w["w_out"] = np.tile(v["L0_attn_w_out"].reshape(H0, DH0, D), (1, 2, 1))
    w["router0"] = v["L0_ffn_Wr"]
    w["router1"] = v["L1_ffn_Wg"]
    w["w1_0"] = np.concatenate([v["L0_ffn_W1"], v["L0_ffn_W1s"][None]])
    w["w3_0"] = np.concatenate([v["L0_ffn_W3"], v["L0_ffn_W3s"][None]])
    w2 = np.concatenate([v["L0_ffn_W2"], v["L0_ffn_W2s"][None]])
    w["w2_0"] = w2.reshape(E, FC, P, D).transpose(0, 2, 1, 3).reshape(E, P, FC * D)
    w["w1_1"] = v["L1_ffn_W1"]
    w["w2_1"] = v["L1_ffn_W2"].reshape(E, FC, P, D).transpose(0, 2, 1, 3).reshape(E, P, FC * D)
    w["b1_1"] = v["L1_ffn_b1"].reshape(E, FC, P).transpose(0, 2, 1)
    b2 = np.zeros((NT, E, NT, D), np.float32)
    for t in range(NT):
        b2[t, :, t] = v["L1_ffn_b2"]
    w["b2_1"] = b2.reshape(P, NT * D)
    def turned(m):
        return m.reshape(H1, DH1 // 2, 2, -1).transpose(2, 0, 1, 3).reshape(D, -1)
    w["w_qkv1"] = np.concatenate([turned(v["L1_attn_W_q"]).T, turned(v["L1_attn_W_k"]).T, v["L1_attn_W_v"].T], 1)
    w["b_qkv1"] = np.concatenate([turned(v["L1_attn_b_q"])[:, 0], turned(v["L1_attn_b_k"])[:, 0], v["L1_attn_b_v"]])[None]
    wo = np.zeros((GROUPS, 2, 2, 32, D), np.float32)
    wo[:, :, :, 0:DH1] = v["L1_attn_W_o"].T.reshape(GROUPS, 2, 1, DH1, D)
    w["w_out1"] = wo.reshape(GROUPS, P, D)
    w["b_o"] = v["L1_attn_b_o"][None]
    return w


def kernel(**inputs):
    import concourse.bacc as bacc
    from concourse.bass_utils import run_bass_kernel_spmd

    nc = bacc.Bacc("TRN2", target_bir_lowering=False, num_devices=1)
    arrays, dram = {}, {}
    every = laid_out({k: np.asarray(a) for k, a in inputs.items()}) | constants()
    for name, a in every.items():
        a = np.ascontiguousarray(a)
        arrays[f"in_{name}"] = a
        dram[name] = nc.dram_tensor(f"in_{name}", a.shape, mybir.dt.from_np(a.dtype), kind="ExternalInput").ap()
    out = nc.dram_tensor("out_0", (T, D), F32, kind="ExternalOutput").ap()
    build(nc, dram, out)
    r = run_bass_kernel_spmd(nc, [arrays], core_ids=[0])
    return r.results[0]["out_0"].reshape(1, T, D)
```

```python
from contextlib import ExitStack

import numpy as np

import concourse.bass as bass
from concourse import mybir

ALU = mybir.AluOpType
ACT = mybir.ActivationFunctionType
F32 = mybir.dt.float32
F16 = mybir.dt.float16
BF16 = mybir.dt.bfloat16
U32 = mybir.dt.uint32
AX_X = mybir.AxisListType.X

P = 128
D = 128
T = 2048
NT = T // P
QW = 512
NQB = T // QW
TPQ = QW // P
EPS = 1e-5
BIG = 1e30
E = 8
F = 512
FC = F // P
CAP0 = 366
CAP1 = 2 * 2 * T // E
ROUTED = (E - 1, E)
BLOCK_W = (CAP0, QW)
BLOCKS_PER = (1, CAP1 // QW)
SLOTS = (ROUTED[0] * CAP0, ROUTED[1] * CAP1)
ZERO_W = 2048
CHOICES = 2 * NT

H0 = 16
DH0 = 64
PAIRS = H0 // 2
NULLS = 2
KW = NULLS + T
ROW_ONE = 64
ROW_POS = 96
ALIBI_REF = QW // 2

H1 = 16
DH1 = 8
GROUPS = H1 // 2
PARTS = 3
STACK = PARTS * PARTS * DH1
ROW_SHIFT = 96


def flat(ap):
    return ap.rearrange("o a b -> (o a) b")


def chain(eng, sem):
    count = [0]

    def link(ins):
        count[0] += 1
        ins.then_inc(sem, 1)
        eng.wait_ge(sem, count[0])
    return link



BLOCKS0 = [(-1, -1)] + [(qb, kb) for qb in range(NQB) for kb in range(TPQ * qb + TPQ)]
NB0 = len(BLOCKS0)
REAL0 = NB0 - 1


def chunks0():
    out = []
    for qt in range(NT):
        end, at, n = NULLS + P * (qt + 1), 0, 0
        while at < end:
            stop = min(end, at + (NULLS + 3 * P if at == 0 else QW))
            out.append((qt, n, at, stop))
            at, n = stop, n + 1
    return out


CHUNKS0 = chunks0()
NC0 = len(CHUNKS0)
MAXCH = max(n for _, n, _, _ in CHUNKS0) + 1
CHUNKS1 = [(qt, c, QW * c, min(QW * (c + 1), P * (qt + 1))) for qt in range(NT) for c in range(qt // TPQ + 1)]
NC1 = len(CHUNKS1)


def spread(items, first, last, slots):
    out = [[] for _ in range(slots)]
    n = last - first + 1
    for k, it in enumerate(items):
        out[first + k * n // len(items)].append(it)
    return out


def spread_weighed(items, costs, first, last, room):
    out = [[] for _ in room]
    total, have = sum(costs), sum(room[first:last + 1])
    slot, used, limit = first, 0, room[first]
    for item, cost in zip(items, costs):
        used += cost
        while slot < last and (used - cost / 2) / total > limit / have:
            slot += 1
            limit += room[slot]
        out[slot].append(item)
    return out


class Memory:
    pass


def layer_norm(link, dve, src, dst, cen, sq, col, last, var_ready, rstd_ready, turn):
    wide = [P, NT, D]
    link(dve.reduce_sum(col[:, 0, :], src, AX_X))
    link(dve.tensor_scalar(col[:, 1, :], col[:, 0, :], 1.0 / D, None, ALU.mult))
    link(dve.tensor_tensor(cen, src, col[:, 1, :].unsqueeze(2).to_broadcast(wide), ALU.subtract))
    link(dve.tensor_tensor(sq, cen, cen, ALU.mult))
    link(dve.reduce_sum(col[:, 2, :], sq, AX_X))
    dve.tensor_scalar(col[:, 3, :], col[:, 2, :], 1.0 / D, EPS, ALU.mult, ALU.add).then_inc(var_ready, 1)
    dve.wait_ge(rstd_ready, turn)
    last(dve.tensor_tensor(dst, cen, col[:, 4, :].unsqueeze(2).to_broadcast(wide), ALU.mult))


def pick_top(link, dve, logits, best, eq, cand, first, mask, expert_less):
    wide = [P, NT, E]
    link(dve.reduce_max(best, logits, AX_X))
    link(dve.tensor_tensor(eq, logits, best.unsqueeze(2).to_broadcast(wide), ALU.is_equal))
    link(dve.tensor_scalar(cand, eq, -100.0, None, ALU.mult))
    link(dve.tensor_tensor(cand, cand, expert_less, ALU.add))
    link(dve.tensor_reduce(first, cand, AX_X, ALU.min))
    link(dve.tensor_scalar(first, first, 100.0, None, ALU.add))
    link(dve.tensor_tensor(mask, expert_less, first.unsqueeze(2).to_broadcast(wide), ALU.is_equal))


def prepare(nc, mem, layer, dram):
    routed = E - 1 if layer == 0 else E
    capacity = CAP0 if layer == 0 else CAP1
    with ExitStack() as ctx:
        def sb(name, shape, dt=F32):
            return ctx.enter_context(nc.sbuf_tensor(f"{name}_{layer}", shape, dt))

        def sem(name):
            return ctx.enter_context(nc.semaphore(f"{name}_{layer}"))

        xn = sb("xn", [P, NT, D])
        cen = sb("cen", [P, NT, D])
        sq = sb("sq", [P, NT, D])
        col = sb("col", [P, 5, NT])
        w_router = sb("w_router", [P, E])
        vecs = mem.vecs
        expert_less = sb("expert_less", [P, NT, E])
        logits = sb("logits", [P, NT, E])
        logits2 = sb("logits2", [P, NT, E])
        soft = sb("soft", [P, NT, E])
        eq = sb("eq", [P, NT, E])
        cand = sb("cand", [P, NT, E])
        mask = sb("mask", [P, 2, NT, E])
        maskb = sb("maskb", [P, 2, NT, E], BF16)
        pos = sb("pos", [P, 2, NT, E])
        total = sb("total", [P, 2 * NT, E])
        before = sb("before", [P, 2 * NT, E])
        small = sb("small", [P, 14, NT])
        keep_slot = sb("keep_slot", [P, 2, CHOICES])
        spare = sb("spare", [P, CHOICES])
        pair = sb("pair", [P, 2, NT])
        ones_row = sb("ones_row", [P, 2 * NT])
        turned = [ctx.enter_context(nc.psum_tensor(f"turned{n}_{layer}", [P, QW], F32)) for n in range(NQB)]
        ps_log = ctx.enter_context(nc.psum_tensor(f"ps_log_{layer}", [P, NT, 32], F32))
        ps_cnt = ctx.enter_context(nc.psum_tensor(f"ps_cnt_{layer}", [P, 2 * NT * E], F32))
        ps_tot = ctx.enter_context(nc.psum_tensor(f"ps_tot_{layer}", [P, 2 * NT * E], F32))

        x_loaded = sem("x_loaded")
        consts_loaded = sem("consts_loaded")
        step = sem("step")
        var_ready = sem("var_ready")
        rstd_ready = sem("rstd_ready")
        normed = sem("normed")
        tiles_turned = sem("tiles_turned")
        act_read = sem("act_read")
        hT_ready = sem("hT_ready")
        logits_ready = sem("logits_ready")
        masks_ready = sem("masks_ready")
        counted = sem("counted")
        diff_ready = sem("diff_ready")
        exp_ready = sem("exp_ready")
        if layer == 0:
            nk = sb("nk", [2 * H0, DH0])
            nk2 = sb("nk2", [2 * H0, DH0])
            nkcol = sb("nkcol", [2 * H0, 2])
            nk_hi = sb("nk_hi", [DH0, 2 * H0], F16)
            nk_lo = sb("nk_lo", [DH0, 2 * H0], F16)
            ps_null = ctx.enter_context(nc.psum_tensor("ps_null", [DH0, 2 * H0], F32))
            nk_ready = sem("nk_ready")
            nk_turned = sem("nk_turned")
            zeros = sb("zeros", [P, ZERO_W])
            zeros_ready = sem("zeros_ready")
            zeros_stored = sem("zeros_stored")
        else:
            gates = sb("gates", [P, NT, E])
            gates_flat = sb("gates_flat", [P, NT * E])
            gates_T = sb("gates_T", [P, P])
            b2 = sb("b2", [P, NT * D])
            b_o = sb("b_o", [P, D])
            ahead_loaded = sem("ahead_loaded")
            gates_ready = sem("gates_ready")
            gates_turned = sem("gates_turned")
            bias_ready = sem("bias_ready")
        block = ctx.enter_context(nc.Block())

        @block.sync
        def _(sp):
            if layer == 0:
                sp.dma_start(mem.acc[:, :, :], dram["x"].rearrange("(t p) d -> p t d", p=P)).then_inc(x_loaded, 16)
                sp.dma_start(mem.ident[:, :], dram["ident"]).then_inc(consts_loaded, 16)
                sp.dma_start(mem.mask_q[:, :], dram["mask_q"]).then_inc(consts_loaded, 16)
                sp.dma_start(mem.mask_k[:, :], dram["mask_k"]).then_inc(consts_loaded, 16)
                sp.dma_start(mem.lower[:, :], dram["lower"]).then_inc(consts_loaded, 16)
                sp.dma_start(vecs[:, :], dram["vecs"]).then_inc(consts_loaded, 16)
                sp.dma_start(nk[:, :], dram["null_k"]).then_inc(consts_loaded, 16)
                sp.dma_start(mem.scales[:, :], dram["scales"]).then_inc(consts_loaded, 16)
            else:
                sp.dma_start(b2[:, :], dram["b2_1"]).then_inc(consts_loaded, 16)
                sp.dma_start(b_o[:, :], dram["b_o"].to_broadcast([P, D])).then_inc(consts_loaded, 16)
            sp.dma_start(w_router[:, 0:routed], dram["router0" if layer == 0 else "router1"]).then_inc(consts_loaded, 16)
            sp.dma_start(spare[:, :], dram[f"spare{layer}"]).then_inc(consts_loaded, 16)
            sp.dma_start(expert_less[:, :, :], dram["expert_less"].rearrange("p (t e) -> p t e", e=E)).then_inc(consts_loaded, 16)

            if layer == 0:
                sp.dma_start(mem.shared["w1"][:, :], dram["w1_0"][E - 1]).then_inc(mem.shared_loaded, 16)
                sp.dma_start(mem.shared["w3"][:, :], dram["w3_0"][E - 1]).then_inc(mem.shared_loaded, 16)
                sp.dma_start(mem.shared["w2"][:, :, :].rearrange("p c d -> p (c d)"), dram["w2_0"][E - 1]).then_inc(mem.shared_loaded, 16)
                sp.dma_start(mem.w_qkv[:, :], dram["w_qkv"][0]).then_inc(mem.w_loaded, 16)
                sp.wait_ge(zeros_ready, 1)
                fills = 0
                for n in range(2):
                    rows = mem.expert_in[n][0:SLOTS[n], :].rearrange("r d -> (r d)").rearrange("(p a) -> p a", p=P)
                    for at in range(0, SLOTS[n], ZERO_W):
                        end = min(at + ZERO_W, SLOTS[n])
                        sp.dma_start(rows[:, at:end], zeros[:, 0:end - at]).then_inc(zeros_stored, 16)
                        fills += 1
                sp.wait_ge(zeros_stored, 16 * fills)

            else:
                sp.dma_start(mem.w_qkv1[:, :], dram["w_qkv1"]).then_inc(ahead_loaded, 16)
                sp.dma_start(mem.b_qkv1[:, :], dram["b_qkv1"].to_broadcast([P, 3 * P])).then_inc(ahead_loaded, 16)
                sp.dma_start(mem.rope[:, :, :, :].rearrange("p c t f -> p (c t f)"), dram["rope"]).then_inc(ahead_loaded, 16)
                sp.wait_ge(ahead_loaded, 48)

        loads = 16 * (10 if layer == 0 else 5)

        @block.vector
        def _(dve):
            link = chain(dve, step)
            link(dve.memset(ones_row[:, :], 1.0))
            if layer == 0:
                link(dve.memset(mem.minus_half[:, :], -0.5))
            if layer == 0:
                dve.wait_ge(x_loaded, 16)
                layer_norm(link, dve, mem.acc[:, :, :], xn[:, :, :], cen[:, :, :], sq[:, :, :], col, link,
                           var_ready, rstd_ready, 1)
                layer_norm(link, dve, xn[:, :, :], mem.y[:, :, :], cen[:, :, :], sq[:, :, :], col,
                           lambda ins: ins.then_inc(normed, 1), var_ready, rstd_ready, 2)
            else:
                layer_norm(link, dve, mem.acc[:, :, :], mem.y[:, :, :], cen[:, :, :], sq[:, :, :], col,
                           lambda ins: ins.then_inc(normed, 1), var_ready, rstd_ready, 1)
            dve.wait_ge(consts_loaded, loads)
            if layer == 0:
                link(dve.tensor_copy(mem.ident_b[:, :], mem.ident[:, :]))
                link(dve.tensor_copy(mem.ident_h[:, :], mem.ident[:, :]))
                link(dve.tensor_copy(mem.mask_qb[:, :], mem.mask_q[:, :]))
                link(dve.tensor_copy(mem.mask_kb[:, :], mem.mask_k[:, :]))
                link(dve.tensor_copy(mem.lower_b[:, :], mem.lower[:, :]))
                link(dve.memset(mem.ones_b[:, :], 1.0))
                link(dve.tensor_scalar(mem.scales[:, 0:1], mem.scales[:, 0:1], 8.0, None, ALU.mult))
            if layer == 0:
                link(dve.tensor_tensor(nk2[:, :], nk[:, :], nk[:, :], ALU.mult))
                link(dve.reduce_sum(nkcol[:, 0:1], nk2[:, :], AX_X))
                dve.tensor_scalar(nkcol[:, 0:1], nkcol[:, 0:1], 1e-24, None, ALU.max).then_inc(var_ready, 1)
                dve.wait_ge(rstd_ready, 3)
                dve.tensor_scalar(nk[:, :], nk[:, :], nkcol[:, 1:2], None, ALU.mult).then_inc(nk_ready, 1)
                link(dve.memset(mem.null_ops[:, :, :], 0.0))
                dve.wait_ge(nk_turned, 1)
                ks = mem.scales[0:DH0, 1:2]
                link(dve.tensor_scalar(nk_hi[:, :], ps_null[:, :], ks, None, ALU.mult))
                link(dve.scalar_tensor_tensor(out=nk_lo[:, :], in0=ps_null[:, :], scalar=ks, in1=nk_hi[:, :],
                                              op0=ALU.mult, op1=ALU.subtract))
                hi = nk_hi[:, :].rearrange("p (h n) -> p h n", n=NULLS)
                lo = nk_lo[:, :].rearrange("p (h n) -> p h n", n=NULLS)
                link(dve.tensor_copy(mem.null_ops[0:DH0, :, 0:2], hi))
                link(dve.tensor_copy(mem.null_ops[DH0:P, :, 0:2], lo))
                link(dve.tensor_copy(mem.null_ops[0:DH0, :, 32:34], hi))
                link(dve.tensor_copy(mem.null_ops[0:DH0, :, 64:66], hi))
                one = slice(ROW_ONE, ROW_ONE + 1)
                link(dve.memset(mem.null_ops[one, :, 32:34], 1.0))
                link(dve.memset(mem.null_ops[one, :, 64:66], 1.0))
                for n in range(NULLS):
                    link(dve.memset(mem.null_ops[ROW_POS:ROW_POS + 1, :, 64 + n:65 + n], float(n - NULLS)))
            for n in range(NQB):
                cols = slice(QW * n, QW * n + QW)
                dve.wait_ge(tiles_turned, TPQ * n + TPQ)
                if layer == 0:
                    dve.wait_ge(act_read, n + 1)
                    dve.tensor_scalar(mem.hT[:, cols], turned[n][:, :], vecs[:, 1:2], vecs[:, 2:3],
                                      ALU.mult, ALU.add).then_inc(hT_ready, 1)
                else:
                    dve.tensor_copy(mem.hT[:, cols], turned[n][:, :]).then_inc(hT_ready, 1)
            if routed < E:
                link(dve.memset(logits[:, :, routed:E], -3e38))
            dve.wait_ge(logits_ready, 1)
            link(dve.tensor_copy(logits[:, :, 0:routed], ps_log[:, :, 0:routed]))
            best1, first1, best2, first2, diff = (small[:, n, :] for n in range(1, 6))
            less = expert_less[:, :, :]
            pick_top(link, dve, logits[:, :, :], best1, eq[:, :, :], cand[:, :, :], first1, mask[:, 0, :, :], less)
            link(dve.tensor_scalar(logits2[:, :, :], mask[:, 0, :, :], -3e38, None, ALU.mult))
            link(dve.tensor_tensor(logits2[:, :, :], logits2[:, :, :], logits[:, :, :], ALU.add))
            pick_top(link, dve, logits2[:, :, :], best2, eq[:, :, :], cand[:, :, :], first2, mask[:, 1, :, :], less)
            dve.tensor_copy(maskb[:, :, :, :], mask[:, :, :, :]).then_inc(masks_ready, 1)
            link(dve.tensor_tensor(diff, best2, best1, ALU.subtract))
            if layer == 1:
                link(dve.tensor_tensor(soft[:, :, :], logits[:, :, :], best1.unsqueeze(2).to_broadcast([P, NT, E]),
                                       ALU.subtract))
            dve.tensor_copy(small[:, 6, :], diff).then_inc(diff_ready, 1)
            dve.wait_ge(exp_ready, 2)
            ediff, den, inv = small[:, 7, :], small[:, 8, :], small[:, 9, :]
            if layer == 0:
                link(dve.tensor_scalar(den, ediff, 1.0, None, ALU.add))
                link(dve.reciprocal(pair[:, 0, :], den))
                link(dve.tensor_tensor(pair[:, 1, :], ediff, pair[:, 0, :], ALU.mult))
            else:
                link(dve.reduce_sum(den, soft[:, :, :], AX_X))
                link(dve.reciprocal(pair[:, 0, :], den))
                link(dve.tensor_tensor(pair[:, 1, :], ediff, pair[:, 0, :], ALU.mult))
                link(dve.tensor_tensor(inv, pair[:, 0, :], pair[:, 1, :], ALU.add))
                link(dve.tensor_scalar(inv, inv, 1e-9, None, ALU.add))
                link(dve.reciprocal(inv, inv))
                link(dve.tensor_tensor(pair[:, :, :], pair[:, :, :], inv.unsqueeze(1).to_broadcast([P, 2, NT]), ALU.mult))
            dve.wait_ge(counted, 2)
            link(dve.tensor_copy(total[:, :, :], ps_tot[:, :].rearrange("p (t e) -> p t e", e=E)))
            for e in range(E):
                link(dve.tensor_tensor_scan(before[:, :, e], ones_row[:, :], total[:, :, e], 0.0, ALU.mult, ALU.add))
            link(dve.tensor_tensor(before[:, :, :], before[:, :, :], total[:, :, :], ALU.subtract))
            pos_t = pos[:, :, :, :].rearrange("p k t e -> p (k t) e")
            mask_t = mask[:, :, :, :].rearrange("p k t e -> p (k t) e")
            link(dve.tensor_tensor(pos_t, before[:, :, :], ps_cnt[:, :].rearrange("p (t e) -> p t e", e=E), ALU.add))
            link(dve.tensor_tensor(pos_t, pos_t, mask_t, ALU.mult))
            place = small[:, 10:12, :].rearrange("p k t -> p (k t)")
            link(dve.reduce_sum(place, pos_t, AX_X))
            keep, slot = keep_slot[:, 0, :], keep_slot[:, 1, :]
            link(dve.tensor_scalar(keep, place, float(capacity), None, ALU.is_lt))
            chosen = small[:, 12:14, :].rearrange("p k t -> p (k t)")
            for k, first in enumerate((first1, first2)):
                link(dve.tensor_scalar(small[:, 12 + k, :], first, 100.0, float(capacity), ALU.add, ALU.mult))
            link(dve.tensor_tensor(slot, chosen, place, ALU.add))
            link(dve.tensor_tensor(slot, slot, keep, ALU.mult))
            link(dve.tensor_copy(mem.slot_from[layer][:, :], slot))
            link(dve.tensor_scalar(place, keep, -1.0, 1.0, ALU.mult, ALU.add))
            link(dve.tensor_tensor(place, place, spare[:, :], ALU.mult))
            link(dve.tensor_tensor(slot, slot, place, ALU.add))
            link(dve.tensor_copy(mem.slot_to[layer][:, :], slot))
            pair_t = pair[:, :, :].rearrange("p k t -> p (k t)")
            link(dve.tensor_tensor(mem.weights[layer][:, :], pair_t, keep, ALU.mult))
            if layer == 1:
                link(dve.tensor_tensor(pos_t, mask_t, mem.weights[layer][:, :].unsqueeze(2).to_broadcast([P, 2 * NT, E]), ALU.mult))
                link(dve.tensor_tensor(gates[:, :, :], pos[:, 0, :, :], pos[:, 1, :, :], ALU.add))
                dve.tensor_copy(gates_flat[:, :], gates[:, :, :].rearrange("p t e -> p (t e)")).then_inc(gates_ready, 1)
                dve.wait_ge(gates_turned, 1)
                dve.tensor_copy(gates_T[:, :], ps_cnt[:, 0:P]).then_inc(gates_ready, 1)
                link(dve.tensor_tensor(mem.acc[:, :, :], mem.acc[:, :, :],
                                       b_o[:, :].unsqueeze(1).to_broadcast([P, NT, D]), ALU.add))
                for n in range(NQB):
                    dve.wait_ge(bias_ready, n + 1)
                    acc = mem.acc[:, TPQ * n:TPQ * n + TPQ, :].rearrange("p t d -> p (t d)")
                    link(dve.tensor_tensor(acc, acc, turned[n][:, :], ALU.add))

        @block.gpsimd
        def _(pool):
            if layer == 0:
                pool.memset(zeros[:, :], 0.0).then_inc(zeros_ready, 1)
            for turn in range(2 if layer == 0 else 1):
                pool.wait_ge(var_ready, turn + 1)
                pool.tensor_tensor(col[:, 4, :], col[:, 3, :], mem.minus_half[:, 0:NT], ALU.pow).then_inc(rstd_ready, 1)
            if layer == 1:
                pool.memset(mem.values_all[:, :, :, :, :], 1.0)
            if layer == 0:
                pool.wait_ge(var_ready, 3)
                pool.tensor_tensor(nkcol[:, 1:2], nkcol[:, 0:1], mem.minus_half[0:2 * H0, 0:1], ALU.pow).then_inc(rstd_ready, 1)

        @block.scalar
        def _(act):
            if layer == 0:
                act.wait_ge(consts_loaded, loads)
            for n in range(NQB):
                cols = slice(QW * n, QW * n + QW)
                act.wait_ge(tiles_turned, TPQ * n + TPQ)
                if layer == 0:
                    act.activation(mem.yaT[:, cols], turned[n][:, :], ACT.Copy, scale=vecs[:, 0:1]).then_inc(act_read, 1)
            act.wait_ge(diff_ready, 1)
            act.activation(small[:, 7, :], small[:, 6, :], ACT.Exp).then_inc(exp_ready, 1)
            if layer == 1:
                act.activation(soft[:, :, :], soft[:, :, :], ACT.Exp).then_inc(exp_ready, 1)
            else:
                act.activation(soft[:, 0, :], small[:, 6, 0:E], ACT.Copy).then_inc(exp_ready, 1)

        @block.tensor
        def _(pe):
            pe.wait_ge(normed, 1)
            if layer == 0:
                pe.wait_ge(consts_loaded, loads)
            for t in range(NT):
                at = P * (t % TPQ)
                pe.transpose(turned[t // TPQ][:, at:at + P], mem.y[:, t, :], mem.ident[:, :]).then_inc(tiles_turned, 1)
            if layer == 0:
                pe.wait_ge(nk_ready, 1)
                pe.transpose(ps_null[:, :], nk[:, :], mem.ident[0:2 * H0, 0:2 * H0]).then_inc(nk_turned, 1)
            for t in range(NT):
                pe.wait_ge(hT_ready, t // TPQ + 1)
                last = pe.matmul(ps_log[:, t, 0:routed], mem.hT[:, P * t:P * t + P], w_router[:, 0:routed],
                                 start=True, stop=True)
            last.then_inc(logits_ready, 1)
            pe.wait_ge(masks_ready, 1)
            chosen = maskb[:, :, :, :].rearrange("p k t e -> p (k t e)")
            pe.matmul(ps_cnt[:, :], mem.lower_b[:, :], chosen, start=True, stop=True).then_inc(counted, 1)
            pe.matmul(ps_tot[:, :], mem.ones_b[:, :], chosen, start=True, stop=True).then_inc(counted, 1)
            if layer == 1:
                pe.wait_ge(gates_ready, 1)
                pe.transpose(ps_cnt[:, 0:P], gates_flat[:, :], mem.ident[:, :]).then_inc(gates_turned, 1)
                pe.wait_ge(gates_ready, 2)
                for n in range(NQB):
                    pe.matmul(turned[n][:, :], gates_T[:, :], b2[:, QW * n:QW * n + QW],
                              start=True, stop=True).then_inc(bias_ready, 1)


def scatter(pool, mem, layer, scattered):
    for c in range(CHOICES):
        pool.indirect_dma_start(mem.expert_in[layer][:, :], bass.IndirectOffsetOnAxis(ap=mem.slot_to[layer][:, c:c + 1], axis=0),
                                mem.y[:, c % NT, :], None).then_inc(scattered, 16)
    pool.wait_ge(scattered, 16 * CHOICES)


def gather(pool, mem, layer, back, gathered):
    for c in range(CHOICES):
        pool.indirect_dma_start(back[:, c, :], None, mem.expert_out[layer][:, :],
                                bass.IndirectOffsetOnAxis(ap=mem.slot_from[layer][:, c:c + 1], axis=0)).then_inc(gathered, 16)
    pool.wait_ge(gathered, 16 * CHOICES)


def combine(dve, mem, layer, back, gathered, combined, part=0, parts=1):
    dve.wait_ge(gathered, 16 * CHOICES)
    for c in range(CHOICES * part // parts, CHOICES * (part + 1) // parts):
        t = c % NT
        if c == NT:
            dve.wait_ge(combined, NT)
        dve.scalar_tensor_tensor(out=mem.acc[:, t, :], in0=back[:, c, :], scalar=mem.weights[layer][:, c:c + 1],
                                 in1=mem.acc[:, t, :], op0=ALU.mult, op1=ALU.add).then_inc(combined, 1)
    dve.wait_ge(combined, CHOICES * (part + 1) // parts)


def experts(nc, mem, layer, dram, beside=None):
    with ExitStack() as ctx:
        def sb(name, shape, dt=F32):
            return ctx.enter_context(nc.sbuf_tensor(f"f_{name}_{layer}", shape, dt))

        def sem(name):
            return ctx.enter_context(nc.semaphore(f"f_{name}_{layer}"))

        def banks(name, n):
            return [ctx.enter_context(nc.psum_tensor(f"f_{name}{k}_{layer}", [P, QW], F32)) for k in range(n)]

        gated = layer == 0
        routed, width, per = ROUTED[layer], BLOCK_W[layer], BLOCKS_PER[layer]
        tiles = [(at, min(P, width - at)) for at in range(0, width, P)]
        shared = NQB if gated else 0
        step_blocks = 2 * per
        w1 = [sb("w10", [P, F]), mem.shared["w1"] if gated else sb("w11", [P, F])]
        w2 = [sb("w20", [P, FC, D]), mem.shared["w2"] if gated else sb("w21", [P, FC, D])]
        if gated:
            w3 = [sb("w30", [P, F]), mem.shared["w3"]]
            act_out = sb("act_out", [P, 2, QW])
            ps_b = banks("ps_b", 2)
        else:
            b1 = [sb(f"b1{k}", [P, FC]) for k in range(2)]
        rows = [sb(f"rows{k}", [P, TPQ, D]) for k in range(2)]
        x_t = [sb(f"x_t{k}", [P, QW]) for k in range(2)]
        hidden = sb("hidden", [P, 2, FC, QW])
        result = [sb(f"result{k}", [P, TPQ, D]) for k in range(2)]
        ps_x = banks("ps_x", 2)
        ps_a = banks("ps_a", 2)
        ps_y = banks("ps_y", 2)

        moved = sem("moved")
        loaded = [sem("loaded0"), mem.shared_loaded if gated else sem("loaded1")]
        rows_loaded = [sem(f"rows_loaded{k}") for k in range(2)]
        turned = sem("turned")
        x_ready = sem("x_ready")
        up_done = sem("up_done")
        act_done = sem("act_done")
        hidden_ready = sem("hidden_ready")
        down_done = sem("down_done")
        y_read = sem("y_read")
        stored = [sem(f"stored{k}") for k in range(2)]
        block = ctx.enter_context(nc.Block())
        per_load = 16 * 3
        whole, odd = divmod(width, P)
        row_dmas = 16 * (2 if odd else 1)
        d_w1 = dram["w1_0" if gated else "w1_1"]
        d_w2 = dram["w2_0" if gated else "w2_1"]
        in_rows = mem.expert_in[layer][0:SLOTS[layer], :].rearrange("(g r) d -> g r d", r=width)
        out_rows = mem.expert_out[layer].rearrange("(g r) d -> g r d", r=width)

        all_blocks = routed * per
        final = (routed + 1) // 2 - 1

        def run(eng, step):
            loops = (routed - 2) // 2
            with eng.Fori(0, loops) as i:
                step(i, step_blocks)
            for i in range(loops, (routed + 1) // 2):
                step(i, min(step_blocks, all_blocks - i * step_blocks))

        def is_final(i):
            return isinstance(i, int) and i == final

        def is_block(g):
            return not isinstance(g, int) or g < all_blocks

        def pieces(sb_rows, dram_block):
            flat_block = dram_block.rearrange("o r d -> (o r) d")
            yield sb_rows[:, 0:whole, :], flat_block[0:P * whole, :].rearrange("(c p) d -> p c d", p=P)
            if odd:
                yield sb_rows[0:odd, whole, :], flat_block[P * whole:width, :]

        @block.sync
        def _(sp):
            def load(k, e):
                sp.dma_start(w1[k][:, :], flat(d_w1[bass.ds(e, 1), :, :])).then_inc(loaded[k], 16)
                sp.dma_start(w2[k][:, :, :].rearrange("p c d -> p (c d)"), flat(d_w2[bass.ds(e, 1), :, :])).then_inc(loaded[k], 16)
                if gated:
                    sp.dma_start(w3[k][:, :], flat(dram["w3_0"][bass.ds(e, 1), :, :])).then_inc(loaded[k], 16)
                else:
                    sp.dma_start(b1[k][:, :], flat(dram["b1_1"][bass.ds(e, 1), :, :])).then_inc(loaded[k], 16)

            def load_rows(k, g):
                for here, there in pieces(rows[k], in_rows[bass.ds(g, 1), :, :]):
                    sp.dma_start(here, there).then_inc(rows_loaded[k], 16)

            def store_rows(n, g):
                sp.wait_ge(y_read, g + (shared + 1 + 2))
                for here, there in pieces(result[n % 2], out_rows[bass.ds(g, 1), :, :]):
                    sp.dma_start(there, here).then_inc(stored[n % 2], 16)

            def step(i, blocks):
                for n in range(blocks):
                    g = i * step_blocks + n
                    if is_block(g + 2):
                        sp.wait_ge(turned, g + 1)
                        load_rows(n % 2, g + 2)
                    if n == per and is_block(g + per):
                        sp.wait_ge(down_done, g + shared)
                        load(0, i * 2 + 2)
                    if beside and is_final(i) and n == 1:
                        beside.sync(sp, 1)
                    if n > 0:
                        store_rows(n - 1, g - 1)
                store_rows(blocks - 1, g)
                if blocks == step_blocks and is_block(g + per + 1):
                    sp.wait_ge(down_done, g + (shared + 1))
                    load(1, i * 2 + 3)

            if not gated:
                load_rows(0, 0)
            load(0, 0)
            if gated:
                sp.wait_ge(down_done, shared)
            if gated:
                load(1, 1)
                sp.wait_ge(moved, 16 * CHOICES)
                load_rows(0, 0)
            load_rows(1, 1)
            if not gated:
                load(1, 1)
            if beside:
                beside.sync(sp, 0)
            run(sp, step)
            for n in range(2):
                sp.wait_ge(stored[n], row_dmas * ((all_blocks + 1 - n) // 2 + 1))

        @block.gpsimd
        def _(pool):
            if gated:
                scatter(pool, mem, layer, moved)
            if beside:
                beside.gpsimd(pool)

        @block.tensor
        def _(pe):
            def turn_rows(i, n):
                k = n % 2
                pe.wait_ge(rows_loaded[k], i * (per * row_dmas) + (n // 2 + 1) * row_dmas)
                for c, (at, count) in enumerate(tiles):
                    mm = pe.transpose(ps_x[k][:, at:at + count], rows[k][0:count, c, :], mem.ident[0:count, 0:count])
                mm.then_inc(turned, 1)

            def up(k, src, w, f, free):
                if free is not None:
                    pe.wait_ge(hidden_ready, free)
                at = slice(P * f, P * f + P)
                mm = pe.matmul(ps_a[f % 2][:, 0:w], w1[k][:, at], src, start=True, stop=True)
                if gated:
                    mm = pe.matmul(ps_b[f % 2][:, 0:w], w3[k][:, at], src, start=True, stop=True)
                mm.then_inc(up_done, 1)

            def down(k, b, where, ready, free, after_tile=None):
                pe.wait_ge(hidden_ready, ready)
                pe.wait_ge(y_read, free)
                for at, count in where:
                    for f in range(FC):
                        mm = pe.matmul(ps_y[b][0:count, at:at + D], hidden[:, b, f, at:at + count],
                                       w2[k][:, f, :], start=(f == 0), stop=(f == FC - 1))
                    if after_tile:
                        after_tile()
                mm.then_inc(down_done, 1)

            def step(i, blocks):
                after = None
                if beside and is_final(i):
                    places = iter(range(2 * FC * blocks))

                    def after():
                        beside.tensor(pe, mem, next(places), 2 * FC * blocks)
                for n in range(blocks):
                    g = i * step_blocks + n
                    k = n // per
                    src = x_t[n % 2][:, 0:width]
                    if n % per == 0:
                        pe.wait_ge(loaded[k], (i + (k if gated else 0)) * per_load + per_load)
                    pe.wait_ge(x_ready, g + 1)
                    for f in range(FC):
                        up(k, src, width, f, g * FC + (shared * FC + f - 1) if n > 0 or f >= 2 else None)
                        if f == 0 and is_block(g + 1):
                            turn_rows(*((i, n + 1) if n + 1 < step_blocks else (i + 1, 0)))
                        if after:
                            after()
                        if f == 1 and n > 0:
                            down((n - 1) // per, (n - 1) % 2, tiles, (g + shared) * FC, g + shared, after)
                down((blocks - 1) // per, (blocks - 1) % 2, tiles, g * FC + (shared + 1) * FC, g + (shared + 1), after)

            if gated:
                pe.wait_ge(loaded[1], per_load)
                full_tiles = [(P * j, P) for j in range(TPQ)]
                for q in range(NQB):
                    for f in range(FC):
                        unit = FC * q + f
                        up(1, mem.hT[:, QW * q:QW * q + QW], QW, f, unit - 1 if unit >= 2 else None)
                        if f == 1 and q > 0:
                            down(1, (q - 1) % 2, full_tiles, FC * q, q)
                down(1, (NQB - 1) % 2, full_tiles, FC * NQB, NQB)
            turn_rows(0, 0)
            run(pe, step)

        @block.scalar
        def _(act):
            def unit(k, b, w, f, done, n):
                act.wait_ge(up_done, done)
                if gated:
                    if n is not None:
                        act.wait_ge(hidden_ready, n)
                    act.activation(act_out[:, f % 2, 0:w], ps_a[f % 2][:, 0:w], ACT.Silu).then_inc(act_done, 1)
                else:
                    act.activation(hidden[:, b, f, 0:w], ps_a[f % 2][:, 0:w], ACT.Gelu,
                                   bias=b1[k][:, f:f + 1]).then_inc(hidden_ready, 1)

            def step(i, blocks):
                for n in range(blocks):
                    g = i * step_blocks + n
                    k = n // per
                    if not gated and n % per == 0:
                        act.wait_ge(loaded[k], i * per_load + per_load)
                    for f in range(FC):
                        unit(k, n % 2, width, f, g * FC + (shared * FC + f + 1), g * FC + (shared * FC + f - 1))

            for q in range(shared):
                for f in range(FC):
                    u = FC * q + f
                    unit(1, q % 2, QW, f, u + 1, u - 1 if u >= 2 else None)
            run(act, step)

        @block.vector
        def _(dve):
            def gate_unit(b, w, f, done):
                dve.wait_ge(act_done, done)
                dve.tensor_tensor(hidden[:, b, f, 0:w], act_out[:, f % 2, 0:w], ps_b[f % 2][:, 0:w],
                                  ALU.mult).then_inc(hidden_ready, 1)

            def turn_x(g, b):
                dve.wait_ge(turned, g + 1)
                if gated:
                    dve.tensor_scalar(x_t[b][:, 0:width], ps_x[b][:, 0:width], mem.vecs[:, 1:2], mem.vecs[:, 2:3],
                                      ALU.mult, ALU.add).then_inc(x_ready, 1)
                else:
                    dve.tensor_copy(x_t[b][:, 0:width], ps_x[b][:, 0:width]).then_inc(x_ready, 1)

            def take(b, done, before):
                dve.wait_ge(down_done, done)
                dve.wait_ge(stored[b], before)
                for here, there in ([(result[b][:, 0:whole, :], ps_y[b][:, 0:P * whole])] +
                                    ([(result[b][0:odd, whole:whole + 1, :], ps_y[b][0:odd, P * whole:P * whole + D])] if odd else [])):
                    ins = dve.tensor_copy(here.rearrange("p c d -> p (c d)"), there)
                ins.then_inc(y_read, 1)

            def add_shared(q):
                dve.wait_ge(down_done, q + 1)
                acc = mem.acc[:, TPQ * q:TPQ * q + TPQ, :].rearrange("p t d -> p (t d)")
                dve.tensor_tensor(acc, ps_y[q % 2][:, :], acc, ALU.add).then_inc(y_read, 1)

            def step(i, blocks):
                places = iter(range(2 * FC * blocks))

                def along(count):
                    for _ in range(count if beside and is_final(i) else 0):
                        beside.vector(dve, next(places), 2 * FC * blocks)
                for n in range(blocks):
                    g = i * step_blocks + n
                    for f in range(FC):
                        if f == 1 and is_block(g + 1):
                            turn_x(g + 1, (n + 1) % 2)
                        if gated:
                            gate_unit(n % 2, width, f, g * FC + (shared * FC + f + 1))
                        along(1 if f != 1 or n == 0 else 1 + TPQ)
                        if f == FC - 1 and n > 0:
                            take((n - 1) % 2, g + shared, i * (per * row_dmas) + ((n - 1) // 2 + 1) * row_dmas)
                along(TPQ)
                take((blocks - 1) % 2, g + (shared + 1), i * (per * row_dmas) + ((blocks - 1) // 2 + 1) * row_dmas)

            if beside:
                beside.clear(dve)
            dve.memset(result[0][:, 0, 0:1], 0.0).then_inc(y_read, 2)
            dve.memset(result[0][:, 0, 1:2], 0.0).then_inc(stored[0], row_dmas)
            dve.memset(result[1][:, 0, 0:1], 0.0).then_inc(stored[1], row_dmas)
            for q in range(shared):
                for f in range(FC):
                    gate_unit(q % 2, QW, f, FC * q + f + 1)
                    if f == FC - 1 and q > 0:
                        add_shared(q - 1)
            if gated:
                add_shared(NQB - 1)
            turn_x(0, 0)
            run(dve, step)


FLAT0 = 5000
SLOT_HEAD = 8
ROOM0 = [FLAT0 + QW - max(P * (kb - TPQ * qb), 0) for qb, kb in BLOCKS0]
MAX_AT = spread_weighed(range(NC0), [64 + end - at for _, _, at, end in CHUNKS0], SLOT_HEAD, 33, ROOM0)
TURN_AT = 35
PROJ_AT = spread(range(NT), SLOT_HEAD, 23, NB0)
TRANS_AT = spread(range(2 * NQB), 28, TURN_AT, NB0)
OUT_AT = {9: 0, 17: 1, 29: 2}
NULLS_AT = 2
OUT_LATE = 6
SQUARE_AT, POWER_AT, NORM_AT = ({first + TPQ * g: g for g in range(NQB)} for first in (12, 15, 18))
TAKE_AT = {sum(TPQ * q + TPQ for q in range(qb + 1)) + 3: (0, qb) for qb in range(NQB - 1)} | {3: (-1, NQB - 1)}
NPROB = 8


PROJECT = NT + 2 * NQB
MISC_FIRST = PROJECT + 1
MISC_PER = PROJECT + 2 + 2 + 4 * NQB


def misc_units(x, more, first):
    out = [[] for _ in range(NB0)]
    for b in range(NB0):
        if x == 0 and more:
            out[b] += [("proj", t) for t in PROJ_AT[b]] + [("trans", c) for c in TRANS_AT[b]]
        if b == TURN_AT and (x == 0 or more):
            out[b].append(("turn", 0))
        if b == NULLS_AT:
            out[b].append(("nulls", x))
        if b in OUT_AT:
            out[b] += [("den", (x, OUT_AT[b])), ("out", (x, OUT_AT[b]))]
        if b == OUT_LATE and (x == 1 or not first):
            out[b] += [("den", (x - 1, NQB - 1)), ("out", (x - 1, NQB - 1))]
    return out


def done_by(kind, n, more, first, x=None):
    done = 0
    for part in range(2):
        for units in misc_units(part, more, first):
            for unit in units:
                done += 1
                if unit == (kind, n) and x in (None, part):
                    return done


def before_step(i, first):
    return MISC_FIRST if first else i * MISC_PER + (MISC_FIRST - 2)


AFTER_LAST = before_step(PAIRS, False) - PROJECT - 1


def upto(x, qb):
    return REAL0 * x + sum(TPQ * q + TPQ for q in range(qb + 1))


HEAD_LOADS = 12


def attention0(nc, mem, dram, routed=True):
    with ExitStack() as ctx:
        def sb(name, shape, dt=F32):
            return ctx.enter_context(nc.sbuf_tensor(f"a0_{name}", shape, dt))

        def sem(name):
            return ctx.enter_context(nc.semaphore(f"a0_{name}"))

        def banks(name, n):
            return [ctx.enter_context(nc.psum_tensor(f"a0_{name}{k}", [P, QW], F32)) for k in range(n)]

        w_qkv, w_loaded = mem.w_qkv, mem.w_loaded
        w_out = sb("w_out", [P, 2, D])
        raw = sb("raw", [P, NT, 3 * P])
        sq = sb("sq", [P, 2, TPQ, 2 * P])
        ssq = sb("ssq", [P, NT * 4])
        ssm = sb("ssm", [P, NT * 4])
        rnorm = sb("rnorm", [P, NT * 4])
        q_hi = sb("q_hi", [P, T], F16)
        q_lo = sb("q_lo", [P, T], F16)
        k_hi = sb("k_hi", [P, T], F16)
        k_lo = sb("k_lo", [P, T], F16)
        q_both = [sb(f"q_both{x}", [P, T], F16) for x in range(2)]
        k_both = [sb(f"k_both{x}", [P, T], F16) for x in range(2)]
        q_rest = [sb(f"q_rest{x}", [P, T], F16) for x in range(2)]
        q_max = [sb(f"q_max{x}", [P, T], F16) for x in range(2)]
        k_ext = [sb(f"k_ext{x}", [P, KW], F16) for x in range(2)]
        values = [sb(f"values{x}", [P, NT, DH0]) for x in range(2)]
        null_k = [sb(f"null_k{x}", [P, 64], F16) for x in range(2)]
        null_v = [sb(f"null_v{x}", [P, DH0]) for x in range(2)]
        table = [sb(f"table{x}", [P, 17 + NT]) for x in range(2)]
        prob = sb("prob", [P, NPROB, QW])
        prob_sum = sb("prob_sum", [P, NQB, QW])
        ones_col = sb("ones_col", [P, 1])
        null_ones = sb("null_ones", [P, NQB])
        null_sum = [sb(f"null_sum{x}", [P, TPQ, NQB]) for x in range(2)]
        den = sb("den", [P, TPQ])
        null_p = [sb(f"null_p{x}", [P, QW]) for x in range(2)]
        rden = sb("rden", [P, NT])
        out_t = sb("out_t", [P, T])
        maxima = sb("maxima", [P, NT, MAXCH])
        max_all = sb("max_all", [P, NT])
        neg_max = sb("neg_max", [P, NT], F16)
        max_row = sb("max_row", [NT, P], F16)
        scratch = nc.dram_tensor("max_rows", (2, NT, P), F16).ap()

        back = sb("back", [P, CHOICES, D])

        ps_st = banks("ps_st", 2)
        ps_ot = banks("ps_ot", 2)
        ps_mx = banks("ps_mx", 2)
        ps_misc = banks("ps_misc", 2)

        gathered = sem("gathered")
        combined = sem("combined")
        wo_loaded = sem("wo_loaded")
        zeroed = sem("zeroed")
        rows_loaded = sem("rows_loaded")
        head_loaded = [sem(f"head_loaded{x}") for x in range(2)]
        v_copied = sem("v_copied")
        st_full = sem("st_full")
        exp_done = sem("exp_done")
        pv_done = sem("pv_done")
        ot_read = sem("ot_read")
        cleared = sem("cleared")
        mx_full = sem("mx_full")
        mx_done = sem("mx_done")
        max_step = sem("max_step")
        misc_full = sem("misc_full")
        misc_done = sem("misc_done")
        row_stored = sem("row_stored")
        row_loaded = sem("row_loaded")
        sq_done = sem("sq_done")
        ss_done = sem("ss_done")
        ssm_ready = sem("ssm_ready")
        rn_ready = sem("rn_ready")
        qn_done = sem("qn_done")
        hi_done = sem("hi_done")
        den_step = sem("den_step")
        added = sem("added")
        block = ctx.enter_context(nc.Block())

        def steps(more, first):
            for x in range(2):
                units = misc_units(x, more, first)
                for b in range(NB0):
                    yield x, b, BLOCKS0[b], (MAX_AT[b] if x == 0 or more else []), units[b]

        @block.sync
        def _(sp):
            def load_head(x, h):
                half = slice(DH0 * x, DH0 * x + DH0)
                low, high = slice(0, DH0), slice(DH0, P)
                done = head_loaded[x]
                sp.dma_start(k_ext[x][low, NULLS:KW], k_hi[half, :]).then_inc(done, 16)
                sp.dma_start(q_max[x][low, :], q_hi[half, :]).then_inc(done, 16)
                sp.dma_start(k_both[x][low, :], k_hi[half, :]).then_inc(done, 16)
                sp.dma_start(k_both[x][high, :], k_lo[half, :]).then_inc(done, 16)
                sp.dma_start(q_both[x][low, :], q_hi[half, :]).then_inc(done, 16)
                sp.dma_start(q_both[x][high, :], q_hi[half, :]).then_inc(done, 16)
                sp.dma_start(q_rest[x][low, :], q_lo[half, :]).then_inc(done, 16)
                sp.dma_start(q_max[x][ROW_POS:ROW_POS + 1, :], dram["slope_rows"][bass.ds(h, 1), :, :]
                             .rearrange("h t o -> h (t o)")).then_inc(done, 16)
                sp.dma_start(table[x][:, :], flat(dram["head_table"][bass.ds(h, 1), :, :])).then_inc(done, 16)
                sp.dma_start(null_k[x][:, :].unsqueeze(1), mem.null_ops[:, bass.ds(h, 1), 0:64]).then_inc(done, 16)
                sp.dma_start(k_ext[x][:, 0:NULLS].unsqueeze(1), mem.null_ops[:, bass.ds(h, 1), 64:66]).then_inc(done, 16)
                sp.dma_start(null_v[x][:, :], flat(dram["null_v"][bass.ds(h, 1), :, :])).then_inc(done, 16)

            def turn_row(x, n, done):
                sp.wait_ge(misc_done, done)
                sp.dma_start(scratch[x, :, :], max_row[:, :]).then_inc(row_stored, 16)
                sp.wait_ge(row_stored, 16 * n + 16)
                sp.dma_start(q_rest[x][ROW_ONE:ROW_ONE + 1, :],
                             scratch[x:x + 1, :, :].rearrange("o t p -> o (t p)")).then_inc(row_loaded, 16)

            def step(i, more, first=False):
                base = before_step(i, first)
                if more:
                    sp.wait_ge(misc_full, base)
                    sp.dma_start(w_qkv[:, :], flat(dram["w_qkv"][bass.ds(i + 1, 1), :, :])).then_inc(w_loaded, 16)
                if not first:
                    sp.wait_ge(misc_full, base + done_by("out", (-1, NQB - 1), more, first))
                sp.dma_start(w_out[:, :, :], dram["w_out"][bass.ds(2 * i, 2), :, :].rearrange("x p d -> p x d")).then_inc(wo_loaded, 16)
                turn_row(1, 2 * i + 1, base + done_by("turn", 0, more, first))
                if more:
                    sp.wait_ge(exp_done, i * (2 * NB0) + NB0)
                    load_head(0, 2 * i + 2)
                    turn_row(0, 2 * i + 2, base + done_by("turn", 0, more, first, x=1))
                    sp.wait_ge(exp_done, i * (2 * NB0) + 2 * NB0)
                    load_head(1, 2 * i + 3)

            sp.dma_start(null_ones[:, :], dram["null_ones"]).then_inc(rows_loaded, 16)
            sp.wait_ge(zeroed, 7)
            for x in range(2):
                for n, row in enumerate((ROW_ONE, ROW_POS)):
                    sp.dma_start(k_ext[x][row:row + 1, :], dram["key_rows"][n:n + 1, :]).then_inc(rows_loaded, 16)
            sp.wait_ge(rows_loaded, 16 * 5)
            sp.wait_ge(misc_done, PROJECT)
            load_head(0, 0)
            load_head(1, 1)
            turn_row(0, 0, MISC_FIRST)
            step(0, True, first=True)
            with sp.Fori(1, PAIRS - 1) as i:
                step(i, True)
            step(PAIRS - 1, False)

        @block.tensor
        def _(pe):
            def transpose(c, bank):
                at = P * (c // NQB)
                for j in range(TPQ):
                    mm = pe.transpose(ps_misc[bank][:, P * j:P * j + P], raw[:, TPQ * (c % NQB) + j, at:at + P],
                                      mem.ident[:, :])
                mm.then_inc(misc_full, 1)

            def unit(kind, n, free, bank, turns, pairs):
                if free is not None:
                    pe.wait_ge(misc_done, free)
                if kind == "proj":
                    if n == 0:
                        pe.wait_ge(w_loaded, 16 * pairs + 16)
                    pe.matmul(ps_misc[bank][:, 0:3 * P], mem.yaT[:, P * n:P * n + P], w_qkv[:, :],
                              start=True, stop=True).then_inc(misc_full, 1)
                elif kind == "trans":
                    pe.wait_ge(qn_done, pairs * NQB + n % NQB + 1)
                    transpose(n, bank)
                elif kind == "turn":
                    pe.wait_ge(max_step, 2 * turns + 2)
                    pe.transpose(ps_misc[bank][:, :].bitcast(F16)[0:NT, 0:P], neg_max[:, :],
                                 mem.ident_h[:, :]).then_inc(misc_full, 1)

            def sums(i, x, qb, bank, free):
                pe.wait_ge(misc_done, free)
                pe.wait_ge(added, i * (2 * REAL0) + upto(x, qb))
                for j in range(TPQ):
                    mm = pe.matmul(ps_misc[bank][:, j:j + 1], prob_sum[:, qb, P * j:P * j + P], ones_col[:, :],
                                   start=True, stop=True)
                mm.then_inc(misc_full, 1)

            def null_sums(i, x, bank, free):
                pe.wait_ge(misc_done, free)
                pe.wait_ge(exp_done, i * (2 * NB0) + NB0 * x + 1)
                for j in range(TPQ):
                    mm = pe.matmul(ps_misc[bank][:, NQB * j:NQB * j + NQB], null_p[x][:, P * j:P * j + P], null_ones[:, :],
                                   start=True, stop=True)
                mm.then_inc(misc_full, 1)

            def output(i, x, qb, bank, free):
                pe.wait_ge(misc_done, free)
                pe.wait_ge(ot_read, i * (2 * NQB) + NQB * x + qb + 1)
                x = x % 2
                if (x, qb) == (0, 0):
                    pe.wait_ge(wo_loaded, 16 * i + 16)
                for j in range(TPQ):
                    at = QW * qb + P * j
                    mm = pe.matmul(ps_misc[bank][:, P * j:P * j + P], out_t[:, at:at + P], w_out[:, x, :],
                                   start=True, stop=True)
                mm.then_inc(misc_full, 1)

            def chunk(x, c, free):
                qt, _, a, z = CHUNKS0[c]
                if free is not None:
                    pe.wait_ge(mx_done, free)
                bank = ps_mx[c % 2]
                diag = z == NULLS + P * (qt + 1)
                mm = pe.matmul(bank[:, 0:z - a], q_max[x][:, P * qt:P * qt + P], k_ext[x][:, a:z],
                               start=True, stop=not diag)
                if diag:
                    mm = pe.matmul(bank[:, z - a - P:z - a], mem.ident_b[:, :], mem.mask_qb[:, :],
                                   start=False, stop=True)
                mm.then_inc(mx_full, 1)

            def scores(x, b):
                qb, kb = BLOCKS0[b]
                bank = ps_st[(NB0 * x + b) % 2]
                if b == 0:
                    for q in range(NQB):
                        cols = slice(QW * q, QW * q + QW)
                        rows = slice(32 * q, 32 * q + 32)
                        pe.matmul(bank[rows, :], null_k[x][:, 0:32], q_both[x][:, cols], start=True, stop=False)
                        mm = pe.matmul(bank[rows, :], null_k[x][:, 32:64], q_rest[x][:, cols], start=False, stop=True)
                else:
                    c0 = max(P * (kb - TPQ * qb), 0)
                    cols = slice(QW * qb + c0, QW * qb + QW)
                    keys = slice(P * kb, P * kb + P)
                    diag = kb >= TPQ * qb
                    pe.matmul(bank[:, c0:QW], k_both[x][:, keys], q_both[x][:, cols], start=True, stop=False)
                    mm = pe.matmul(bank[:, c0:QW], k_ext[x][:, NULLS + P * kb:NULLS + P * kb + P], q_rest[x][:, cols],
                                   start=False, stop=not diag)
                    if diag:
                        mm = pe.matmul(bank[:, c0:c0 + P], mem.ident_b[:, :], mem.mask_kb[:, P:2 * P],
                                       start=False, stop=True)
                mm.then_inc(st_full, 1)

            def weighted(i, x, b, first):
                qb, kb = BLOCKS0[b]
                bank = ps_ot[qb % 2]
                pe.wait_ge(exp_done, i * (2 * NB0) + NB0 * x + b + 1)
                x = x % 2
                if kb == 1:
                    if NQB * x + qb >= 2 or not first:
                        pe.wait_ge(ot_read, i * (2 * NQB) + NQB * x + qb - 1)
                    rows = slice(32 * qb, 32 * qb + 32)
                    pe.matmul(bank[0:DH0, :], null_v[x][rows, :], null_p[x][rows, :], start=True, stop=False)
                last = kb == TPQ * qb + TPQ - 1
                for back, half in ((1, slice(DH0, P)), (0, slice(0, DH0))):
                    c0 = max(P * (kb - back - TPQ * qb), 0)
                    n = REAL0 * x + b - 1 - back
                    mm = pe.matmul(bank[half, c0:QW], values[x][:, kb - back, :], prob[:, n % NPROB, c0:QW],
                                   start=kb - back == 0, stop=last)
                mm.then_inc(pv_done, 2)

            def step(i, more, first=False):
                base = before_step(i, first)
                done = 0
                chunks = 0
                before = None if first else (-1, NB0 - 1)
                for x, b, _, maxes, units in steps(more, first):
                    if b == 0:
                        pe.wait_ge(head_loaded[x], i * (16 * HEAD_LOADS) + 16 * HEAD_LOADS)
                        pe.wait_ge(v_copied, 2 * i + x + 1)
                        pe.wait_ge(row_loaded, i * 32 + 16 * x + 16)
                    if NB0 * x + b >= 2 or not first:
                        pe.wait_ge(exp_done, i * (2 * NB0) + NB0 * x + b - 1)
                    scores(x, b)
                    for c in maxes:
                        if c == 0:
                            pe.wait_ge(head_loaded[1 - x], (i + x) * (16 * HEAD_LOADS) + 16 * HEAD_LOADS)
                        chunk(1 - x, c, NC0 + i * (2 * NC0) + chunks - 1)
                        chunks += 1
                    for kind, n in units:
                        free = base + done - 1
                        bank = (MISC_FIRST + done) % 2
                        if kind == "nulls":
                            null_sums(i, n, bank, free)
                        elif kind == "den":
                            sums(i, *n, bank, free)
                        elif kind == "out":
                            output(i, *n, bank, free)
                        else:
                            unit(kind, n, free, bank, 2 * i + 1 + x, i + 1)
                        done += 1
                    if b % 2 == 0:
                        if before is not None:
                            weighted(i, *before, first)
                        before = (x, b) if b > 0 else None

            for u, (kind, n) in enumerate([("proj", t) for t in range(NT)] + [("trans", c) for c in range(2 * NQB)]):
                unit(kind, n, u - 1 if u >= 2 else None, u % 2, 0, 0)
            pe.wait_ge(head_loaded[0], 16 * HEAD_LOADS)
            for c in range(NC0):
                chunk(0, c, c - 1 if c >= 2 else None)
            unit("turn", 0, PROJECT - 1, PROJECT % 2, 0, 0)
            step(0, True, first=True)
            with pe.Fori(1, PAIRS - 1) as i:
                step(i, True)
            step(PAIRS - 1, False)
            weighted(PAIRS, -1, NB0 - 1, False)
            sums(PAIRS, -1, NQB - 1, AFTER_LAST % 2, AFTER_LAST - 1)
            output(PAIRS, -1, NQB - 1, (AFTER_LAST + 1) % 2, AFTER_LAST)

        @block.scalar
        def _(act):
            def high(c, full, bank, pairs):
                cols = slice(QW * (c % NQB), QW * (c % NQB) + QW)
                act.wait_ge(misc_full, full)
                if pairs is not None:
                    act.wait_ge(head_loaded[1], pairs)
                k = c // NQB
                dst = (q_hi, k_hi)[k]
                act.activation(dst[:, cols], ps_misc[bank][:, :], ACT.Copy, scale=mem.scales[:, k:k + 1]).then_inc(hi_done, 1)

            def copy_values(x):
                at = 2 * P + DH0 * x
                act.activation(values[x][:, :, :], raw[:, :, at:at + DH0], ACT.Copy).then_inc(v_copied, 1)

            def take_out(i, x, qb, base, more, first):
                act.wait_ge(pv_done, i * (2 * REAL0) + upto(x, qb))
                if x == 1 or (x, qb) == (0, NQB - 1) and not first:
                    act.wait_ge(misc_full, base + done_by("out", (x - 1, qb), more, first))
                elif not first:
                    act.wait_ge(misc_full, base)
                act.activation(out_t[:, QW * qb:QW * qb + QW], ps_ot[qb % 2][:, :], ACT.Copy).then_inc(ot_read, 1)

            def squares(pairs, g, projected):
                if g >= 2:
                    act.wait_ge(ss_done, pairs * NQB + g - 1)
                act.wait_ge(misc_done, projected)
                act.activation(sq[:, g % 2, :, :], raw[:, TPQ * g:TPQ * g + TPQ, 0:2 * P], ACT.Square).then_inc(sq_done, 1)

            def step(i, more, first=False):
                base = before_step(i, first)
                done = 0
                for x, b, (qb, kb), _, units in steps(more, first):
                    if (x, b) == (0, 3):
                        if not first:
                            act.wait_ge(pv_done, i * (2 * REAL0))
                        act.wait_ge(misc_done, base)
                        copy_values(1)
                    if (x, b) == (1, 6) and more:
                        act.wait_ge(pv_done, i * (2 * REAL0) + REAL0)
                        act.wait_ge(misc_done, base + done_by("turn", 0, more, first))
                        copy_values(0)
                    act.wait_ge(st_full, i * (2 * NB0) + NB0 * x + b + 1)
                    bank = ps_st[(NB0 * x + b) % 2]
                    if b == 0:
                        act.activation(null_p[x][:, :], bank[:, :], ACT.Exp, bias=table[x][:, 16:17]).then_inc(exp_done, 1)
                    else:
                        n = REAL0 * x + b - 1
                        c0 = max(P * (kb - TPQ * qb), 0)
                        at = kb - TPQ * qb + TPQ * (NQB - 1)
                        if n >= NPROB or not first:
                            act.wait_ge(pv_done, i * (2 * REAL0) + (n - NPROB) // 2 * 2 + 2)
                            act.wait_ge(added, i * (2 * REAL0) + (n - NPROB) // 2 * 2 + 2)
                        act.activation(prob[:, n % NPROB, c0:QW], bank[:, c0:QW], ACT.Exp,
                                       bias=table[x][:, at:at + 1]).then_inc(exp_done, 1)
                    for kind, n in units:
                        done += 1
                        if kind == "trans":
                            high(n, base + done, (MISC_FIRST + done - 1) % 2, (i + 1) * (16 * HEAD_LOADS))
                    if x == 0 and more and b in SQUARE_AT:
                        g = SQUARE_AT[b]
                        squares(i + 1, g, base + done_by("proj", TPQ * g + TPQ - 1, more, first))
                    if b in TAKE_AT and not (first and x + TAKE_AT[b][0] < 0):
                        take_out(i, x + TAKE_AT[b][0], TAKE_AT[b][1], base, more, first)

            for g in range(NQB):
                squares(0, g, TPQ * g + TPQ)
            for c in range(2 * NQB):
                high(c, NT + c + 1, (NT + c) % 2, None)
            copy_values(0)
            step(0, True, first=True)
            with act.Fori(1, PAIRS - 1) as i:
                step(i, True)
            step(PAIRS - 1, False)
            take_out(PAIRS, -1, NQB - 1, AFTER_LAST, False, False)

        @block.gpsimd
        def _(pool):
            def power(pairs, g):
                at = slice(4 * TPQ * g, 4 * TPQ * (g + 1))
                pool.wait_ge(ssm_ready, pairs * NQB + g + 1)
                pool.tensor_tensor(rnorm[:, at], ssm[:, at], mem.minus_half[:, at], ALU.pow).then_inc(rn_ready, 1)

            def add(i, x, b, base, more, first):
                qb, kb = BLOCKS0[b]
                n = REAL0 * x + b - 1
                c0 = max(P * (kb - TPQ * qb), 0)
                into = prob_sum[:, qb, :]
                if kb == 0:
                    return
                pool.wait_ge(exp_done, i * (2 * NB0) + NB0 * x + b + 1)
                if kb == 1:
                    if x == 1 or qb == NQB - 1 and not first:
                        pool.wait_ge(misc_full, base + done_by("den", (x - 1, qb), more, first))
                    elif not first:
                        pool.wait_ge(misc_full, base)
                    if c0 > 0:
                        first = prob[:, (n - 1) % NPROB, 0:c0]
                        pool.tensor_tensor(into[:, 0:c0], first, ones_col[:, :].to_broadcast([P, c0]), ALU.mult).then_inc(added, 1)
                    pool.tensor_tensor(into[:, c0:QW], prob[:, (n - 1) % NPROB, c0:QW], prob[:, n % NPROB, c0:QW],
                                       ALU.add).then_inc(added, 1 if c0 > 0 else 2)
                else:
                    pool.wait_ge(added, i * (2 * REAL0) + n)
                    pool.tensor_tensor(into[:, c0:QW], into[:, c0:QW], prob[:, n % NPROB, c0:QW],
                                       ALU.add).then_inc(added, 1)

            def step(i, more, first=False):
                base = before_step(i, first)
                for x, b, _, _, _ in steps(more, first):
                    if b > 0:
                        add(i, x, b, base, more, first)
                    if x == 0 and more:
                        if b in POWER_AT:
                            power(i + 1, POWER_AT[b])

            link = chain(pool, zeroed)
            link(pool.memset(ones_col[:, :], 1.0))
            for x in range(2):
                link(pool.memset(q_rest[x][DH0:P, :], 0.0))
                link(pool.memset(q_max[x][DH0:P, :], 0.0))
                link(pool.memset(k_ext[x][DH0:P, :], 0.0))
            for g in range(NQB):
                power(0, g)
            if routed:
                gather(pool, mem, 0, back, gathered)
            step(0, True, first=True)
            with pool.Fori(1, PAIRS - 1) as i:
                step(i, True)
            step(PAIRS - 1, False)

        @block.vector
        def _(dve):
            def unit(kind, n, full, bank, pairs, turns, dens=None):
                ps = ps_misc[bank]
                dve.wait_ge(misc_full, full)
                if kind == "proj":
                    if n == 0 and pairs is not None:
                        dve.wait_ge(v_copied, 2 * pairs)
                    dve.tensor_copy(raw[:, n, :], ps[:, 0:3 * P]).then_inc(misc_done, 1)
                elif kind == "trans":
                    cols = slice(QW * (n % NQB), QW * (n % NQB) + QW)
                    k = n // NQB
                    hi, lo = ((q_hi, q_lo), (k_hi, k_lo))[k]
                    dve.wait_ge(hi_done, (0 if pairs is None else pairs * (2 * NQB)) + n + 1)
                    dve.scalar_tensor_tensor(out=lo[:, cols], in0=ps[:, :], scalar=mem.scales[:, k:k + 1],
                                             in1=hi[:, cols], op0=ALU.mult, op1=ALU.subtract).then_inc(misc_done, 1)
                elif kind == "turn":
                    if turns is not None:
                        dve.wait_ge(row_stored, 16 * turns)
                    dve.tensor_copy(max_row[:, :], ps[:, :].bitcast(F16)[0:NT, 0:P]).then_inc(misc_done, 1)
                elif kind == "den":
                    at = TPQ * n[1]
                    dve.tensor_tensor(den[:, :], ps[:, 0:TPQ], null_sum[n[0] % 2][:, :, n[1]], ALU.add).then_inc(den_step, 1)
                    dve.wait_ge(den_step, dens + 1)
                    dve.reciprocal(rden[:, at:at + TPQ], den[:, :]).then_inc(misc_done, 1)
                elif kind == "nulls":
                    dve.tensor_copy(null_sum[n][:, :, :].rearrange("p j q -> p (j q)"), ps[:, 0:NQB * TPQ]).then_inc(misc_done, 1)
                elif kind == "out":
                    dve.wait_ge(misc_done, full - 1)
                    for j in range(TPQ):
                        t = TPQ * n[1] + j
                        ins = dve.scalar_tensor_tensor(out=mem.acc[:, t, :], in0=ps[:, P * j:P * j + P],
                                                       scalar=rden[:, t:t + 1], in1=mem.acc[:, t, :],
                                                       op0=ALU.mult, op1=ALU.add)
                    ins.then_inc(misc_done, 1)

            def sums(g, base):
                dve.wait_ge(sq_done, base + g + 1)
                view = sq[:, g % 2, :, :].rearrange("p t (g d) -> p (t g) d", d=DH0)
                dve.reduce_sum(ssq[:, 4 * TPQ * g:4 * TPQ * (g + 1)], view, AX_X).then_inc(ss_done, 1)
                dve.wait_ge(ss_done, base + g + 1)
                at = slice(4 * TPQ * g, 4 * TPQ * (g + 1))
                dve.tensor_scalar(ssm[:, at], ssq[:, at], 1e-24, None, ALU.max).then_inc(ssm_ready, 1)

            def chunk(c, full):
                qt, n, a, z = CHUNKS0[c]
                dve.wait_ge(mx_full, full)
                dve.reduce_max(maxima[:, qt, n:n + 1], ps_mx[c % 2][:, 0:z - a], AX_X).then_inc(mx_done, 1)

            def finish_max(x, all_done, turns):
                dve.wait_ge(mx_done, all_done)
                dve.reduce_max(max_all[:, :], maxima[:, :, :], AX_X).then_inc(max_step, 1)
                dve.wait_ge(max_step, 2 * turns + 1)
                dve.tensor_tensor(neg_max[:, :], table[x][:, 17:17 + NT], max_all[:, :], ALU.subtract).then_inc(max_step, 1)

            def normalise(pairs, g):
                dve.wait_ge(rn_ready, pairs * NQB + g + 1)
                rows = raw[:, TPQ * g:TPQ * g + TPQ, 0:2 * P].rearrange("p t (g d) -> p t g d", d=DH0)
                r = rnorm[:, 4 * TPQ * g:4 * TPQ * (g + 1)].rearrange("p (t g) -> p t g", g=4)
                dve.tensor_tensor(rows, rows, r.unsqueeze(3).to_broadcast([P, TPQ, 4, DH0]),
                                  ALU.mult).then_inc(qn_done, 1)

            def step(i, more, first=False):
                base = before_step(i, first)
                done = 0
                chunks = 0
                for x, b, _, maxes, units in steps(more, first):
                    for c in maxes:
                        chunks += 1
                        chunk(c, NC0 + i * (2 * NC0) + chunks)
                        if c == NC0 - 1:
                            finish_max(1 - x, NC0 + i * (2 * NC0) + chunks, 2 * i + 1 + x)
                    for kind, n in units:
                        dens = i * (2 * NQB) + NQB * n[0] + n[1] if kind == "den" else None
                        unit(kind, n, base + done + 1, (MISC_FIRST + done) % 2, i + 1, 2 * i + 1 + x, dens)
                        done += 1
                    if x == 0 and more and b - 1 in SQUARE_AT:
                        sums(SQUARE_AT[b - 1], (i + 1) * NQB)
                    if x == 0 and more and b in NORM_AT:
                        normalise(i + 1, NORM_AT[b])

            dve.memset(maxima[:, :, :], -BIG).then_inc(cleared, 1)
            dve.wait_ge(cleared, 1)
            for t in range(NT):
                unit("proj", t, t + 1, t % 2, None, None)
            for g in range(NQB):
                sums(g, 0)
            for g in range(NQB):
                normalise(0, g)
            for c in range(2 * NQB):
                unit("trans", c, NT + c + 1, (NT + c) % 2, None, None)
            dve.wait_ge(head_loaded[0], 16 * HEAD_LOADS)
            for c in range(NC0):
                chunk(c, c + 1)
            finish_max(0, NC0, 0)
            unit("turn", 0, PROJECT + 1, PROJECT % 2, None, None)
            if routed:
                combine(dve, mem, 0, back, gathered, combined)
            step(0, True, first=True)
            with dve.Fori(1, PAIRS - 1) as i:
                step(i, True)
            step(PAIRS - 1, False)
            for n, kind in enumerate(("den", "out")):
                unit(kind, (-1, NQB - 1), AFTER_LAST + n + 1, (AFTER_LAST + n) % 2, None, None, PAIRS * (2 * NQB) - 1)


SLOTS1 = [(qb, m) for qb in range(NQB) for m in range(TPQ * (qb + 1) // 2)]
NS1 = len(SLOTS1)
EARLY1 = [(a, c) for a in range(2) for c in range(NC1) if CHUNKS1[c][0] < NT - TPQ]
LATE1 = [(a, c) for a in range(2) for c in range(NC1) if CHUNKS1[c][0] >= NT - TPQ]
LATE_AT1 = spread(LATE1, 0, 6, NS1)
EARLY_AT1 = spread(EARLY1, 7, 16, NS1)
TURN_LATE1, TURN_EARLY1 = 9, 17
FIRST_LATE1 = SLOTS1.index((NQB - 1, 0))
EARLY_END = P * (NT - TPQ)
COMBINE_AT1 = list(range(9, 17))
PER_STEP1 = 2 * (len(EARLY1) + len(LATE1))
SCALE1 = float(1 / np.sqrt(np.float32(DH1)))


def units1(more):
    out = [[] for _ in range(2 * NS1 + 5)]
    for x in range(2):
        out[NS1 * x + TURN_LATE1].append(("late", x, 0))
        if x == 0 or more:
            out[NS1 * x + TURN_EARLY1].append(("early", x, 0))
        for s, (qb, m) in enumerate(SLOTS1):
            if m == TPQ * (qb + 1) // 2 - 1:
                out[NS1 * x + s + 2].append(("den", x, qb))
                for a in range(2):
                    out[NS1 * x + s + 3 + a].append((("out", a), x, qb))
    return out


def turn_number(kind, x):
    return 1 + 2 * x + (kind == "early")


def before1(kind, x, qb, more):
    n = 0
    for units in units1(more):
        for u in units:
            n += 1
            if u == (kind, x, qb):
                return n


MISC_PER1 = 4 + 6 * NQB
HEAD_LOADS1 = 6
GROUP_LOADS = 2 * HEAD_LOADS1 + 1


def project1(nc, mem, dram, parts, values_all):
    with ExitStack() as ctx:
        def sb(name, shape, dt=F32):
            return ctx.enter_context(nc.sbuf_tensor(f"p1_{name}", shape, dt))

        def sem(name):
            return ctx.enter_context(nc.semaphore(f"p1_{name}"))

        w, bias, rope = mem.w_qkv1, mem.b_qkv1, mem.rope
        raw = sb("raw", [P, NT, 3 * P])
        a_cos = sb("a_cos", [P, NT, 64])
        b_sin = sb("b_sin", [P, NT, 64])
        a_sin = sb("a_sin", [P, NT, 64])
        b_cos = sb("b_cos", [P, NT, 64])
        turned = sb("turned", [P, NT, P])
        part = sb("part", [P, 2, PARTS, NT, P], BF16)
        part_t = sb("part_t", [P, 2, T], BF16)
        ps = [ctx.enter_context(nc.psum_tensor(f"p1_ps{k}", [P, QW], F32)) for k in range(2)]
        ps_t = [ctx.enter_context(nc.psum_tensor(f"p1_pt{k}", [P, 2 * QW], BF16)) for k in range(4)]

        projected = sem("projected")
        step = sem("step")
        raw_ready = sem("raw_ready")
        parts_ready = sem("parts_ready")
        turned_full = sem("turned_full")
        turned_read = sem("turned_read")
        stored = [sem(f"stored{k}") for k in range(2)]
        scattered = sem("scattered")
        block = ctx.enter_context(nc.Block())

        @block.sync
        def _(sp):
            for n in range(2 * PARTS):
                sp.wait_ge(turned_read, 2 * n + 2)
                sp.dma_start(parts[n // PARTS, n % PARTS, :, :], part_t[:, n % 2, :]).then_inc(stored[n % 2], 16)
            for k in range(2):
                sp.wait_ge(stored[k], 16 * PARTS)

        @block.tensor
        def _(pe):
            for t in range(NT):
                if t >= 2:
                    pe.wait_ge(raw_ready, t - 1)
                pe.matmul(ps[t % 2][:, 0:3 * P], mem.hT[:, P * t:P * t + P], w[:, :], start=True, stop=True)\
                  .then_inc(projected, 1)
            for n in range(2 * PARTS):
                pe.wait_ge(parts_ready, n + 1)
                for half in range(2):
                    u = 2 * n + half
                    if u >= 4:
                        pe.wait_ge(turned_read, u - 3)
                    for j in range(NT // 2):
                        mm = pe.transpose(ps_t[u % 4][:, P * j:P * j + P],
                                          part[:, n // PARTS, n % PARTS, NT // 2 * half + j, :], mem.ident_b[:, :])
                    mm.then_inc(turned_full, 1)

        @block.scalar
        def _(act):
            act.wait_ge(raw_ready, NT)
            for a in range(2):
                v = raw[:, :, 2 * P:3 * P].rearrange("p t (g a d) -> p g t a d", a=2, d=DH1)
                act.copy(values_all[:, :, :, a, 0:DH1], v[:, :, :, a, :])
            for n in range(2 * PARTS):
                for half in range(2):
                    u = 2 * n + half
                    act.wait_ge(turned_full, u + 1)
                    if n >= 2:
                        act.wait_ge(stored[n % 2], 16 * (n // 2))
                    act.copy(part_t[:, n % 2, 2 * QW * half:2 * QW * (half + 1)], ps_t[u % 4][:, :]).then_inc(turned_read, 1)

        @block.gpsimd
        def _(pool):
            scatter(pool, mem, 1, scattered)

        @block.vector
        def _(dve):
            link = chain(dve, step)
            for t in range(NT):
                dve.wait_ge(projected, t + 1)
                dve.tensor_tensor(raw[:, t, :], ps[t % 2][:, 0:3 * P], bias[:, :], ALU.add).then_inc(raw_ready, 1)
            dve.wait_ge(raw_ready, NT)
            cos, sin = rope[:, 0, :, :], rope[:, 1, :, :]
            for k in range(2):
                even, odd = raw[:, :, P * k:P * k + 64], raw[:, :, P * k + 64:P * k + P]
                link(dve.tensor_tensor(a_cos[:, :, :], even, cos, ALU.mult))
                link(dve.tensor_tensor(b_sin[:, :, :], odd, sin, ALU.mult))
                link(dve.tensor_tensor(a_sin[:, :, :], even, sin, ALU.mult))
                link(dve.tensor_tensor(b_cos[:, :, :], odd, cos, ALU.mult))
                view = turned[:, :, :].rearrange("p t (h c f) -> p t h c f", h=H1, c=2)

                def by_head(m):
                    return m[:, :, :].rearrange("p t (h f) -> p t h f", h=H1)

                link(dve.tensor_tensor(view[:, :, :, 0, :], by_head(a_cos), by_head(b_sin), ALU.subtract))
                link(dve.tensor_tensor(view[:, :, :, 1, :], by_head(a_sin), by_head(b_cos), ALU.add))
                for n in range(PARTS):
                    ins = dve.tensor_copy(part[:, k, n, :, :], turned[:, :, :])
                    ins.then_inc(parts_ready, 1)
                    dve.wait_ge(parts_ready, PARTS * k + n + 1)
                    if n < PARTS - 1:
                        link(dve.tensor_tensor(turned[:, :, :], turned[:, :, :], part[:, k, n, :, :], ALU.subtract))


def attention1(nc, mem, dram):
    with ExitStack() as outer:
        parts = nc.dram_tensor("parts1", (2, PARTS, P, T), BF16).ap()
        values_all = mem.values_all
        project1(nc, mem, dram, parts, values_all)
        own = first_memory1(outer, nc)
        experts(nc, mem, 1, dram, FirstMaxima(own, dram, parts, values_all))
        attend1(nc, mem, dram, parts, values_all, own)


def first_memory1(ctx, nc):
    own = Memory()
    own.qs, own.ks = [[[ctx.enter_context(nc.sbuf_tensor(f"a1_{name}{x}{a}", [P, T], BF16)) for a in range(2)]
                       for x in range(2)] for name in ("qs", "ks")]
    own.values = [ctx.enter_context(nc.sbuf_tensor(f"a1_values{x}", [P, NT, 2, 32], F32)) for x in range(2)]
    own.w_out = [ctx.enter_context(nc.sbuf_tensor(f"a1_w_out{x}", [P, D], F32)) for x in range(2)]
    own.select = ctx.enter_context(nc.sbuf_tensor("a1_select", [P, 2], F32))
    own.maxima = ctx.enter_context(nc.sbuf_tensor("a1_maxima", [P, 2 * NT, NQB], F32))
    own.ps_mx = [ctx.enter_context(nc.psum_tensor(f"a1_mx{k}", [P, QW], F32)) for k in range(2)]
    own.zeroed = [ctx.enter_context(nc.semaphore(f"a1_zeroed{x}")) for x in range(2)]
    own.loaded = [ctx.enter_context(nc.semaphore(f"a1_loaded{x}")) for x in range(2)]
    own.out_loaded = [ctx.enter_context(nc.semaphore(f"a1_out_loaded{x}")) for x in range(2)]
    own.select_loaded = ctx.enter_context(nc.semaphore("a1_select_loaded"))
    own.mx_full = ctx.enter_context(nc.semaphore("a1_mx_full"))
    own.mx_done = ctx.enter_context(nc.semaphore("a1_mx_done"))
    own.cleared = ctx.enter_context(nc.semaphore("a1_cleared"))
    return own


def clear_operands1(eng, own, x):
    ones_twice = float(np.array([0x3F803F80], np.uint32).view(np.float32)[0])
    for a in range(2):
        eng.memset(own.qs[x][a][64:ROW_SHIFT, :], 0.0).then_inc(own.zeroed[x], 1)
        eng.memset(own.ks[x][a][64:ROW_SHIFT, :], 0.0).then_inc(own.zeroed[x], 1)
        eng.memset(own.ks[x][a][:, :].bitcast(F32)[ROW_SHIFT:ROW_SHIFT + 1, :], ones_twice).then_inc(own.zeroed[x], 1)


def load_operands1(sp, own, parts, x, g):
    for a in range(2):
        for n in range(PARTS):
            rows = slice(PARTS * DH1 * n, PARTS * DH1 * (n + 1))
            sp.dma_start(own.qs[x][a][rows, :],
                         parts[0].rearrange("n (g f) t -> g n f t", f=DH1)[bass.ds(2 * g + a, 1), :, :, :]
                         .rearrange("o n f t -> (o n) f t")).then_inc(own.loaded[x], 16)
            key = parts[1, n].rearrange("(g f) t -> g f t", f=DH1)[bass.ds(2 * g + a, 1), :, :]
            sp.dma_start(own.ks[x][a][rows, :], key.to_broadcast([PARTS, DH1, T])).then_inc(own.loaded[x], 16)


def load_values1(sp, own, values_all, x, g):
    sp.dma_start(own.values[x][:, :, :, :].rearrange("p t a f -> p (t a f)").unsqueeze(1),
                 values_all[:, bass.ds(g, 1), :, :, :].rearrange("p g t a f -> p g (t a f)")).then_inc(own.loaded[x], 16)


def load_out1(sp, own, dram, x, g):
    sp.dma_start(own.w_out[x][:, :], flat(dram["w_out1"][bass.ds(g, 1), :, :])).then_inc(own.out_loaded[x], 16)


def max_product1(pe, mem, own, x, a, c, nth, free):
    qt, _, lo, hi = CHUNKS1[c]
    if free is not None:
        pe.wait_ge(own.mx_done, free)
    bank = own.ps_mx[nth % 2]
    diag = hi == P * (qt + 1)
    mm = pe.matmul(bank[:, 0:hi - lo], own.qs[x][a][0:STACK, P * qt:P * qt + P], own.ks[x][a][0:STACK, lo:hi],
                   start=True, stop=not diag)
    if diag:
        mm = pe.matmul(bank[:, hi - lo - P:hi - lo], mem.ident_b[:, :], mem.mask_qb[:, :], start=False, stop=True)
    mm.then_inc(own.mx_full, 1)


def max_reduce1(dve, own, a, c, nth, full):
    qt, n, lo, hi = CHUNKS1[c]
    dve.wait_ge(own.mx_full, full)
    dve.reduce_max(own.maxima[:, NT * a + qt, n:n + 1], own.ps_mx[nth % 2][:, 0:hi - lo], AX_X).then_inc(own.mx_done, 1)


class FirstMaxima:

    def __init__(self, own, dram, parts, values_all):
        self.own, self.dram, self.parts, self.values_all = own, dram, parts, values_all

    def gpsimd(self, pool):
        clear_operands1(pool, self.own, 1)

    def clear(self, dve):
        clear_operands1(dve, self.own, 0)

    def sync(self, sp, x):
        if x == 0:
            sp.dma_start(self.own.select[:, :], self.dram["den_select"]).then_inc(self.own.select_loaded, 16)
        sp.wait_ge(self.own.zeroed[x], 6)
        load_operands1(sp, self.own, self.parts, x, x)
        load_values1(sp, self.own, self.values_all, x, x)
        load_out1(sp, self.own, self.dram, x, x)

    def chunks(self, unit, units):
        return list(enumerate(EARLY1))[len(EARLY1) * unit // units:len(EARLY1) * (unit + 1) // units]

    def tensor(self, pe, mem, unit, units):
        if unit == 0:
            pe.wait_ge(self.own.loaded[0], 16 * GROUP_LOADS)
        for n, (a, c) in self.chunks(unit, units):
            max_product1(pe, mem, self.own, 0, a, c, n, n - 1 if n >= 2 else None)

    def vector(self, dve, unit, units):
        if unit == 0:
            dve.memset(self.own.maxima[:, :, :], -BIG).then_inc(self.own.cleared, 1)
            dve.wait_ge(self.own.cleared, 1)
        for n, (a, c) in self.chunks(unit, units):
            max_reduce1(dve, self.own, a, c, n, n + 1)


def attend1(nc, mem, dram, parts, values_all, own):
    with ExitStack() as ctx:
        def sb(name, shape, dt=F32):
            return ctx.enter_context(nc.sbuf_tensor(f"a1_{name}", shape, dt))

        def sem(name):
            return ctx.enter_context(nc.semaphore(f"a1_{name}"))

        qs, ks, values, w_out, select, maxima = own.qs, own.ks, own.values, own.w_out, own.select, own.maxima
        prob = sb("prob", [P, 2, 2, 2, QW])
        sums = sb("sums", [P, 2, QW])
        rden = sb("rden", [P, 2 * TPQ])
        max_all = sb("max_all", [P, 2 * NT])
        neg_max = sb("neg_max", [P, 2 * NT], BF16)
        max_row = sb("max_row", [2 * NT, P], BF16)
        scratch = nc.dram_tensor("max_rows1", (2, 2 * NT, P), BF16).ap()
        ps_st = [ctx.enter_context(nc.psum_tensor(f"a1_st{k}", [P, 2, QW], F32)) for k in range(2)]
        ps_ot = ctx.enter_context(nc.psum_tensor("a1_ot", [P, QW], F32))
        ps_misc = ctx.enter_context(nc.psum_tensor("a1_misc", [P, QW], F32))

        back = sb("back", [P, CHOICES, D])
        gathered = sem("gathered")
        combined = sem("combined")
        loaded, out_loaded, mx_done = own.loaded, own.out_loaded, own.mx_done
        st_full = sem("st_full")
        exp_done = sem("exp_done")
        pv_done = sem("pv_done")
        ot_read = sem("ot_read")
        max_step = sem("max_step")
        misc_full = sem("misc_full")
        misc_done = sem("misc_done")
        row_stored = sem("row_stored")
        row_loaded = sem("row_loaded")
        block = ctx.enter_context(nc.Block())

        def slots(more):
            units = units1(more)
            for n in range(2 * NS1 + 5):
                x, s = n // NS1, n % NS1
                maxes = []
                if n < 2 * NS1:
                    maxes = [(x, *m) for m in LATE_AT1[s]]
                    if x == 0 or more:
                        maxes += [(1 - x, *m) for m in EARLY_AT1[s]]
                yield n, x, s, maxes, units[n]

        def upto1(x, qb):
            return NS1 * x + sum(TPQ * (q + 1) // 2 for q in range(qb + 1))

        @block.sync
        def _(sp):
            def load_group(x, g, used):
                load_operands1(sp, own, parts, x, g)
                sp.wait_ge(pv_done, used)
                load_values1(sp, own, values_all, x, g)

            def turn_row(x, late, n, done):
                sp.wait_ge(misc_done, done)
                sp.dma_start(scratch[x, :, :], max_row[:, :]).then_inc(row_stored, 16)
                sp.wait_ge(row_stored, 16 * n + 16)
                tiles = slice(NT - TPQ, NT) if late else slice(0, NT - TPQ)
                cols = slice(EARLY_END, T) if late else slice(0, EARLY_END)
                for a in range(2):
                    sp.dma_start(qs[x][a][ROW_SHIFT:ROW_SHIFT + 1, cols],
                                 scratch[x:x + 1, NT * a + tiles.start:NT * a + tiles.stop, :]
                                 .rearrange("o t p -> o (t p)")).then_inc(row_loaded, 16)

            def step(i, more):
                base = 1 + i * MISC_PER1
                turn_row(0, True, 4 * i + 1, base + before1("late", 0, 0, more))
                turn_row(1, False, 4 * i + 2, base + before1("early", 0, 0, more))
                if more:
                    sp.wait_ge(exp_done, i * (4 * NS1) + 2 * NS1)
                    load_group(0, 2 * i + 2, i * (2 * NS1) + NS1)
                    sp.wait_ge(misc_done, 1 + i * MISC_PER1 + before1(("out", 1), 0, NQB - 1, more))
                    load_out1(sp, own, dram, 0, 2 * i + 2)
                turn_row(1, True, 4 * i + 3, base + before1("late", 1, 0, more))
                if more:
                    turn_row(0, False, 4 * i + 4, base + before1("early", 1, 0, more))
                    sp.wait_ge(exp_done, i * (4 * NS1) + 4 * NS1)
                    load_group(1, 2 * i + 3, i * (2 * NS1) + 2 * NS1)
                    sp.wait_ge(misc_done, 1 + i * MISC_PER1 + MISC_PER1)
                    load_out1(sp, own, dram, 1, 2 * i + 3)

            turn_row(0, False, 0, 1)
            with sp.Fori(0, GROUPS // 2 - 1) as i:
                step(i, True)
            step(GROUPS // 2 - 1, False)

        @block.gpsimd
        def _(pool):
            gather(pool, mem, 1, back, gathered)

        @block.tensor
        def _(pe):
            def turn(turns, free):
                pe.wait_ge(max_step, 2 * turns + 2)
                if free is not None:
                    pe.wait_ge(misc_done, free)
                pe.transpose(ps_misc[:, :].bitcast(BF16)[0:2 * NT, 0:P], neg_max[:, :], mem.ident_b[:, :]).then_inc(misc_full, 1)

            def scores(x, a, s, between):
                qb, m = SLOTS1[s]
                bank = ps_st[a]
                c0 = max(P * (2 * m - TPQ * qb), 0)
                diag = 2 * m >= TPQ * qb
                cols = slice(QW * qb + c0, QW * qb + QW)
                for k in range(2):
                    keys = slice(P * (2 * m + k), P * (2 * m + k) + P)
                    masked = diag or (2 * m + k >= TPQ * qb)
                    mm = pe.matmul(bank[:, k, c0:QW], ks[x][a][0:ROW_SHIFT + 1, keys], qs[x][a][0:ROW_SHIFT + 1, cols],
                                   start=True, stop=not masked)
                    if masked:
                        mm = pe.matmul(bank[:, k, c0:c0 + P * (k + 1)], mem.ident_b[:, :],
                                       mem.mask_kb[:, P * (1 - k):2 * P], start=False, stop=True)
                    if k == 0:
                        between(2 * a)
                mm.then_inc(st_full, 1)
                between(2 * a + 1)

            def weighted(i, n, x, s):
                qb, m = SLOTS1[s]
                c0 = max(P * (2 * m - TPQ * qb), 0)
                pe.wait_ge(exp_done, i * (4 * NS1) + 2 * n + 2)
                if m == 0 and NQB * x + qb >= 1:
                    pe.wait_ge(ot_read, i * (2 * NQB) + NQB * x + qb)
                for a in range(2):
                    for k in range(2):
                        rows = slice(64 * a + 32 * k, 64 * a + 32 * k + 32)
                        mm = pe.matmul(ps_ot[rows, c0:QW], values[x][:, 2 * m + k, a, :], prob[:, n % 2, a, k, c0:QW],
                                       start=(m == 0), stop=(m == TPQ * (qb + 1) // 2 - 1))
                mm.then_inc(pv_done, 1)

            def step(i, more):
                done = 0
                chunks = 0
                for n, x, s, maxes, units in slots(more):
                    if n < 2 * NS1:
                        if s == 0:
                            pe.wait_ge(loaded[x], i * (16 * GROUP_LOADS) + 16 * GROUP_LOADS)
                            pe.wait_ge(row_loaded, i * 128 + 64 * x + 32)
                        if s == FIRST_LATE1:
                            pe.wait_ge(row_loaded, i * 128 + 64 * x + 64)

                        def between(place):
                            nonlocal chunks
                            for buffer, head, c in maxes[len(maxes) * place // 4:len(maxes) * (place + 1) // 4]:
                                if buffer != x and (head, c) == EARLY1[0]:
                                    pe.wait_ge(loaded[1 - x], (i + x) * (16 * GROUP_LOADS) + 16 * GROUP_LOADS)
                                max_product1(pe, mem, own, buffer, head, c, chunks,
                                             i * PER_STEP1 + (len(EARLY1) + chunks - 1))
                                chunks += 1

                        for a in range(2):
                            if n >= 1:
                                pe.wait_ge(exp_done, i * (4 * NS1) + 2 * n + a - 1)
                            scores(x, a, s, between)
                    for kind, gx, qb in units:
                        free = 1 + i * MISC_PER1 + done
                        if kind in ("late", "early"):
                            turn(4 * i + turn_number(kind, gx), free)
                        elif kind == "den":
                            pe.wait_ge(misc_done, free)
                            pe.wait_ge(ot_read, i * (2 * NQB) + NQB * gx + qb + 1)
                            for j in range(TPQ):
                                mm = pe.matmul(ps_misc[:, 2 * j:2 * j + 2], sums[:, qb % 2, P * j:P * j + P], select[:, :],
                                               start=True, stop=True)
                            mm.then_inc(misc_full, 1)
                        else:
                            pe.wait_ge(misc_done, free)
                            pe.wait_ge(out_loaded[gx], 16 * i + 16)
                            rows = slice(64 * kind[1], 64 * kind[1] + 64)
                            for j in range(TPQ):
                                mm = pe.matmul(ps_misc[:, P * j:P * j + P], sums[rows, qb % 2, P * j:P * j + P],
                                               w_out[gx][rows, :], start=True, stop=True)
                            mm.then_inc(misc_full, 1)
                        done += 1
                    if 1 <= n <= 2 * NS1:
                        weighted(i, n - 1, (n - 1) // NS1, (n - 1) % NS1)

            pe.wait_ge(own.select_loaded, 16)
            turn(0, None)
            with pe.Fori(0, GROUPS // 2 - 1) as i:
                step(i, True)
            step(GROUPS // 2 - 1, False)

        @block.scalar
        def _(act):
            def take_out(i, n, qb, more):
                act.wait_ge(pv_done, i * (2 * NS1) + n)
                x, before = divmod(NQB * ((n - 1) // NS1) + qb - 2, NQB)
                act.wait_ge(misc_full, 1 + i * MISC_PER1 + (before1(("out", 1), x, before, more) if x >= 0 else 0))
                act.activation(sums[:, qb % 2, :], ps_ot[:, :], ACT.Copy).then_inc(ot_read, 1)

            ends = {upto1(x, qb): (x, qb) for x in range(2) for qb in range(NQB)}

            def step(i, more):
                for n in range(2 * NS1):
                    s = n % NS1
                    qb, m = SLOTS1[s]
                    c0 = max(P * (2 * m - TPQ * qb), 0)
                    for a in range(2):
                        act.wait_ge(st_full, i * (4 * NS1) + 2 * n + a + 1)
                        if n >= 2:
                            act.wait_ge(pv_done, i * (2 * NS1) + n - 1)
                        act.activation(prob[:, n % 2, a, :, c0:QW], ps_st[a][:, :, c0:QW], ACT.Exp,
                                       scale=SCALE1).then_inc(exp_done, 1)
                    if n in ends:
                        take_out(i, n, ends[n][1], more)
                take_out(i, 2 * NS1, NQB - 1, more)

            with act.Fori(0, GROUPS // 2 - 1) as i:
                step(i, True)
            step(GROUPS // 2 - 1, False)

        @block.vector
        def _(dve):
            def finish_max(all_done, turns):
                dve.wait_ge(mx_done, all_done)
                dve.reduce_max(max_all[:, :], maxima[:, :, :], AX_X).then_inc(max_step, 1)
                dve.wait_ge(max_step, 2 * turns + 1)
                dve.tensor_scalar(neg_max[:, :], max_all[:, :], -1.0, None, ALU.mult).then_inc(max_step, 1)

            def turn(turns, full):
                dve.wait_ge(misc_full, full)
                if turns is not None:
                    dve.wait_ge(row_stored, 16 * turns)
                dve.tensor_copy(max_row[:, :], ps_misc[:, :].bitcast(BF16)[0:2 * NT, 0:P]).then_inc(misc_done, 1)

            def step(i, more):
                done = 0
                chunks = 0
                for n, x, s, maxes, units in slots(more):
                    if n < 2 * NS1:
                        for buffer, head, c in maxes:
                            max_reduce1(dve, own, head, c, chunks, i * PER_STEP1 + (len(EARLY1) + chunks + 1))
                            chunks += 1
                            if (head, c) in (LATE1[-1], EARLY1[-1]):
                                kind = "late" if buffer == x else "early"
                                finish_max(i * PER_STEP1 + (len(EARLY1) + chunks), 4 * i + turn_number(kind, x))
                    for kind, gx, qb in units:
                        full = 1 + i * MISC_PER1 + done + 1
                        if kind in ("late", "early"):
                            turn(4 * i + turn_number(kind, gx), full)
                        elif kind == "den":
                            dve.wait_ge(misc_full, full)
                            dve.reciprocal(rden[:, :], ps_misc[:, 0:2 * TPQ]).then_inc(misc_done, 1)
                        else:
                            dve.wait_ge(misc_full, full)
                            dve.wait_ge(misc_done, full - 1)
                            for j in range(TPQ):
                                t = TPQ * qb + j
                                ins = dve.scalar_tensor_tensor(
                                    out=mem.acc[:, t, :], in0=ps_misc[:, P * j:P * j + P],
                                    scalar=rden[:, 2 * j + kind[1]:2 * j + kind[1] + 1], in1=mem.acc[:, t, :],
                                    op0=ALU.mult, op1=ALU.add)
                            ins.then_inc(misc_done, 1)
                        done += 1
                    if not more and x == 1 and s in COMBINE_AT1:
                        dve.wait_ge(misc_done, 1 + i * MISC_PER1 + done)
                        combine(dve, mem, 1, back, gathered, combined, COMBINE_AT1.index(s), len(COMBINE_AT1))

            finish_max(len(EARLY1), 0)
            turn(None, 1)
            with dve.Fori(0, GROUPS // 2 - 1) as i:
                step(i, True)
            step(GROUPS // 2 - 1, False)




def store(nc, mem, out):
    with ExitStack() as ctx:
        stored = ctx.enter_context(nc.semaphore("stored"))
        block = ctx.enter_context(nc.Block())

        @block.sync
        def _(sp):
            sp.dma_start(out.rearrange("(t p) d -> p t d", p=P), mem.acc[:, :, :]).then_inc(stored, 16)
            sp.wait_ge(stored, 16)


def build(nc, dram, out, phases="0af1AFs"):
    mem = Memory()
    with ExitStack() as ctx:
        def sb(name, shape, dt=F32):
            return ctx.enter_context(nc.sbuf_tensor(name, shape, dt))

        mem.acc = sb("acc", [P, NT, D])
        mem.y = sb("y", [P, NT, D])
        mem.hT = sb("hT", [P, T])
        mem.yaT = sb("yaT", [P, T])
        mem.vecs = sb("vecs", [P, 3])
        mem.slot_to = [sb(f"slot_to{n}", [P, CHOICES], U32) for n in range(2)]
        mem.slot_from = [sb(f"slot_from{n}", [P, CHOICES], U32) for n in range(2)]
        mem.weights = [sb(f"weights{n}", [P, CHOICES]) for n in range(2)]
        mem.expert_in = [nc.dram_tensor(f"expert_in{n}", (SLOTS[n] + 2 * T, D), F32).ap() for n in range(2)]
        mem.expert_out = [nc.dram_tensor(f"expert_out{n}", (SLOTS[n], D), F32).ap() for n in range(2)]
        mem.ident = sb("ident_f", [P, P])
        mem.ident_b = sb("ident_b", [P, P], BF16)
        mem.ident_h = sb("ident_h", [P, P], F16)
        mem.mask_q = sb("mask_qf", [P, P])
        mem.mask_k = sb("mask_kf", [P, 2 * P])
        mem.mask_qb = sb("mask_qb", [P, P], BF16)
        mem.mask_kb = sb("mask_kb", [P, 2 * P], BF16)
        mem.lower = sb("lower_f", [P, P])
        mem.lower_b = sb("lower_b", [P, P], BF16)
        mem.ones_b = sb("ones_b", [P, P], BF16)
        mem.minus_half = sb("minus_half", [P, 4 * NT])
        mem.scales = sb("scales_s", [P, 2])
        mem.null_ops = sb("null_ops", [P, H0, 66], F16)
        mem.w_qkv = sb("w_qkv", [P, 3 * P])
        mem.w_loaded = ctx.enter_context(nc.semaphore("w_loaded"))
        with ExitStack() as early:
            mem.shared = {n: early.enter_context(nc.sbuf_tensor(f"shared_{n}", shape, F32))
                          for n, shape in (("w1", [P, F]), ("w3", [P, F]), ("w2", [P, FC, D]))}
            mem.shared_loaded = early.enter_context(nc.semaphore("shared_loaded"))
            if "0" in phases:
                prepare(nc, mem, 0, dram)
            if "f" in phases:
                experts(nc, mem, 0, dram)
        if "a" in phases:
            attention0(nc, mem, dram, "f" in phases)
        mem.w_qkv1 = sb("w_qkv1", [P, 3 * P])
        mem.b_qkv1 = sb("b_qkv1", [P, 3 * P])
        mem.rope = sb("rope", [P, 2, NT, 64])
        mem.values_all = sb("values_all", [P, GROUPS, NT, 2, 32])
        if "1" in phases:
            prepare(nc, mem, 1, dram)
        if "A" in phases:
            attention1(nc, mem, dram)
        store(nc, mem, out)



def slopes():
    start = 2.0 ** (-2.0 ** (-(np.log2(H0) - 3.0)))
    return np.array([start * start ** n for n in range(H0)], np.float32)


def constants():
    f = np.float32
    p = np.arange(P)
    c = {"ident": np.eye(P, dtype=f)}
    later = p[None, :] > p[:, None]
    c["mask_q"] = np.where(later, f(-BIG), f(0)).astype(f)
    c["mask_k"] = np.concatenate([np.full((P, P), -BIG, f),
                                  np.where(later.T, f(-BIG), f(0)).astype(f)], 1)
    for n in range(2):
        c[f"spare{n}"] = (SLOTS[n] + P * np.arange(CHOICES)[None, :] + p[:, None]).astype(f)
    c["lower"] = later.astype(f)
    c["expert_less"] = np.tile(np.arange(E, dtype=f) - 100, (P, NT)).astype(f)
    s = slopes()
    blocks = np.arange(-(TPQ * (NQB - 1)), TPQ)
    table = np.zeros((H0, P, len(blocks) + 1 + NT), f)
    dist = (P * blocks[None, :] + p[:, None] - ALIBI_REF).astype(f)
    s16 = s.astype(np.float16).astype(f)
    for h in range(H0):
        table[h, :, :len(blocks)] = s[h] * dist
        for q in range(NQB):
            for n in range(NULLS):
                table[h, 32 * q + n, len(blocks)] = s[h] * f(n - NULLS - QW * q - ALIBI_REF)
        table[h, :, len(blocks) + 1:] = (s16[h] * (QW * (np.arange(NT) // TPQ) + ALIBI_REF).astype(f))[None, :]
    c["head_table"] = table
    c["slope_rows"] = np.repeat(s.astype(np.float16)[:, None, None], T, 2)
    c["key_rows"] = np.stack([np.ones(KW), np.arange(KW) - NULLS]).astype(np.float16)
    ones = np.zeros((P, NQB), f)
    for q in range(NQB):
        ones[32 * q:32 * q + NULLS, q] = 1
    c["null_ones"] = ones
    theta = f(1) / (f(10000.0) ** (np.arange(DH1 // 2, dtype=f) / f(DH1 // 2)))
    ang = (np.arange(T, dtype=f)[:, None] * theta[None, :]).astype(f)
    cs = np.stack([np.cos(ang.astype(np.float64)), np.sin(ang.astype(np.float64))]).astype(f)
    c["rope"] = np.ascontiguousarray(np.tile(cs, (1, 1, H1)).reshape(2, NT, P, 64).transpose(2, 0, 1, 3)).reshape(P, -1)
    sel = np.zeros((P, 2), f)
    for a in range(2):
        for k in range(2):
            sel[64 * a + 32 * k + DH1, a] = 1
    c["den_select"] = sel
    return c


def laid_out(v):
    w = {"x": v["L0_attn_x"].reshape(T, D)}
    w["vecs"] = np.stack([v["L0_attn_gamma"], v["L0_ffn_ln_g"], v["L0_ffn_ln_b"]], 1)
    w["scales"] = np.stack([np.tile(v["L0_attn_q_scale"], 2), np.tile(v["L0_attn_k_scale"], 2)], 1)
    nkv = v["L0_attn_null_kv"].reshape(H0, NULLS, 2, DH0)
    w["null_k"] = nkv[:, :, 0].reshape(H0 * NULLS, DH0)
    nv = np.zeros((H0, P, DH0), np.float32)
    for q in range(NQB):
        nv[:, 32 * q:32 * q + NULLS] = nkv[:, :, 1]
    w["null_v"] = nv
    wq = v["L0_attn_w_q"].reshape(D, PAIRS, P)
    wk, wv = v["L0_attn_w_kv"].reshape(D, 2, PAIRS, P).transpose(1, 0, 2, 3)
    w["w_qkv"] = np.concatenate([wq, wk, wv], 2).transpose(1, 0, 2)
    w["w_out"] = np.tile(v["L0_attn_w_out"].reshape(H0, DH0, D), (1, 2, 1))
    w["router0"] = v["L0_ffn_Wr"]
    w["router1"] = v["L1_ffn_Wg"]
    w["w1_0"] = np.concatenate([v["L0_ffn_W1"], v["L0_ffn_W1s"][None]])
    w["w3_0"] = np.concatenate([v["L0_ffn_W3"], v["L0_ffn_W3s"][None]])
    w2 = np.concatenate([v["L0_ffn_W2"], v["L0_ffn_W2s"][None]])
    w["w2_0"] = w2.reshape(E, FC, P, D).transpose(0, 2, 1, 3).reshape(E, P, FC * D)
    w["w1_1"] = v["L1_ffn_W1"]
    w["w2_1"] = v["L1_ffn_W2"].reshape(E, FC, P, D).transpose(0, 2, 1, 3).reshape(E, P, FC * D)
    w["b1_1"] = v["L1_ffn_b1"].reshape(E, FC, P).transpose(0, 2, 1)
    b2 = np.zeros((NT, E, NT, D), np.float32)
    for t in range(NT):
        b2[t, :, t] = v["L1_ffn_b2"]
    w["b2_1"] = b2.reshape(P, NT * D)
    def turned(m):
        return m.reshape(H1, DH1 // 2, 2, -1).transpose(2, 0, 1, 3).reshape(D, -1)
    w["w_qkv1"] = np.concatenate([turned(v["L1_attn_W_q"]).T, turned(v["L1_attn_W_k"]).T, v["L1_attn_W_v"].T], 1)
    w["b_qkv1"] = np.concatenate([turned(v["L1_attn_b_q"])[:, 0], turned(v["L1_attn_b_k"])[:, 0], v["L1_attn_b_v"]])[None]
    wo = np.zeros((GROUPS, 2, 2, 32, D), np.float32)
    wo[:, :, :, 0:DH1] = v["L1_attn_W_o"].T.reshape(GROUPS, 2, 1, DH1, D)
    w["w_out1"] = wo.reshape(GROUPS, P, D)
    w["b_o"] = v["L1_attn_b_o"][None]
    return w


def kernel(**inputs):
    import concourse.bacc as bacc
    from concourse.bass_utils import run_bass_kernel_spmd

    nc = bacc.Bacc("TRN2", target_bir_lowering=False, num_devices=1)
    arrays, dram = {}, {}
    every = laid_out({k: np.asarray(a) for k, a in inputs.items()}) | constants()
    for name, a in every.items():
        a = np.ascontiguousarray(a)
        arrays[f"in_{name}"] = a
        dram[name] = nc.dram_tensor(f"in_{name}", a.shape, mybir.dt.from_np(a.dtype), kind="ExternalInput").ap()
    out = nc.dram_tensor("out_0", (T, D), F32, kind="ExternalOutput").ap()
    build(nc, dram, out)
    r = run_bass_kernel_spmd(nc, [arrays], core_ids=[0])
    return r.results[0]["out_0"].reshape(1, T, D)
```
